# Optimizing a Trainium2 kernel written in Bass

```python
import numpy as np
import jax
import jax.numpy as jnp

def _softmax(x, axis=-1):
    return jax.nn.softmax(x, axis=axis)

def _gelu(x):
    return jax.nn.gelu(x, approximate=True)

def _silu(x):
    return jax.nn.silu(x)

def _sigmoid(x):
    return jax.nn.sigmoid(x)

def _layernorm(x, axis=-1, eps=1e-05):
    m = jnp.mean(x, axis=axis, keepdims=True)
    v = jnp.var(x, axis=axis, keepdims=True)
    return (x - m) / jnp.sqrt(v + eps)

def _scatter_add(tgt, idx, src, axis=0):
    return tgt.at[idx].add(src)

def _segment_sum(src, seg, n):
    return jax.ops.segment_sum(src, seg, n)
kernel_name = 'mk_adaln_d2_jaxref_r8_26f376'

def setup_inputs(seed: int=0):
    np.random.seed(seed)
    _w = jnp.asarray

    def _L0_attn_setup():
        import math
        import jax, jax.numpy as jnp
        import numpy as np
        N_HEADS = 8
        EPS = 1e-05
        key = jax.random.key(seed)
        ks = jax.random.split(key, 5)
        B, L, D = (4, 256, 128)
        w_scale = 0.02
        return {'x': jax.random.normal(ks[0], (B, L, D), dtype=jnp.float32), 'Wq': jax.random.normal(ks[1], (D, D), dtype=jnp.float32) * w_scale, 'Wk': jax.random.normal(ks[2], (D, D), dtype=jnp.float32) * w_scale, 'Wv': jax.random.normal(ks[3], (D, D), dtype=jnp.float32) * w_scale, 'Wo': jax.random.normal(ks[4], (D, D), dtype=jnp.float32) * w_scale, 'gn_weight': jnp.ones((D,), dtype=jnp.float32), 'gn_bias': jnp.zeros((D,), dtype=jnp.float32)}
    _L0_attn_in = _L0_attn_setup()

    def _L0_ffn_setup():
        import jax, jax.numpy as jnp
        import numpy as np
        NUM_EXPERTS = 8
        EXPERT_CAPACITY = 2.0
        key = jax.random.key(seed)
        k1, k2, k3, k4 = jax.random.split(key, 4)
        B, T, C, H, E = (4, 512, 128, 512, NUM_EXPERTS)
        x = jax.random.normal(k1, (B, T, C), jnp.float32)
        gate_w = jax.random.normal(k2, (C, E), jnp.float32) * 0.02
        w1 = jax.random.normal(k3, (E, C, H), jnp.float32) * 0.02
        w2 = jax.random.normal(k4, (E, H, C), jnp.float32) * 0.02
        return {'x': x, 'gate_w': gate_w, 'w1': w1, 'w2': w2}
    _L0_ffn_in = _L0_ffn_setup()
    _L0_c = _w((lambda *s: np.random.randn(*s).astype(np.float32) * 0.05)(16, 128))
    _L0_wmod = _w((lambda *s: np.random.randn(*s).astype(np.float32) * 0.05)(128, 6 * 128) * 128 ** (-0.5))

    def _L1_attn_setup():
        import jax, jax.numpy as jnp
        import numpy as np
        D_MODEL = 128
        D_STATE = 16
        D_CONV = 4
        EXPAND = 2
        D_INNER = D_MODEL * EXPAND
        DT_RANK = max(1, D_MODEL // 16)
        BSZ, SEQ = (2, 256)
        LN_EPS = 1e-05

        def _silu(v):
            return v * jax.nn.sigmoid(v)

        def _selective_scan(u, delta, A, B_s, C_s, D):
            b, l, d = u.shape
            n = A.shape[1]
            h0 = jnp.zeros((b, d, n), dtype=u.dtype)
            sw = lambda a: jnp.swapaxes(a, 0, 1)

            def step(h, inp):
                dt_t, u_t, b_t, c_t = inp
                dA = jnp.exp(dt_t[..., None] * A)
                h = dA * h + dt_t[..., None] * b_t[:, None, :] * u_t[..., None]
                y = jnp.einsum('bdn,bn->bd', h, c_t)
                return (h, y)
            _, ys = jax.lax.scan(step, h0, (sw(delta), sw(u), sw(B_s), sw(C_s)))
            return jnp.swapaxes(ys, 0, 1) + u * D[None, None, :]
        key = jax.random.key(seed)
        ks = jax.random.split(key, 9)
        x = jax.random.normal(ks[0], (BSZ, SEQ, D_MODEL), dtype=jnp.float32)
        W_in = jax.random.normal(ks[1], (2 * D_INNER + 2 * D_STATE + DT_RANK, D_MODEL), dtype=jnp.float32) * 0.02
        W_dt = jax.random.normal(ks[2], (D_INNER, DT_RANK), dtype=jnp.float32) * 0.1
        b_dt = jax.random.uniform(ks[3], (D_INNER,), minval=-4.0, maxval=-1.0, dtype=jnp.float32)
        A_log = jnp.log(jnp.broadcast_to(jnp.arange(1, D_STATE + 1, dtype=jnp.float32), (D_INNER, D_STATE)))
        D = jnp.ones((D_INNER,), dtype=jnp.float32)
        conv_w = jax.random.normal(ks[4], (D_INNER, 1, D_CONV), dtype=jnp.float32) * 0.3
        conv_b = jax.random.normal(ks[5], (D_INNER,), dtype=jnp.float32) * 0.1
        W_out = jax.random.normal(ks[6], (D_MODEL, D_INNER), dtype=jnp.float32) * 0.02
        ln_g = jnp.ones((D_MODEL,), dtype=jnp.float32)
        ln_b = jnp.zeros((D_MODEL,), dtype=jnp.float32)
        return {'x': x, 'W_in': W_in, 'W_dt': W_dt, 'b_dt': b_dt, 'A_log': A_log, 'D': D, 'conv_w': conv_w, 'conv_b': conv_b, 'W_out': W_out, 'ln_g': ln_g, 'ln_b': ln_b}
    _L1_attn_in = _L1_attn_setup()

    def _L1_ffn_setup():
        import jax, jax.numpy as jnp
        import numpy as np
        EPS = 1e-06
        TOP_K = 2
        key = jax.random.key(seed)
        k0, k1, k2, k3, k4 = jax.random.split(key, 5)
        B, S, H, I, E = (1, 256, 128, 448, 8)
        return {'hidden_states': jax.random.normal(k0, (B, S, H), jnp.float32), 'rms_weight': jnp.ones((H,), jnp.float32), 'gate_w': jax.random.normal(k1, (E, H), jnp.float32) * H ** (-0.5), 'w1': jax.random.normal(k2, (E, I, H), jnp.float32) * H ** (-0.5), 'w2': jax.random.normal(k3, (E, H, I), jnp.float32) * I ** (-0.5), 'w3': jax.random.normal(k4, (E, I, H), jnp.float32) * H ** (-0.5)}
    _L1_ffn_in = _L1_ffn_setup()
    _L1_c = _w((lambda *s: np.random.randn(*s).astype(np.float32) * 0.05)(16, 128))
    _L1_wmod = _w((lambda *s: np.random.randn(*s).astype(np.float32) * 0.05)(128, 6 * 128) * 128 ** (-0.5))
    _d = {'L0_attn_x': _L0_attn_in['x'], 'L0_attn_Wq': _L0_attn_in['Wq'], 'L0_attn_Wk': _L0_attn_in['Wk'], 'L0_attn_Wv': _L0_attn_in['Wv'], 'L0_attn_Wo': _L0_attn_in['Wo'], 'L0_attn_gn_weight': _L0_attn_in['gn_weight'], 'L0_attn_gn_bias': _L0_attn_in['gn_bias'], 'L0_ffn_gate_w': _L0_ffn_in['gate_w'], 'L0_ffn_w1': _L0_ffn_in['w1'], 'L0_ffn_w2': _L0_ffn_in['w2'], 'L0_c': _L0_c, 'L0_wmod': _L0_wmod, 'L1_attn_W_in': _L1_attn_in['W_in'], 'L1_attn_W_dt': _L1_attn_in['W_dt'], 'L1_attn_b_dt': _L1_attn_in['b_dt'], 'L1_attn_A_log': _L1_attn_in['A_log'], 'L1_attn_D': _L1_attn_in['D'], 'L1_attn_conv_w': _L1_attn_in['conv_w'], 'L1_attn_conv_b': _L1_attn_in['conv_b'], 'L1_attn_W_out': _L1_attn_in['W_out'], 'L1_attn_ln_g': _L1_attn_in['ln_g'], 'L1_attn_ln_b': _L1_attn_in['ln_b'], 'L1_ffn_rms_weight': _L1_ffn_in['rms_weight'], 'L1_ffn_gate_w': _L1_ffn_in['gate_w'], 'L1_ffn_w1': _L1_ffn_in['w1'], 'L1_ffn_w2': _L1_ffn_in['w2'], 'L1_ffn_w3': _L1_ffn_in['w3'], 'L1_c': _L1_c, 'L1_wmod': _L1_wmod}
    _x0 = _d['L0_attn_x']
    _d['L0_attn_x'] = jax.random.normal(jax.random.fold_in(jax.random.key(seed), 1), (16, 256, 128), dtype=_x0.dtype)
    del _x0
    return _d

def reference(L0_attn_x, L0_attn_Wq, L0_attn_Wk, L0_attn_Wv, L0_attn_Wo, L0_attn_gn_weight, L0_attn_gn_bias, L0_ffn_gate_w, L0_ffn_w1, L0_ffn_w2, L0_c, L0_wmod, L1_attn_W_in, L1_attn_W_dt, L1_attn_b_dt, L1_attn_A_log, L1_attn_D, L1_attn_conv_w, L1_attn_conv_b, L1_attn_W_out, L1_attn_ln_g, L1_attn_ln_b, L1_ffn_rms_weight, L1_ffn_gate_w, L1_ffn_w1, L1_ffn_w2, L1_ffn_w3, L1_c, L1_wmod):

    def _L0_attn_ref(x, Wq, Wk, Wv, Wo, gn_weight, gn_bias):
        import math
        import jax, jax.numpy as jnp
        import numpy as np
        N_HEADS = 8
        EPS = 1e-05
        B, L, D = x.shape
        H = N_HEADS
        dh = D // H
        gammas = 1.0 - jnp.exp(jnp.linspace(math.log(1.0 / 32.0), math.log(1.0 / 512.0), H)).astype(x.dtype)

        def proj(W):
            return (x @ W.T).reshape(B, L, H, dh).transpose(1, 0, 2, 3)
        qT, kT, vT = (proj(Wq), proj(Wk), proj(Wv))
        g = gammas[None, :, None, None]

        def step(S, qkv_t):
            q_t, k_t, v_t = qkv_t
            S = g * S + k_t[..., :, None] * v_t[..., None, :]
            y_t = jnp.einsum('bhde,bhd->bhe', S, q_t)
            return (S, y_t)
        S0 = jnp.zeros((B, H, dh, dh), dtype=x.dtype)
        _, ys = jax.lax.scan(step, S0, (qT, kT, vT))
        out = ys.transpose(1, 0, 2, 3)
        mean = out.mean(axis=(1, 3), keepdims=True)
        var = out.var(axis=(1, 3), keepdims=True)
        out = (out - mean) * jax.lax.rsqrt(var + EPS)
        out = out.reshape(B, L, D) * gn_weight + gn_bias
        return out @ Wo.T

    def _L0_ffn_ref(x, gate_w, w1, w2):
        import jax, jax.numpy as jnp
        import numpy as np
        NUM_EXPERTS = 8
        EXPERT_CAPACITY = 2.0
        B, T, C = x.shape
        E = gate_w.shape[1]
        cap = int(EXPERT_CAPACITY * T / E)
        scores = jnp.einsum('BTC,CE->BTE', x, gate_w)
        probs = jax.nn.softmax(scores, axis=-1)
        probs_et = jnp.transpose(probs, (0, 2, 1))
        top_p, top_idx = jax.lax.top_k(probs_et, cap)
        xin = jnp.take_along_axis(x[:, None, :, :], top_idx[..., None], axis=2)
        h = jax.nn.gelu(jnp.einsum('BElC,ECH->BElH', xin, w1), approximate=False)
        y = jnp.einsum('BElH,EHC->BElC', h, w2)
        y = y * top_p[..., None]
        b_idx = jnp.arange(B)[:, None, None]
        out = jnp.zeros((B, T, C), x.dtype).at[b_idx, top_idx].add(y)
        return out

    def _L1_attn_ref(x, W_in, W_dt, b_dt, A_log, D, conv_w, conv_b, W_out, ln_g, ln_b):
        import jax, jax.numpy as jnp
        import numpy as np
        D_MODEL = 128
        D_STATE = 16
        D_CONV = 4
        EXPAND = 2
        D_INNER = D_MODEL * EXPAND
        DT_RANK = max(1, D_MODEL // 16)
        BSZ, SEQ = (2, 256)
        LN_EPS = 1e-05

        def _silu(v):
            return v * jax.nn.sigmoid(v)

        def _selective_scan(u, delta, A, B_s, C_s, D):
            b, l, d = u.shape
            n = A.shape[1]
            h0 = jnp.zeros((b, d, n), dtype=u.dtype)
            sw = lambda a: jnp.swapaxes(a, 0, 1)

            def step(h, inp):
                dt_t, u_t, b_t, c_t = inp
                dA = jnp.exp(dt_t[..., None] * A)
                h = dA * h + dt_t[..., None] * b_t[:, None, :] * u_t[..., None]
                y = jnp.einsum('bdn,bn->bd', h, c_t)
                return (h, y)
            _, ys = jax.lax.scan(step, h0, (sw(delta), sw(u), sw(B_s), sw(C_s)))
            return jnp.swapaxes(ys, 0, 1) + u * D[None, None, :]
        residual = x
        b, l, _ = x.shape
        proj = jnp.einsum('bld,od->blo', x, W_in)
        x_s, z, B_s, C_s, dt = jnp.split(proj, [D_INNER, 2 * D_INNER, 2 * D_INNER + D_STATE, 2 * D_INNER + 2 * D_STATE], axis=-1)
        xc = jnp.transpose(x_s, (0, 2, 1))
        xc = jax.lax.conv_general_dilated(xc, conv_w, window_strides=(1,), padding=[(D_CONV - 1, D_CONV - 1)], feature_group_count=D_INNER, dimension_numbers=('NCH', 'OIH', 'NCH'))
        xc = xc[..., :l] + conv_b[None, :, None]
        x_s = _silu(jnp.transpose(xc, (0, 2, 1)))
        dt = jax.nn.softplus(jnp.einsum('blr,dr->bld', dt, W_dt) + b_dt)
        A = -jnp.exp(A_log)
        y = _selective_scan(x_s, dt, A, B_s, C_s, D)
        y = y * _silu(z)
        out = residual + jnp.einsum('bld,od->blo', y, W_out)
        mu = jnp.mean(out, axis=-1, keepdims=True)
        var = jnp.mean(jnp.square(out - mu), axis=-1, keepdims=True)
        return (out - mu) * jax.lax.rsqrt(var + LN_EPS) * ln_g + ln_b

    def _L1_ffn_ref(hidden_states, rms_weight, gate_w, w1, w2, w3):
        import jax, jax.numpy as jnp
        import numpy as np
        EPS = 1e-06
        TOP_K = 2
        B, S, H = hidden_states.shape
        E = gate_w.shape[0]
        x = hidden_states.astype(jnp.float32)
        var = jnp.mean(x * x, axis=-1, keepdims=True)
        h = rms_weight * (x * jax.lax.rsqrt(var + EPS))
        logits = jnp.einsum('bsh,eh->bse', h, gate_w)
        scores = jax.nn.softmax(logits.astype(jnp.float32), axis=-1)
        top_w, top_i = jax.lax.top_k(scores, TOP_K)
        top_w = top_w / jnp.sum(top_w, axis=-1, keepdims=True)
        top_w = top_w.astype(h.dtype)
        hf = h.reshape(-1, H)
        oh = jax.nn.one_hot(top_i.reshape(-1, TOP_K), E, dtype=h.dtype)
        cw = jnp.einsum('tke,tk->te', oh, top_w.reshape(-1, TOP_K))
        a = jnp.einsum('th,eih->eti', hf, w1)
        g = jnp.einsum('th,eih->eti', hf, w3)
        eo = jnp.einsum('eti,ehi->eth', jax.nn.silu(a) * g, w2)
        out = jnp.einsum('eth,te->th', eo, cw)
        return hidden_states + out.reshape(B, S, H)
    x = L0_attn_x
    mod = (_silu(L0_c) @ L0_wmod).reshape(L0_c.shape[0], 6, 1, -1)
    sa, ca, ga, sb, cb, gb = (mod[:, 0], mod[:, 1], mod[:, 2], mod[:, 3], mod[:, 4], mod[:, 5])
    ga = (2 * (ga >= 0) - 1) * jnp.maximum(jnp.abs(ga), 0.25)
    gb = (2 * (gb >= 0) - 1) * jnp.maximum(jnp.abs(gb), 0.25)
    h = _layernorm(x, axis=-1) * (1 + ca) + sa
    x = x + ga * _L0_attn_ref(h, L0_attn_Wq, L0_attn_Wk, L0_attn_Wv, L0_attn_Wo, L0_attn_gn_weight, L0_attn_gn_bias)
    h = _layernorm(x, axis=-1) * (1 + cb) + sb
    x = x + gb * _L0_ffn_ref(h, L0_ffn_gate_w, L0_ffn_w1, L0_ffn_w2)
    mod = (_silu(L1_c) @ L1_wmod).reshape(L1_c.shape[0], 6, 1, -1)
    sa, ca, ga, sb, cb, gb = (mod[:, 0], mod[:, 1], mod[:, 2], mod[:, 3], mod[:, 4], mod[:, 5])
    ga = (2 * (ga >= 0) - 1) * jnp.maximum(jnp.abs(ga), 0.25)
    gb = (2 * (gb >= 0) - 1) * jnp.maximum(jnp.abs(gb), 0.25)
    h = _layernorm(x, axis=-1) * (1 + ca) + sa
    x = x + ga * _L1_attn_ref(h, L1_attn_W_in, L1_attn_W_dt, L1_attn_b_dt, L1_attn_A_log, L1_attn_D, L1_attn_conv_w, L1_attn_conv_b, L1_attn_W_out, L1_attn_ln_g, L1_attn_ln_b)
    h = _layernorm(x, axis=-1) * (1 + cb) + sb
    x = x + gb * _L1_ffn_ref(h, L1_ffn_rms_weight, L1_ffn_gate_w, L1_ffn_w1, L1_ffn_w2, L1_ffn_w3)
    return x

_drawn_inputs = setup_inputs


def setup_inputs(seed=0):
    import zlib

    import numpy as np

    out = dict(_drawn_inputs(seed))
    spreads = {'L0_attn_gn_weight': (1.0, 0.6),
     'L0_attn_gn_bias': (0.0, 0.8),
     'L1_attn_D': (1.0, 0.6),
     'L1_attn_ln_g': (1.0, 0.2),
     'L1_attn_ln_b': (0.0, 0.306),
     'L1_ffn_rms_weight': (1.0, 0.2)}
    factors = {'L0_ffn_gate_w': 8.0,
     'L0_ffn_w1': 8.0,
     'L0_ffn_w2': 8.0,
     'L1_attn_W_in': 8.0,
     'L1_attn_W_dt': 8.0,
     'L1_attn_b_dt': 8.0,
     'L1_attn_A_log': 8.0,
     'L1_attn_conv_w': 8.0,
     'L1_attn_conv_b': 8.0,
     'L1_attn_W_out': 8.0}
    for name, (base, spread) in spreads.items():
        noise = np.random.default_rng([zlib.crc32(name.encode()), seed]).standard_normal(out[name].shape)
        drawn = base * np.exp(spread * noise) if base else spread * noise
        out[name] = jnp.asarray(drawn.astype(out[name].dtype))
    for name, factor in factors.items():
        out[name] = (out[name] * factor).astype(out[name].dtype)
    return out
```

```python
from contextlib import ExitStack

import numpy as np

import concourse.bass as bass
from concourse import mybir

F32 = mybir.dt.float32
BF16 = mybir.dt.bfloat16
U32 = mybir.dt.uint32
ALU = mybir.AluOpType
ACT = mybir.ActivationFunctionType
AX = mybir.AxisListType.X

P = 128
B, L, D = 16, 256, 128
NCH = L // P
PAIRS = B // 2
TILES = B * NCH
HEADS, DH = 8, 16
E0, CAP, H0 = 8, 64, 512
HC0 = H0 // P
DI, NST, KCONV, RDT = 256, 16, 4, 8
NH = DI // P
E1, I1, TOPK = 8, 448, 2
IC, NIC = 112, I1 // 112
LN_EPS, RMS_EPS = 1e-5, 1e-6
EXPLN = "natural_log_exp_and_others"

C_DEC, C_INV, C_INVT, C_TRI, C_BLK, C_AVG, C_ID = 0, 256, 512, 640, 768, 896, 1024
C_PAR, C_IOTA, C_IOTA8, C_REP = 1152, 1154, 1218, 1226
C_T72, C_I128, C_VAL, C_PAD, C_END = 1258, 1330, 1458, 1522, 1594


def constants():
    gam = (1.0 - np.exp(np.linspace(np.log(1 / 32), np.log(1 / 512), HEADS)).astype(np.float32)).astype(np.float64)
    p = np.arange(P)
    g = gam[p // DH]
    t = np.arange(L)
    c = np.zeros((P, C_END), np.float32)
    c[:, C_DEC:C_DEC + L] = g[:, None] ** t
    c[:, C_INV:C_INV + L] = g[:, None] ** -t.astype(np.float64)
    c[:, C_INVT:C_INVT + P] = g[None, :] ** -p[:, None].astype(np.float64)
    c[:, C_TRI:C_TRI + P] = p[:, None] <= p[None, :]
    same = p[:, None] // DH == p[None, :] // DH
    c[:, C_BLK:C_BLK + P] = same
    c[:, C_AVG:C_AVG + P] = same / DH
    c[:, C_ID:C_ID + P] = np.eye(P)
    c[:, C_PAR] = (p // DH) % 2 == 0
    c[:, C_PAR + 1] = (p // DH) % 2 == 1
    c[:, C_IOTA:C_IOTA + CAP] = np.arange(1, CAP + 1)
    c[:, C_IOTA8:C_IOTA8 + E1] = np.arange(E1)
    c[:, C_REP:C_REP + 32] = p[:, None] % 32 == np.arange(32)[None, :]
    tiles = np.arange(72)
    c[:, C_T72:C_T72 + 72] = tiles
    c[:, C_I128:C_I128 + P] = p
    rank, tile = np.divmod(np.arange(B * L * TOPK // P), TILES)
    c[:, C_VAL:C_VAL + 64] = 1 + TOPK * (P * tile[None, :] + p[:, None]) + rank[None, :]
    c[:, C_PAD:C_PAD + 72] = B * L * TOPK + P * tiles[None, :] + p[:, None]
    return c


def ticker(eng, sem, per_round=0):
    n = [0]

    def tick(ins):
        ins.then_inc(sem, 1)
        n[0] += 1

    def settle(rnd=0):
        eng.wait_ge(sem, rnd * per_round + n[0])

    def ends():
        assert n[0] == per_round, (sem, n[0], per_round)

    return tick, settle, ends


def pause(eng, passed):
    eng.sem_inc(passed, 1)


def semaphores(nc, ctx, prefix=""):
    taken = []

    def clear():
        nc.clear_and_free_semaphores(taken)
        nc.all_engine_barrier()

    def sem(n):
        taken.append(nc.alloc_semaphore(name=prefix + n))
        return taken[-1]

    ctx.callback(clear)
    return sem


class Mem:
    pass


def setup_phase(nc, d, m, ps):
    with ExitStack() as ctx:
        sem = semaphores(nc, ctx)

        def sb(n, s, dt=F32):
            return ctx.enter_context(nc.sbuf_tensor(n, s, dt))

        cT = sb("cT", [P, 2, B])
        wmod = sb("wmod", [P, 2, 6 * D])
        lnrow = sb("lnrow", [B, 2, D])
        sgn = sb("sgn", [B, 2, 2 * D])
        mag = sb("mag", [B, 2, 2 * D])
        s_c, s_w, s_x, s_sc, s_mod, s_row = (sem("ld_c"), sem("ld_mod"), sem("ld_x"), sem("silu_c"),
                                             sem("mod_ps"), sem("v_own0"))
        block = ctx.enter_context(nc.Block())
        BIG = [(m.x_res[:, 8 * i:8 * i + 8, :],
                d["x"][4 * i:4 * i + 4].rearrange("b (c t) d -> t (b c) d", t=P)) for i in range(4)]
        SMALL = [(m.wq, d["wqT"]), (m.wk, d["wkT"]), (m.wv, d["wvT"]), (m.wo, d["woT"]), (m.gate0, d["gate0"]),
                 (m.gn, d["gn"]), (m.w_in, d["winT"]), (m.bcol, d["cols"]), (m.gate1, d["gate1T"]),
                 (m.w_outT, d["woutT"]), (m.wdt[96:96 + RDT, :], d["wdtT"])]

        @block.sync
        def _(sp):
            sp.dma_start(cT[:], d["cT"]).then_inc(s_c, 16)
            sp.dma_start(lnrow[:], d["lnrow"]).then_inc(s_c, 16)
            sp.dma_start(wmod[:], d["wmod"]).then_inc(s_w, 16)
            sp.dma_start(m.const[:], d["const"]).then_inc(s_w, 16)
            for dst, src in BIG:
                sp.dma_start(dst, src).then_inc(s_x, 16)
            for dst, src in SMALL:
                sp.dma_start(dst if dst is not m.wdt else dst, src).then_inc(s_x, 16)
            sp.wait_ge(s_x, 16 * (len(BIG) + len(SMALL)))

        @block.scalar
        def _(act):
            act.wait_ge(s_c, 32)
            act.activation(m.silu_c[:], cT[:], ACT.Silu).then_inc(s_sc, 1)

        @block.tensor
        def _(pe):
            pe.wait_ge(s_sc, 1)
            pe.wait_ge(s_w, 32)
            for ly in range(2):
                for k, w in enumerate((0, 1, 3, 4)):
                    pe.matmul(ps[ly][:, k * B:(k + 1) * B], wmod[:, ly, w * D:(w + 1) * D], m.silu_c[:, ly, :],
                              start=True, stop=True)
                for k, w in enumerate((2, 5)):
                    mm = pe.matmul(ps[2 + ly][0:B, k * D:(k + 1) * D], m.silu_c[:, ly, :],
                                   wmod[:, ly, w * D:(w + 1) * D], start=True, stop=True)
            mm.then_inc(s_mod, 1)

        @block.vector
        def _(dve):
            tick, settle, _ = ticker(dve, s_row)
            tick(dve.memset(m.eps[:, 0:1], LN_EPS))
            tick(dve.memset(m.eps[:, 1:2], RMS_EPS))
            tick(dve.memset(m.eps[:, 2:3], 1.0))
            tick(dve.memset(m.ones16[:], 1.0))
            tick(dve.memset(m.ones128[:], 1.0 / D))
            dve.wait_ge(s_mod, 1)
            for ly in range(2):
                for k in range(4):
                    tick(dve.tensor_scalar(m.modT[:, ly, k, :], ps[ly][:, k * B:(k + 1) * B],
                                           float(k % 2), None, ALU.add))
                rows = ps[2 + ly][0:B, 0:2 * D]
                tick(dve.tensor_scalar(sgn[:, ly, :], rows, 0.0, 2.0, ALU.is_ge, ALU.mult))
            settle()
            tick(dve.tensor_scalar(sgn[:], sgn[:], -1.0, None, ALU.add))
            settle()
            for ly in range(2):
                tick(dve.tensor_tensor(mag[:, ly, :], sgn[:, ly, :], ps[2 + ly][0:B, 0:2 * D], ALU.mult))
            settle()
            for ly in range(2):
                tick(dve.scalar_tensor_tensor(m.gates[:, ly, 0:2 * D], mag[:, ly, :], 0.25, sgn[:, ly, :],
                                              ALU.max, ALU.mult))
            settle()
            dve.wait_ge(s_c, 32)
            tick(dve.tensor_tensor(m.gates[:, 1, 2 * D:3 * D], m.gates[:, 1, 0:D], lnrow[:, 1, :], ALU.mult))
            settle()
            tick(dve.tensor_tensor(m.gates[:, 1, 0:D], m.gates[:, 1, 0:D], lnrow[:, 0, :], ALU.mult))
            settle()


A1_DVE = 35
A1_ACT = 3


def attention_phase(nc, d, m, ps):
    with ExitStack() as ctx:
        sem = semaphores(nc, ctx)

        def sb(n, s, dt=F32):
            return ctx.enter_context(nc.sbuf_tensor(n, s, dt))

        Q = 2 * NCH
        stats = sb("stats", [P, Q, 6])
        mv = sb("mv", [P, Q, 2])
        lnv = sb("lnv", [P, Q])
        rstd = sb("rstd", [P, Q])
        xn = sb("xn", [P, Q, D])
        hT = sb("hT", [P, 2, L])
        qm = sb("qm", [P, 2, 2, L])
        kd = sb("kd", [P, 2, L])
        kt0 = sb("kt0", [P, 2, D])
        v = sb("v", [P, Q, D])
        state = sb("state", [P, 2, D])
        prob = sb("prob", [P, 2, 4, 2 * NCH, P])
        y = sb("y", [P, Q, D])
        gst = sb("gst", [P, 2, 6])
        gmv = sb("gmv", [P, 2, 2])
        gin = sb("gin", [P, 2, 2])
        gm = sb("gm", [P, 2, 2])
        gvar = sb("gvar", [P, 2])
        gr = sb("gr", [P, 2])
        gsc = sb("gsc", [P, 2])
        gbi = sb("gbi", [P, 2])
        ynT = sb("ynT", [P, 2, L])
        gsel = sb("gsel", [B, 2, 2 * D])
        gate = sb("gate", [P, 2, 2 * D])
        att = sb("att", [P, Q, D])
        h2T = sb("h2T", [P, 2, L])
        mx = sb("mx", [P, Q])
        sh = sb("sh", [P, Q, E0])
        ex = sb("ex", [P, Q, E0])
        sm = sb("sm", [P, Q])
        rs = sb("rs", [P, Q])

        names = ("v_own v_passed a_own ln_stats ln_rstd xn_ready xn_T h_ready proj_ps qk_ready v_sb state_ps state_sb "
                 "score_ps score_sb y_ps y_sb yT_ps gn_in gn_ps gn_var gn_rstd gn_aff yn_ready out_ps gsel_ready "
                 "gate_ps gate_sb x_stats x_rstd x_norm x_T h2_ready rt_ps rt_shift rt_exp").split()
        S = {n: sem("a1_" + n) for n in names}
        ident = m.const[:, C_ID:C_ID + P]
        block = ctx.enter_context(nc.Block())
        bT, bQ, bK, bV = ps[0], ps[1], ps[2], ps[3]
        bS = ps[4:8]

        @block.vector
        def _(dve):
            with dve.Fori(0, PAIRS, 1) as r:
                tick, settle, ends = ticker(dve, S["v_own"], A1_DVE)

                def stats_of():
                    pause(dve, S["v_passed"])
                    for q in range(Q):
                        tick(dve.bn_stats(stats[:, q, :], m.x_res[:, r * Q + q, :]))
                    settle(r)
                    pause(dve, S["v_passed"])
                    for q in range(Q):
                        ins = dve.bn_aggr(mv[:, q, :], stats[:, q, :])
                        if q < Q - 1:
                            tick(ins)
                    return ins

                stats_of().then_inc(S["ln_stats"], 1)
                dve.wait_ge(S["ln_rstd"], r + 1)
                dve.wait_ge(S["ln_stats"], r + 1)
                for q in range(Q):
                    ins = dve.tensor_scalar(xn[:, q, :], m.x_res[:, r * Q + q, :], mv[:, q, 0:1], rstd[:, q:q + 1],
                                            ALU.subtract, ALU.mult)
                    ins.then_inc(S["xn_ready"], 1)
                for k in range(2):
                    dve.tensor_scalar(gsel[:, k, :], m.gates[:, 0, 0:2 * D], m.const[0:B, bass.ds(C_ID + 2 * r + k, 1)],
                                      None, ALU.mult).then_inc(S["gsel_ready"], 1)
                dve.wait_ge(S["proj_ps"], r + 1)
                dec = m.const[:, C_DEC:C_DEC + L].unsqueeze(1).broadcast_to([P, 2, L])
                inv = m.const[:, C_INV:C_INV + L].unsqueeze(1).broadcast_to([P, 2, L])
                invt = m.const[:, C_INVT:C_INVT + D].unsqueeze(1).broadcast_to([P, 2, D])
                v3 = lambda b_: b_[:, :].rearrange("p (s t) -> p s t", s=2)
                dve.tensor_tensor(kt0[:], ps[4][:, 0:2 * D].rearrange("p (s d) -> p s d", s=2), invt,
                                  ALU.mult).then_inc(S["qk_ready"], 1)
                dve.tensor_tensor(kd[:], v3(bK), inv, ALU.mult).then_inc(S["qk_ready"], 1)
                for k in range(2):
                    dve.scalar_tensor_tensor(qm[:, k], v3(bQ), m.const[:, C_PAR + k:C_PAR + k + 1], dec,
                                             ALU.mult, ALU.mult).then_inc(S["qk_ready"], 1)
                dve.wait_ge(S["state_ps"], r + 1)
                blk = m.const[:, C_BLK:C_BLK + D].unsqueeze(1).broadcast_to([P, 2, D])
                dve.tensor_tensor(state[:], ps[4][:, 2 * D:4 * D].rearrange("p (s d) -> p s d", s=2), blk,
                                  ALU.mult).then_inc(S["state_sb"], 1)
                tri = m.const[:, C_TRI:C_TRI + P].unsqueeze(1).broadcast_to([P, 4, P])
                for k in range(2):
                    for j in range(4):
                        dve.wait_ge(S["score_ps"], r * 8 + k * 4 + j + 1)
                        dve.tensor_tensor(prob[:, k, j], bS[j][:, :].rearrange("p (a t) -> p a t", a=4), tri,
                                          ALU.mult).then_inc(S["score_sb"], 1)
                dve.wait_ge(S["yT_ps"], r + 1)
                for k in range(2):
                    tick(dve.bn_stats(gst[:, k, :], bT[:, k * L:(k + 1) * L]))
                settle(r)
                pause(dve, S["v_passed"])
                for k in range(2):
                    tick(dve.bn_aggr(gmv[:, k, :], gst[:, k, :]))
                settle(r)
                tick(dve.tensor_tensor(gin[:, :, 1], gmv[:, :, 0], gmv[:, :, 0], ALU.mult))
                tick(dve.tensor_copy(gin[:, :, 0], gmv[:, :, 0]))
                settle(r)
                dve.tensor_tensor(gin[:, :, 1], gin[:, :, 1], gmv[:, :, 1], ALU.add).then_inc(S["gn_in"], 1)
                dve.wait_ge(S["gn_ps"], r + 1)
                tick(dve.tensor_copy(gm[:], ps[3][:, 0:4].rearrange("p (s k) -> p s k", s=2)))
                settle(r)
                tick(dve.tensor_tensor(gvar[:], gm[:, :, 0], gm[:, :, 0], ALU.mult))
                settle(r)
                tick(dve.tensor_tensor(gvar[:], gm[:, :, 1], gvar[:], ALU.subtract))
                settle(r)
                dve.tensor_scalar(gvar[:], gvar[:], 0.0, None, ALU.max).then_inc(S["gn_var"], 1)
                dve.wait_ge(S["gn_rstd"], r + 1)
                tick(dve.tensor_scalar(gsc[:], gr[:], m.gn[:, 0:1], None, ALU.mult))
                settle(r)
                tick(dve.tensor_tensor(gbi[:], gm[:, :, 0], gsc[:], ALU.mult))
                settle(r)
                dve.tensor_scalar(gbi[:], gbi[:], -1.0, m.gn[:, 1:2], ALU.mult, ALU.add).then_inc(S["gn_aff"], 1)
                dve.wait_ge(S["out_ps"], r + 1)
                dve.wait_ge(S["gate_sb"], r + 1)
                for k in range(2):
                    tick(dve.tensor_tensor(att[:, 2 * k:2 * k + 2, :],
                                           bQ[:, k * L:(k + 1) * L].rearrange("p (c d) -> p c d", c=2),
                                           gate[:, k, 0:D].unsqueeze(1).broadcast_to([P, NCH, D]), ALU.mult))
                settle(r)
                tick(dve.tensor_tensor(m.x_res[:, bass.ts(r, Q), :], att[:], m.x_res[:, bass.ts(r, Q), :], ALU.add))
                settle(r)
                stats_of().then_inc(S["x_stats"], 1)
                dve.wait_ge(S["x_rstd"], r + 1)
                dve.wait_ge(S["x_stats"], r + 1)
                for q in range(Q):
                    dve.tensor_scalar(m.xn2[:, r * Q + q, :], m.x_res[:, r * Q + q, :], mv[:, q, 0:1],
                                      rstd[:, q:q + 1], ALU.subtract, ALU.mult).then_inc(S["x_norm"], 1)
                    dve.tensor_scalar(xn[:, q, :], m.x_res[:, r * Q + q, :], mv[:, q, 0:1],
                                      rstd[:, q:q + 1], ALU.subtract, ALU.mult).then_inc(S["x_norm"], 1)
                dve.wait_ge(S["rt_ps"], r + 1)
                lg = bQ[:, 0:Q * E0].rearrange("p (q e) -> p q e", q=Q)
                tick(dve.tensor_reduce(mx[:], lg, AX, ALU.max))
                settle(r)
                dve.tensor_tensor(sh[:], lg, mx[:].unsqueeze(2).broadcast_to([P, Q, E0]),
                                  ALU.subtract).then_inc(S["rt_shift"], 1)
                dve.wait_ge(S["rt_exp"], r + 1)
                tick(dve.tensor_reduce(sm[:], ex[:], AX, ALU.add))
                settle(r)
                tick(dve.reciprocal(rs[:], sm[:]))
                settle(r)
                for q in range(Q):
                    tick(dve.tensor_scalar(m.probs[:, q % NCH, bass.ds(r * 2 * E0 + (q // NCH) * E0, E0)],
                                           ex[:, q, :], rs[:, q:q + 1], None, ALU.mult))
                settle(r)
                ends()

        @block.scalar
        def _(act):
            act.preload_act_table_set(EXPLN)
            with act.Fori(0, PAIRS, 1) as r:
                tick, settle, ends = ticker(act, S["a_own"], A1_ACT)

                def rsqrt(out, tmp, var, eps):
                    tick(act.activation(tmp, var, ACT.Ln, bias=eps))
                    settle(r)
                    return act.activation(out, tmp, ACT.Exp, scale=-0.5)

                act.wait_ge(S["ln_stats"], r + 1)
                rsqrt(rstd[:], lnv[:], mv[:, :, 1], m.eps[:, 0:1]).then_inc(S["ln_rstd"], 1)
                act.wait_ge(S["xn_T"], r + 1)
                for k in range(2):
                    act.activation(hT[:, k, :], bT[:, k * L:(k + 1) * L], ACT.Identity,
                                   bias=m.modT[:, 0, 0, bass.ds(2 * r + k, 1)],
                                   scale=m.modT[:, 0, 1, bass.ds(2 * r + k, 1)]).then_inc(S["h_ready"], 1)
                act.wait_ge(S["proj_ps"], r + 1)
                act.activation(v[:], bV[:, :].rearrange("p (q d) -> p q d", q=Q), ACT.Copy).then_inc(S["v_sb"], 1)
                act.wait_ge(S["y_ps"], r + 1)
                for c in range(NCH):
                    act.activation(y[:, c:Q:NCH, :], ps[1 + c][:, 0:2 * D].rearrange("p (s d) -> p s d", s=2),
                                   ACT.Copy).then_inc(S["y_sb"], 1)
                act.wait_ge(S["gn_var"], r + 1)
                rsqrt(gr[:], lnv[:, 0:2], gvar[:], m.eps[:, 0:1]).then_inc(S["gn_rstd"], 1)
                act.wait_ge(S["gn_aff"], r + 1)
                for k in range(2):
                    act.activation(ynT[:, k, :], bT[:, k * L:(k + 1) * L], ACT.Identity, bias=gbi[:, k:k + 1],
                                   scale=gsc[:, k:k + 1]).then_inc(S["yn_ready"], 1)
                act.wait_ge(S["gate_ps"], r + 1)
                act.activation(gate[:], bK[:, :].rearrange("p (s d) -> p s d", s=2), ACT.Copy).then_inc(S["gate_sb"], 1)
                act.wait_ge(S["x_stats"], r + 1)
                rsqrt(rstd[:], lnv[:], mv[:, :, 1], m.eps[:, 0:1]).then_inc(S["x_rstd"], 1)
                act.wait_ge(S["x_T"], r + 1)
                for k in range(2):
                    act.activation(h2T[:, k, :], bV[:, k * L:(k + 1) * L], ACT.Identity,
                                   bias=m.modT[:, 0, 2, bass.ds(2 * r + k, 1)],
                                   scale=m.modT[:, 0, 3, bass.ds(2 * r + k, 1)]).then_inc(S["h2_ready"], 1)
                act.wait_ge(S["rt_shift"], r + 1)
                act.activation(ex[:], sh[:], ACT.Exp).then_inc(S["rt_exp"], 1)
                ends()

        @block.tensor
        def _(pe):
            with pe.Fori(0, PAIRS, 1) as r:
                pe.wait_ge(S["xn_ready"], (r + 1) * Q)
                for q in range(Q):
                    mm = pe.transpose(bT[:, q * P:(q + 1) * P], xn[:, q, :], ident)
                mm.then_inc(S["xn_T"], 1)
                pe.wait_ge(S["h_ready"], (r + 1) * 2)
                for k in range(2):
                    pe.matmul(ps[4][:, k * D:(k + 1) * D], hT[:, k, 0:P], m.wk, start=True, stop=True)
                flat = hT[:].rearrange("p s t -> p (s t)")
                pe.matmul(bK[:, :], m.wk, flat, start=True, stop=True)
                pe.matmul(bQ[:, :], m.wq, flat, start=True, stop=True)
                for q in range(Q):
                    mm = pe.matmul(bV[:, q * D:(q + 1) * D], flat[:, q * P:(q + 1) * P], m.wv, start=True, stop=True)
                mm.then_inc(S["proj_ps"], 1)
                pe.wait_ge(S["v_sb"], r + 1)
                pe.wait_ge(S["qk_ready"], r * 4 + 1)
                for k in range(2):
                    mm = pe.matmul(ps[4][:, (2 + k) * D:(3 + k) * D], kt0[:, k, :], v[:, k * NCH, :],
                                   start=True, stop=True)
                mm.then_inc(S["state_ps"], 1)
                pe.wait_ge(S["qk_ready"], (r + 1) * 4)
                for k in range(2):
                    for j in range(4):
                        if k == 0 and j == 0:
                            pe.wait_ge(S["state_sb"], r + 1)
                        if k == 1:
                            pe.wait_ge(S["score_sb"], r * 8 + j + 1)
                        for c in range(NCH):
                            rows = slice(32 * j, 32 * j + 32)
                            mm = pe.matmul(bS[j][:, c * 2 * P:(c + 1) * 2 * P].rearrange("p (a t) -> p a t", a=2),
                                           kd[rows, k, c * P:(c + 1) * P], qm[rows, :, k, c * P:(c + 1) * P],
                                           start=True, stop=True)
                        mm.then_inc(S["score_ps"], 1)
                for k in range(2):
                    pe.wait_ge(S["score_sb"], r * 8 + 4 * k + 4)
                    for a in range(2):
                        pe.matmul(ps[2][:, k * D:(k + 1) * D], qm[:, a, k, P:L], state[:, k, :],
                                  start=(a == 0), stop=False, skip_group_check=True)
                    for c in (1, 0):
                        for h in range(HEADS):
                            col = slice(k * D + h * DH, k * D + (h + 1) * DH)
                            mm = pe.matmul(ps[1 + c][:, col], prob[:, k, h // 2, 2 * c + h % 2, :],
                                           v[:, k * NCH + c, h * DH:(h + 1) * DH], start=(c == 0), stop=True,
                                           skip_group_check=(c == 1))
                mm.then_inc(S["y_ps"], 1)
                pe.wait_ge(S["y_sb"], (r + 1) * 2)
                for q in range(Q):
                    mm = pe.transpose(bT[:, q * P:(q + 1) * P], y[:, q, :], ident)
                mm.then_inc(S["yT_ps"], 1)
                pe.wait_ge(S["gsel_ready"], (r + 1) * 2)
                pe.matmul(bK[:, :], m.ones16[:], gsel[:].rearrange("p s d -> p (s d)"), start=True,
                          stop=True).then_inc(S["gate_ps"], 1)
                pe.wait_ge(S["gn_in"], r + 1)
                pe.matmul(ps[3][:, 0:4], m.const[:, C_AVG:C_AVG + P], gin[:].rearrange("p s k -> p (s k)"),
                          start=True, stop=True).then_inc(S["gn_ps"], 1)
                pe.wait_ge(S["yn_ready"], (r + 1) * 2)
                yf = ynT[:].rearrange("p s t -> p (s t)")
                for q in range(Q):
                    mm = pe.matmul(bQ[:, q * D:(q + 1) * D], yf[:, q * P:(q + 1) * P], m.wo, start=True, stop=True)
                mm.then_inc(S["out_ps"], 1)
                pe.wait_ge(S["x_norm"], (r + 1) * 2 * Q)
                for q in range(Q):
                    mm = pe.transpose(bV[:, q * P:(q + 1) * P], xn[:, q, :], ident)
                mm.then_inc(S["x_T"], 1)
                pe.wait_ge(S["h2_ready"], (r + 1) * 2)
                hf = h2T[:].rearrange("p s t -> p (s t)")
                for q in range(Q):
                    mm = pe.matmul(bQ[:, q * E0:(q + 1) * E0], hf[:, q * P:(q + 1) * P], m.gate0, start=True,
                                   stop=True)
                mm.then_inc(S["rt_ps"], 1)


def route_phase(nc, d, m, ps):
    with ExitStack() as ctx:
        sem = semaphores(nc, ctx)

        def sb(n, s, dt=F32):
            return ctx.enter_context(nc.sbuf_tensor(n, s, dt))

        left = sb("left", [P, L])
        top8 = sb("top8", [P, 8])
        zeros = sb("zeros", [P, L])
        taken = sb("taken", [P, L])
        place = sb("place", [P, L])
        listed = sb("listed", [P, L])
        s_in, s_own, s_out, s_back = sem("rt_in"), sem("rt_own"), sem("rt_out"), sem("rt_back")
        ident = m.const[:, C_ID:C_ID + P]
        block = ctx.enter_context(nc.Block())

        @block.tensor
        def _(pe):
            for c in range(NCH):
                mm = pe.transpose(ps[0][:, c * P:(c + 1) * P], m.probs[:, c, :], ident)
            mm.then_inc(s_in, 1)
            pe.wait_ge(s_out, 1)
            for c in range(NCH):
                mm = pe.transpose(ps[1][:, c * P:(c + 1) * P], listed[:, c * P:(c + 1) * P], ident)
            mm.then_inc(s_back, 1)

        @block.vector
        def _(dve):
            tick, settle, _ = ticker(dve, s_own)
            tick(dve.memset(zeros[:], 0.0))
            dve.wait_ge(s_in, 1)
            tick(dve.tensor_copy(left[:], ps[0][:, 0:L]))
            settle()
            for _ in range(CAP // 8):
                tick(dve.max(top8[:], left[:]))
                settle()
                tick(dve.match_replace(left[:], top8[:], left[:], -1.0))
                settle()
            tick(dve.tensor_scalar(taken[:], left[:], 0.0, None, ALU.is_lt))
            settle()
            tick(dve.tensor_tensor_scan(place[:], taken[:], zeros[:], 0.0, ALU.add, ALU.add))
            settle()
            dve.tensor_tensor(listed[:], place[:], taken[:], ALU.mult).then_inc(s_out, 1)
            dve.wait_ge(s_back, 1)
            tick(dve.tensor_copy(m.places[:], ps[1][:, 0:L].rearrange("p (c n) -> p c n", c=NCH)))
            settle()


def one_hot(dve, out, places, iota, c, first):
    return dve.tensor_tensor(out, places[:, c, bass.ds(first, E0)].unsqueeze(2).broadcast_to([P, E0, CAP]),
                             iota.unsqueeze(1).broadcast_to([P, E0, CAP]), ALU.is_equal)


def gather_phase(nc, d, m, ps):
    with ExitStack() as ctx:
        new = semaphores(nc, ctx, "")

        def sem(n):
            return [new(f"{n}{k}") for k in range(2)]

        def sb(n, s, dt=F32):
            return ctx.enter_context(nc.sbuf_tensor(n, s, dt))

        pick = sb("pick", [P, 2, NCH, E0, CAP])
        xst = sb("xst", [P, 2, NCH, D])
        picked, staged, product, taken = sem("g_picked"), sem("g_staged"), sem("g_product"), sem("g_taken")
        iota = m.const[:, C_IOTA:C_IOTA + CAP]
        block = ctx.enter_context(nc.Block())

        @block.vector
        def _(dve):
            with dve.Fori(0, PAIRS, 1) as r:
                for k in range(2):
                    dve.wait_ge(product[k], r)
                    for c in range(NCH):
                        one_hot(dve, pick[:, k, c], m.places, iota, c, r * 2 * E0 + k * E0).then_inc(picked[k], 1)

        @block.gpsimd
        def _(pool):
            with pool.Fori(0, PAIRS, 1) as r:
                for k in range(2):
                    pool.wait_ge(product[k], r)
                    pool.tensor_copy(xst[:, k], m.xn2[:, bass.ds(r * 2 * NCH + k * NCH, NCH), :]).then_inc(staged[k], 1)

        @block.tensor
        def _(pe):
            with pe.Fori(0, PAIRS, 1) as r:
                for k in range(2):
                    pe.wait_ge(staged[k], r + 1)
                    pe.wait_ge(taken[k], r)
                    for c in range(NCH):
                        pe.wait_ge(picked[k], 2 * r + c + 1)
                        mm = pe.matmul(ps[k][:, :], xst[:, k, c, :], pick[:, k, c].rearrange("p e s -> p (e s)"),
                                       start=(c == 0), stop=(c == NCH - 1))
                    mm.then_inc(product[k], 1)

        @block.scalar
        def _(act):
            with act.Fori(0, PAIRS, 1) as r:
                for k in range(2):
                    act.wait_ge(product[k], r + 1)
                    seq = bass.ds(2 * r + k, 1)
                    act.activation(m.xin[:, :, bass.ds(2 * r * CAP + k * CAP, CAP)],
                                   ps[k][:, :].rearrange("p (e s) -> p e s", e=E0), ACT.Identity,
                                   bias=m.modT[:, 0, 2, seq], scale=m.modT[:, 0, 3, seq]).then_inc(taken[k], 1)


def expert_phase(nc, d, m, ps):
    N = B * CAP // 2
    with ExitStack() as ctx:
        sem = semaphores(nc, ctx)

        def sb(n, s, dt=F32):
            return ctx.enter_context(nc.sbuf_tensor(n, s, dt))

        w1 = sb("w1", [P, 2, H0])
        w2 = sb("w2", [P, 2, HC0, D])
        g = sb("g", [P, 2, HC0, N])
        loaded = [sem(f"e_loaded{k}") for k in range(2)]
        hidden = [sem(f"e_hidden{h}") for h in range(HC0)]
        gelued = [sem(f"e_gelued{h}") for h in range(HC0)]
        result = [[sem(f"e_result{k}{a}") for a in range(2)] for k in range(2)]
        kept = [sem(f"e_kept{a}") for a in range(2)]
        block = ctx.enter_context(nc.Block())

        @block.sync
        def _(sp):
            with sp.Fori(0, E0 // 2, 1) as r:
                for k in range(2):
                    sp.wait_ge(result[k][1], r)
                    sp.dma_start(w1[:, k, :], d["w1"][bass.ds(2 * r + k, 1), :, :].rearrange(
                        "e p h -> (e p) h")).then_inc(loaded[k], 16)
                    sp.dma_start(w2[:, k], d["w2"][bass.ds(2 * r + k, 1), :, :].rearrange(
                        "e (h p) c -> p (e h) c", p=P)).then_inc(loaded[k], 16)

        @block.tensor
        def _(pe):
            with pe.Fori(0, E0 // 2, 1) as r:
                for k in range(2):
                    pe.wait_ge(loaded[k], 32 * (r + 1))
                    for a in range(2):
                        for h in range(HC0):
                            pe.wait_ge(gelued[h], 4 * r + 2 * k + a)
                            pe.matmul(ps[h][:, :], w1[:, k, h * P:(h + 1) * P],
                                      m.xin[:, 2 * r + k, a * N:(a + 1) * N], start=True,
                                      stop=True).then_inc(hidden[h], 1)
                    for a in range(2):
                        pe.wait_ge(kept[a], 2 * r + k)
                        for h in range(HC0):
                            pe.wait_ge(gelued[h], 4 * r + 2 * k + a + 1)
                            mm = pe.matmul(ps[4 + a][:, :], w2[:, k, h, :], g[:, a, h, :], start=(h == 0),
                                           stop=(h == HC0 - 1))
                        mm.then_inc(result[k][a], 1)

        @block.scalar
        def _(act):
            with act.Fori(0, E0 // 2, 1) as r:
                for k in range(2):
                    for a in range(2):
                        act.wait_ge(result[1 - k][a], r + k)
                        for h in range(HC0):
                            act.wait_ge(hidden[h], 4 * r + 2 * k + a + 1)
                            act.activation(g[:, a, h, :], ps[h][:, :], ACT.Gelu).then_inc(gelued[h], 1)

        @block.vector
        def _(dve):
            with dve.Fori(0, E0 // 2, 1) as r:
                for k in range(2):
                    for a in range(2):
                        dve.wait_ge(result[k][a], r + 1)
                        dve.tensor_copy(m.yT[:, 2 * r + k, a * N:(a + 1) * N], ps[4 + a][:, :]).then_inc(kept[a], 1)


def combine_phase(nc, d, m, ps):
    with ExitStack() as ctx:
        sem = semaphores(nc, ctx)

        def sb(n, s, dt=F32):
            return ctx.enter_context(nc.sbuf_tensor(n, s, dt))

        hot = sb("hot", [P, 2, NCH, E0, CAP])
        pick = sb("pickw", [P, 2, NCH, E0, CAP])
        pickT = sb("pickT", [P, 2, E0 // 2, L])
        yst = sb("yst", [P, 2, E0, CAP])
        ysl = sb("ysl", [P, 2, E0 // 2, D])
        gsel = sb("gsel2", [B, 2, D])
        gate = sb("gate2", [P, 2, D])
        out = sb("moe0", [P, 2, NCH, D])
        names = "hot pick yst pickT_ps pickT y_ps ysl gsel gate_ps gate out_ps prod sum".split()
        S = {n: [sem(f"c_{n}{k}") for k in range(2)] for n in names}
        ident = m.const[:, C_ID:C_ID + P]
        iota = m.const[:, C_IOTA:C_IOTA + CAP]
        block = ctx.enter_context(nc.Block())

        @block.gpsimd
        def _(pool):
            with pool.Fori(0, PAIRS, 1) as r:
                for k in range(2):
                    pool.wait_ge(S["y_ps"][k], r)
                    pool.tensor_copy(yst[:, k], m.yT[:, :, bass.ds(2 * r * CAP + k * CAP, CAP)]).then_inc(S["yst"][k], 1)

        @block.vector
        def _(dve):
            with dve.Fori(0, PAIRS, 1) as r:
                for k in range(2):
                    dve.wait_ge(S["pickT_ps"][k], r)
                    for c in range(NCH):
                        one_hot(dve, hot[:, k, c], m.places, iota, c, r * 2 * E0 + k * E0).then_inc(S["hot"][k], 1)
                    for c in range(NCH):
                        dve.wait_ge(S["hot"][k], 2 * r + c + 1)
                        dve.tensor_tensor(pick[:, k, c], hot[:, k, c],
                                          m.probs[:, c, bass.ds(r * 2 * E0 + k * E0, E0)].unsqueeze(2).broadcast_to(
                                              [P, E0, CAP]), ALU.mult).then_inc(S["pick"][k], 1)
                    if k == 0:
                        dve.wait_ge(S["gate_ps"][0], r)
                        for s in range(2):
                            dve.tensor_scalar(gsel[:, s, :], m.gates[:, 0, D:2 * D],
                                              m.const[0:B, bass.ds(C_ID + 2 * r + s, 1)], None,
                                              ALU.mult).then_inc(S["gsel"][0], 1)
                for k in range(2):
                    dve.wait_ge(S["y_ps"][k], r + 1)
                    dve.tensor_copy(ysl[:, k], ps[4 + k][:, :].rearrange("p (a d) -> p a d", d=D)).then_inc(S["ysl"][k], 1)
                dve.wait_ge(S["gate"][0], r + 1)
                for k in range(2):
                    dve.wait_ge(S["out_ps"][k], r + 1)
                    dve.tensor_tensor(out[:, k], ps[4 + k][:, 0:L].rearrange("p (c d) -> p c d", c=NCH),
                                      gate[:, k, :].unsqueeze(1).broadcast_to([P, NCH, D]),
                                      ALU.mult).then_inc(S["prod"][k], 1)
                    dve.wait_ge(S["prod"][k], r + 1)
                    xs = m.x_res[:, bass.ds(r * 2 * NCH + k * NCH, NCH), :]
                    dve.tensor_tensor(xs, out[:, k], xs, ALU.add).then_inc(S["sum"][k], 1)

        @block.tensor
        def _(pe):
            with pe.Fori(0, PAIRS, 1) as r:
                for k in range(2):
                    pe.wait_ge(S["pickT"][k], 2 * r)
                    for c in range(NCH):
                        pe.wait_ge(S["pick"][k], 2 * r + c + 1)
                        for a in range(E0 // 2):
                            mm = pe.transpose(ps[2 * k + a // 2][:, (a % 2) * L + c * P:(a % 2) * L + (c + 1) * P],
                                              pick[:, k, c, 2 * a:2 * a + 2, :].rearrange("p e s -> p (e s)"), ident)
                    mm.then_inc(S["pickT_ps"][k], 1)
                    pe.wait_ge(S["yst"][k], r + 1)
                    pe.wait_ge(S["prod"][k], r)
                    for a in range(E0 // 2):
                        mm = pe.transpose(ps[4 + k][:, a * P:(a + 1) * P],
                                          yst[:, k, 2 * a:2 * a + 2, :].rearrange("p e s -> p (e s)"), ident)
                    mm.then_inc(S["y_ps"][k], 1)
                pe.wait_ge(S["gsel"][0], 2 * r + 2)
                pe.wait_ge(S["gate"][0], r)
                pe.matmul(ps[7][:, 0:2 * D], m.ones16[:], gsel[:].rearrange("p s d -> p (s d)"), start=True,
                          stop=True).then_inc(S["gate_ps"][0], 1)
                for k in range(2):
                    pe.wait_ge(S["ysl"][k], r + 1)
                    pe.wait_ge(S["pickT"][k], 2 * r + 2)
                    for c in range(NCH):
                        for a in range(E0 // 2):
                            mm = pe.matmul(ps[4 + k][:, c * D:(c + 1) * D], pickT[:, k, a, c * P:(c + 1) * P],
                                           ysl[:, k, a, :], start=(a == 0), stop=(a == E0 // 2 - 1))
                    mm.then_inc(S["out_ps"][k], 1)

        @block.scalar
        def _(act):
            with act.Fori(0, PAIRS, 1) as r:
                for k in range(2):
                    act.wait_ge(S["out_ps"][k], r)
                    act.wait_ge(S["pickT_ps"][k], r + 1)
                    for a in range(2):
                        act.activation(pickT[:, k, 2 * a:2 * a + 2, :],
                                       ps[2 * k + a][:, :].rearrange("p (a t) -> p a t", a=2),
                                       ACT.Copy).then_inc(S["pickT"][k], 1)
                act.wait_ge(S["gate_ps"][0], r + 1)
                act.wait_ge(S["prod"][1], r)
                act.activation(gate[:], ps[7][:, 0:2 * D].rearrange("p (s d) -> p s d", s=2),
                               ACT.Copy).then_inc(S["gate"][0], 1)


SCAN_J = NST // 2
RING = 4


def scan_phase(nc, d, m, ps):
    with ExitStack() as ctx:
        sem = semaphores(nc, ctx, "s_")

        def sb(n, s, dt=F32):
            return ctx.enter_context(nc.sbuf_tensor("s_" + n, s, dt))

        stats, mv = sb("stats", [P, NCH, 6]), sb("mv", [P, NCH, 2])
        lnv, rstd = sb("lnv", [P, NCH]), sb("rstd", [P, NCH])
        ostats, omv = sb("ostats", [P, NCH, 6]), sb("omv", [P, NCH, 2])
        olnv, orstd = sb("olnv", [P, NCH]), sb("orstd", [P, NCH])
        xn = sb("xn", [P, NCH, D])
        hT = sb("hT", [P, 2, L])
        acc = sb("acc", [P, NH, L])
        u = sb("u", [P, 2, NH, L])
        z = sb("z", [P, 2, NH, L])
        dlow = sb("dlow", [P, L])
        t1 = sb("t1", [P, NH, L])
        soft, e, ebig, cub = (sb(n, [P, NH, L]) for n in ("soft", "e", "ebig", "cub"))
        dt = sb("dt", [P, 2, NH, L])
        dtu = sb("dtu", [P, 2, NH, L])
        bc = sb("bc", [3 * 32, 2, L], BF16)
        r1 = sb("r1", [3 * 32, L])
        mid = sb("mid", [3 * 32, L], BF16)
        spread = sb("spread", [3 * 32, 32, P], BF16)
        aneg = sb("aneg", [P, NH, NST])
        dA = sb("dA", [P, RING, NH, 2, L])
        dbu = sb("dbu", [P, 2, NH, 2, L])
        hs = sb("hs", [P, 2, NH, 2, L])
        hc = sb("hc", [P, 2, NH, 2, L])
        yt, yz = sb("yt", [P, NH, L]), sb("yz", [P, NH, L])
        gsel, gate = sb("gsel", [B, 2, D]), sb("gate", [P, 2, D])
        oh = sb("oh", [P, NCH, D])
        names = ("v_passed p_passed v_pre v_prep v_fin init a_exp "
                 "B_ps C_ps dA_ready dbu_done scanned hc_ready y_part "
                 "e_ready e_bound e_cubic st rs xn xT h xs_ps z_ps conv dlow u_ready z_ready dt_ps t1 abs soft dt_ready dtu_ready "
                 "bc_mid oln bc_ready gsel gate_ps gate "
                 "weights y_read yz out_ps ost ors o_read done").split()
        S = {n: sem(n) for n in names}
        ident = m.const[:, C_ID:C_ID + P]
        bB, bC, bY, bX, bZ, bT = ps[0:2], ps[2:4], ps[4], ps[5], ps[6], ps[7]
        col = lambda h, i: m.bcol[:, h, i:i + 1]
        CONV_B, DT_B, DSKIP, ALOG = 4, 5, 6, 7
        block = ctx.enter_context(nc.Block())

        def sequences(eng, body, last):
            body(0, 0, True, True)
            with eng.Fori(0, PAIRS - 1, 1) as r:
                body(2 * r + 1, 1, False, True)
                body(2 * r + 2, 0, False, True)
            body(B - 1, 1, False, False)
            last(B - 1, 1)

        @block.vector
        def _(dve):
            tick0, settle0, _ = ticker(dve, S["v_pre"])
            tick0(dve.tensor_copy(spread[:], m.const[0:96, C_REP:C_REP + 32].unsqueeze(2).broadcast_to([96, 32, P])))
            tick0(dve.memset(dA[:, :, :, :, 0:1], 0.0))
            dve.wait_ge(S["a_exp"], 1)
            tick0(dve.tensor_scalar(aneg[:], aneg[:], -1.0, None, ALU.mult))
            settle0()
            dve.sem_inc(S["init"], 1)

            def prepare(step, b, k, T):
                tick, settle = T
                if step == 0:
                    for c in range(NCH):
                        tick(dve.bn_stats(stats[:, c, :], m.x_res[:, b * NCH + c, :]))
                    settle(b)
                    pause(dve, S["v_passed"])
                    for c in range(NCH):
                        dve.bn_aggr(mv[:, c, :], stats[:, c, :]).then_inc(S["st"], 1)
                if step == 1:
                    dve.wait_ge(S["rs"], b + 1)
                    dve.wait_ge(S["st"], 2 * b + 2)
                    for c in range(NCH):
                        dve.tensor_scalar(xn[:, c, :], m.x_res[:, b * NCH + c, :], mv[:, c, 0:1], rstd[:, c:c + 1],
                                          ALU.subtract, ALU.mult).then_inc(S["xn"], 1)
                if step == 4:
                    dve.wait_ge(S["xs_ps"], b + 1)
                    for h in range(NH):
                        tick(dve.tensor_scalar(acc[:, h, :], bX[:, h * L:(h + 1) * L], col(h, KCONV - 1),
                                               col(h, CONV_B), ALU.mult, ALU.add))
                    dve.tensor_copy(bc[:, k, :], bT[0:96, 0:L]).then_inc(S["bc_mid"], 1)
                    for s in range(1, KCONV):
                        settle(b)
                        for h in range(NH):
                            ins = dve.scalar_tensor_tensor(acc[:, h, s:], bX[:, h * L:(h + 1) * L - s],
                                                           col(h, KCONV - 1 - s), acc[:, h, s:], ALU.mult, ALU.add)
                            if s < KCONV - 1:
                                tick(ins)
                            else:
                                ins.then_inc(S["conv"], 1)
                        if s == 1:
                            dve.wait_ge(S["bc_mid"], b + 1)
                            tick(dve.tensor_tensor(r1[:], bT[0:96, 0:L], bc[:, k, :], ALU.subtract))
                        if s == 2:
                            tick(dve.tensor_copy(bc[32:64, k, :], r1[32:64, :]))
                            tick(dve.tensor_copy(mid[64:96, :], r1[64:96, :]))
                    dve.tensor_tensor(bc[64:96, k, :], r1[64:96, :], mid[64:96, :], ALU.subtract)\
                        .then_inc(S["bc_ready"], 1)
                if step == 5:
                    dve.wait_ge(S["dt_ps"], b + 1)
                    for h in range(NH):
                        dve.tensor_scalar(t1[:, h, :], bX[:, h * L:(h + 1) * L], col(h, DT_B), None,
                                          ALU.add).then_inc(S["t1"], 1)
                if step == 6:
                    dve.wait_ge(S["e_cubic"], b + 1)
                    tick(dve.tensor_tensor(cub[:], cub[:], e[:], ALU.mult))
                    settle(b)
                    tick(dve.scalar_tensor_tensor(cub[:], cub[:], 1.0, e[:], ALU.add, ALU.mult))
                    settle(b)
                    dve.wait_ge(S["soft"], b + 1)
                    tick(dve.tensor_tensor(cub[:], cub[:], soft[:], ALU.min))
                    settle(b)
                    dve.scalar_tensor_tensor(dt[:, k], t1[:], 0.0, cub[:], ALU.max, ALU.add)\
                        .then_inc(S["dt_ready"], 1)
                    dve.wait_ge(S["dt_ready"], b + 1)
                    dve.wait_ge(S["u_ready"], b + 1)
                    dve.tensor_tensor(dtu[:, k], dt[:, k], u[:, k], ALU.mult).then_inc(S["dtu_ready"], 1)

            def finish(step, b, k, T):
                tick, settle = T
                if step == 0:
                    dve.wait_ge(S["y_part"], 8 * b + 8)
                    for h in range(NH):
                        dve.scalar_tensor_tensor(yt[:, h, :], u[:, k, h, :], col(h, DSKIP), bY[:, h * L:(h + 1) * L],
                                                 ALU.mult, ALU.add).then_inc(S["y_read"], 1)
                    dve.wait_ge(S["y_read"], 2 * b + 2)
                    dve.wait_ge(S["z_ready"], b + 1)
                    dve.tensor_tensor(yz[:], yt[:], z[:, k], ALU.mult).then_inc(S["yz"], 1)
                if step == 2:
                    dve.wait_ge(S["out_ps"], b + 1)
                    for c in range(NCH):
                        tick(dve.bn_stats(ostats[:, c, :], bZ[:, c * D:(c + 1) * D]))
                    settle(b)
                    pause(dve, S["v_passed"])
                    for c in range(NCH):
                        dve.bn_aggr(omv[:, c, :], ostats[:, c, :]).then_inc(S["ost"], 1)
                if step == 3:
                    dve.wait_ge(S["ors"], b + 1)
                    dve.wait_ge(S["ost"], 2 * b + 2)
                    for c in range(NCH):
                        dve.tensor_scalar(oh[:, c, :], bZ[:, c * D:(c + 1) * D], omv[:, c, 0:1], orstd[:, c:c + 1],
                                          ALU.subtract, ALU.mult).then_inc(S["o_read"], 1)
                    dve.wait_ge(S["o_read"], 2 * b + 2)
                    dve.wait_ge(S["gate"], b + 1)
                    tick(dve.tensor_tensor(oh[:], oh[:], gate[:, 0:1, :].broadcast_to([P, NCH, D]), ALU.mult))
                    settle(b)
                    tick(dve.tensor_tensor(oh[:], oh[:], gate[:, 1:2, :].broadcast_to([P, NCH, D]), ALU.add))
                    settle(b)
                    xs = m.x_res[:, bass.ds(b * NCH, NCH), :]
                    dve.tensor_tensor(xs, xs, oh[:], ALU.add).then_inc(S["done"], 1)

            def times_B(b, k, j):
                dve.wait_ge(S["B_ps"], 8 * b + j + 1)
                if j == 0:
                    dve.wait_ge(S["dtu_ready"], b + 1)
                dve.tensor_tensor(dbu[:, j % 2], dtu[:, k].unsqueeze(2).broadcast_to([P, NH, 2, L]),
                                  bB[j % 2][:, :].rearrange("p (n t) -> p n t", n=2).unsqueeze(1).broadcast_to(
                                      [P, NH, 2, L]), ALU.mult).then_inc(S["dbu_done"], 1)

            def recur(b, j):
                flat = lambda a: a.rearrange("p h n t -> p (h n t)")
                dve.wait_ge(S["dbu_done"], 8 * b + j + 1)
                dve.wait_ge(S["dA_ready"], 8 * b + j + 1)
                dve.tensor_tensor_scan(flat(hs[:, j % 2]), flat(dA[:, j % RING]), flat(dbu[:, j % 2]), 0.0,
                                       ALU.mult, ALU.add).then_inc(S["scanned"], 1)

            def times_C(b, j, first):
                dve.wait_ge(S["scanned"], 8 * b + j + 1)
                dve.wait_ge(S["C_ps"], 8 * b + j + 1)
                if not (first and j < 2):
                    dve.wait_ge(S["y_part"], 8 * b + j - 1)
                dve.tensor_tensor(hc[:, j % 2], hs[:, j % 2],
                                  bC[j % 2][:, :].rearrange("p (n t) -> p n t", n=2).unsqueeze(1).broadcast_to(
                                      [P, NH, 2, L]), ALU.mult).then_inc(S["hc_ready"], 1)

            def body(b, k, first, prepares):
                tp, sp_, _ = ticker(dve, S["v_prep"], SCAN_PREP)
                tf, sf, _ = ticker(dve, S["v_fin"], SCAN_FIN)
                for j in range(SCAN_J):
                    recur(b, j)
                    if j + 1 < SCAN_J:
                        times_B(b, k, j + 1)
                    elif prepares:
                        times_B(b + 1, 1 - k, 0)
                    if not first:
                        finish(j, b - 1, 1 - k, (tf, sf))
                    if prepares:
                        prepare(j, b + 1, 1 - k, (tp, sp_))
                    times_C(b, j, first)
                    if j == SCAN_J - 1:
                        if not first:
                            dve.wait_ge(S["gate_ps"], b)
                        dve.tensor_scalar(gsel[:], m.gates[:, 1, :].rearrange("p (a d) -> p a d", a=3)[:, 0:3:2, :],
                                          m.const[0:B, bass.ds(C_ID + b, 1)], None, ALU.mult).then_inc(S["gsel"], 1)

            def last(b, k):
                tf, sf, _ = ticker(dve, S["v_fin"], SCAN_FIN)
                for j in range(SCAN_J):
                    finish(j, b, k, (tf, sf))

            tp, sp_, _ = ticker(dve, S["v_prep"], SCAN_PREP)
            for j in range(SCAN_J):
                prepare(j, 0, 0, (tp, sp_))
            times_B(0, 0, 0)
            sequences(dve, body, last)

        @block.scalar
        def _(act):
            act.activation(aneg[:], m.bcol[:, :, ALOG:], ACT.Exp).then_inc(S["a_exp"], 1)
            act.preload_act_table_set(EXPLN)
            act.wait_ge(S["init"], 1)

            def prepare(step, b, k):
                if step == 0:
                    act.wait_ge(S["st"], 2 * b + 2)
                    act.activation(lnv[:], mv[:, :, 1], ACT.Ln, bias=m.eps[:, 0:1]).then_inc(S["abs"], 1)
                    act.wait_ge(S["abs"], 2 * b + 1)
                    act.activation(rstd[:], lnv[:], ACT.Exp, scale=-0.5).then_inc(S["rs"], 1)
                if step == 2:
                    act.wait_ge(S["xT"], b + 1)
                    act.activation(hT[:, k, :], bT[:, 0:L], ACT.Identity, bias=m.modT[:, 1, 0, bass.ds(b, 1)],
                                   scale=m.modT[:, 1, 1, bass.ds(b, 1)]).then_inc(S["h"], 1)
                if step == 3:
                    act.wait_ge(S["xs_ps"], b + 1)
                    act.activation(dlow[96:96 + RDT, :], bT[96:96 + RDT, 0:L], ACT.Copy).then_inc(S["dlow"], 1)
                if step == 4:
                    act.wait_ge(S["z_ps"], b + 1)
                    act.activation(z[:, k], bZ[:, :].rearrange("p (h t) -> p h t", h=NH), ACT.Silu)\
                       .then_inc(S["z_ready"], 1)
                    act.wait_ge(S["conv"], 2 * b + 2)
                    act.activation(u[:, k], acc[:], ACT.Silu).then_inc(S["u_ready"], 1)
                    act.preload_act_table_set(EXPLN)
                if step == 5:
                    act.wait_ge(S["t1"], 2 * b + 2)
                    act.activation(soft[:], t1[:], ACT.Abs).then_inc(S["abs"], 1)
                    act.wait_ge(S["abs"], 2 * b + 2)
                    act.activation(e[:], soft[:], ACT.Exp, scale=-1.0).then_inc(S["e_ready"], 1)
                    act.wait_ge(S["e_bound"], b + 1)
                    act.activation(soft[:], ebig[:], ACT.Ln, bias=m.eps[:, 2:3]).then_inc(S["soft"], 1)

            def finish(step, b, k):
                if step == 0:
                    act.wait_ge(S["gate_ps"], b + 1)
                    act.activation(gate[:], bT[:, 0:2 * D].rearrange("p (a d) -> p a d", a=2), ACT.Copy)\
                       .then_inc(S["gate"], 1)
                if step == 2:
                    act.wait_ge(S["ost"], 2 * b + 2)
                    act.activation(olnv[:], omv[:, :, 1], ACT.Ln, bias=m.eps[:, 0:1]).then_inc(S["oln"], 1)
                    act.wait_ge(S["oln"], b + 1)
                    act.activation(orstd[:], olnv[:], ACT.Exp, scale=-0.5).then_inc(S["ors"], 1)

            def decays(b, k, j, free):
                if j == 0:
                    act.wait_ge(S["dt_ready"], b + 1)
                if free:
                    act.wait_ge(S["scanned"], 8 * b + j - RING + 1)
                for h in range(NH):
                    for n in range(2):
                        ins = act.activation(dA[:, j % RING, h, n, 1:], dt[:, k, h, 1:], ACT.Exp,
                                             scale=aneg[:, h, 2 * j + n:2 * j + n + 1])
                ins.then_inc(S["dA_ready"], 1)

            def body(b, k, first, prepares):
                for j in range(SCAN_J):
                    if j < RING:
                        decays(b, k, j + RING, True)
                    if not first:
                        finish(j, b - 1, 1 - k)
                    if prepares:
                        prepare(j, b + 1, 1 - k)
                        if j == 6:
                            decays(b + 1, 1 - k, 0, True)
                            decays(b + 1, 1 - k, 1, True)
                        if j == 7:
                            decays(b + 1, 1 - k, 2, True)
                            decays(b + 1, 1 - k, 3, True)

            def last(b, k):
                for j in range(SCAN_J):
                    finish(j, b, k)

            for j in range(SCAN_J):
                prepare(j, 0, 0)
            for j in range(RING):
                decays(0, 0, j, False)
            sequences(act, body, last)

        @block.sync
        def _(sp):
            sp.dma_start(m.w13[:], d["w13"]).then_inc(S["weights"], 16)
            sp.dma_start(m.w2d[:], d["w2d"]).then_inc(S["weights"], 16)
            sp.wait_ge(S["weights"], 32)

        @block.gpsimd
        def _(pool):
            with pool.Fori(0, B, 1) as b:
                pool.wait_ge(S["e_ready"], b + 1)
                pause(pool, S["p_passed"])
                pool.tensor_scalar(ebig[:], e[:], SMALL_E, None, ALU.max).then_inc(S["e_bound"], 1)
                pool.tensor_scalar(cub[:], e[:], 1.0 / 3, -0.5, ALU.mult, ALU.add).then_inc(S["e_cubic"], 1)

        @block.tensor
        def _(pe):
            pe.wait_ge(S["init"], 1)

            def prepare(step, b, k):
                if step == 2:
                    pe.wait_ge(S["xn"], 2 * b + 2)
                    if not (isinstance(b, int) and b == 0):
                        pe.wait_ge(S["gate"], b - 1)
                    for c in range(NCH):
                        mm = pe.transpose(bT[:, c * P:(c + 1) * P], xn[:, c, :], ident)
                    mm.then_inc(S["xT"], 1)
                if step == 3:
                    pe.wait_ge(S["h"], b + 1)
                    for h in range(NH):
                        pe.matmul(bX[:, h * L:(h + 1) * L], m.w_in[:, h * P:(h + 1) * P], hT[:, k, :],
                                  start=True, stop=True)
                    pe.matmul(bT[0:104, 0:L], m.w_in[:, 2 * DI:2 * DI + 104], hT[:, k, :], start=True,
                              stop=True).then_inc(S["xs_ps"], 1)
                if step == 4:
                    if not (isinstance(b, int) and b == 0):
                        pe.wait_ge(S["o_read"], 2 * b - 2)
                    for h in range(NH):
                        mm = pe.matmul(bZ[:, h * L:(h + 1) * L], m.w_in[:, DI + h * P:DI + (h + 1) * P], hT[:, k, :],
                                       start=True, stop=True)
                    mm.then_inc(S["z_ps"], 1)
                if step == 5:
                    pe.wait_ge(S["dlow"], b + 1)
                    pe.wait_ge(S["conv"], 2 * b + 2)
                    for h in range(NH):
                        mm = pe.matmul(bX[:, h * L:(h + 1) * L], m.wdt[96:96 + RDT, h * P:(h + 1) * P],
                                       dlow[96:96 + RDT, :], start=True, stop=True)
                    mm.then_inc(S["dt_ps"], 1)

            def finish(step, b, k):
                if step == 0:
                    pe.wait_ge(S["gsel"], b + 1)
                    pe.matmul(bT[:, 0:2 * D], m.ones16[:], gsel[:].rearrange("p a d -> p (a d)"), start=True,
                              stop=True).then_inc(S["gate_ps"], 1)
                if step == 1:
                    pe.wait_ge(S["yz"], b + 1)
                    for c in range(NCH):
                        o = bZ[:, c * D:(c + 1) * D]
                        for h in range(NH):
                            pe.matmul(o, yz[:, h, c * P:(c + 1) * P], m.w_outT[:, h, :], start=(h == 0), stop=False)
                        mm = pe.matmul(o, hT[:, k, c * P:(c + 1) * P], ident, start=False, stop=True)
                    mm.then_inc(S["out_ps"], 1)

            def rows(bank, b, k, j, first_row, ready):
                for n in range(2):
                    mm = pe.matmul(bank[:, n * L:(n + 1) * L], spread[:, first_row + 2 * j + n, :], bc[:, k, :],
                                   start=True, stop=True)
                mm.then_inc(ready, 1)

            def B_rows(b, k, j, first):
                if j == 0:
                    pe.wait_ge(S["bc_ready"], b + 1)
                if not (first and j < 2):
                    pe.wait_ge(S["dbu_done"], 8 * b + j - 1)
                rows(bB[j % 2], b, k, j, 0, S["B_ps"])

            def C_rows(b, k, j, first):
                if not (first and j < 2):
                    pe.wait_ge(S["hc_ready"], 8 * b + j - 1)
                rows(bC[j % 2], b, k, j, NST, S["C_ps"])

            def sum_states(b, j, first):
                pe.wait_ge(S["hc_ready"], 8 * b + j + 1)
                if j == 0 and not first:
                    pe.wait_ge(S["y_read"], 2 * b)
                for n in range(2):
                    mm = pe.matmul(bY[:, :].rearrange("p (h t) -> p h t", h=NH), ident, hc[:, j % 2, :, n, :],
                                   start=(j == 0 and n == 0), stop=(j == SCAN_J - 1 and n == 1))
                mm.then_inc(S["y_part"], 1)

            def body(b, k, first, prepares):
                for j in range(SCAN_J):
                    if j + 1 < SCAN_J:
                        B_rows(b, k, j + 1, first)
                    elif prepares:
                        B_rows(b + 1, 1 - k, 0, False)
                    C_rows(b, k, j, first)
                    if j > 0:
                        sum_states(b, j - 1, first)
                    elif not first:
                        sum_states(b - 1, SCAN_J - 1, False)
                    if not first:
                        finish(j, b - 1, 1 - k)
                    if prepares:
                        prepare(j, b + 1, 1 - k)

            def last(b, k):
                sum_states(b, SCAN_J - 1, False)
                for j in range(SCAN_J):
                    finish(j, b, k)

            for j in range(SCAN_J):
                prepare(j, 0, 0)
            B_rows(0, 0, 0, True)
            sequences(pe, body, last)


SCAN_PREP, SCAN_FIN = 14, 4
SMALL_E = 2.0 ** -6


MAX_TILES = (B * L * TOPK + E1 * (P - 1)) // P
MOE_TILES = MAX_TILES + MAX_TILES % 2
ASSIGN = TILES * TOPK


def router_phase(nc, d, m, ps):
    with ExitStack() as ctx:
        sem = semaphores(nc, ctx, "r_")

        def sb(n, s, dt=F32):
            return ctx.enter_context(nc.sbuf_tensor("r_" + n, s, dt))

        Q = 2 * NCH
        stats, mv = sb("stats", [P, Q, 6]), sb("mv", [P, Q, 2])
        lnv, rstd = sb("lnv", [P, Q]), sb("rstd", [P, Q])
        xn = sb("xn", [P, Q, D])
        hT = sb("hT", [P, 2, L])
        sq = sb("sq", [P, 2 * L])
        lrms, rrms = sb("lrms", [P, 2 * L]), sb("rrms", [P, 2 * L])
        hf = sb("hf", [P, 2 * L])
        rows = sb("rows", [P, Q, D])
        gsel, gate = sb("gsel", [B, 2, D]), sb("gate", [P, 2, D])
        gh = sb("gh", [P, Q, D])
        mx, sh, ex = sb("mx", [P, Q]), sb("sh", [P, Q, E1]), sb("ex", [P, Q, E1])
        top = sb("top", [P, Q, 8])
        idx = sb("idx", [P, Q, 8], U32)
        den, rden = sb("den", [P, Q]), sb("rden", [P, Q])
        names = ("v_own v_passed a_own st rs xn xT h sq ms_ps rms hf lg_ps sh ex gsel gate_ps gate back_ps rows_ps rows "
                 "stored").split()
        S = {n: sem(n) for n in names}
        ident = m.const[:, C_ID:C_ID + P]
        block = ctx.enter_context(nc.Block())

        @block.vector
        def _(dve):
            with dve.Fori(0, PAIRS, 1) as r:
                tick, settle, ends = ticker(dve, S["v_own"], ROUTER_DVE)
                for q in range(Q):
                    tick(dve.bn_stats(stats[:, q, :], m.x_res[:, r * Q + q, :]))
                settle(r)
                pause(dve, S["v_passed"])
                for q in range(Q):
                    dve.bn_aggr(mv[:, q, :], stats[:, q, :]).then_inc(S["st"], 1)
                for k in range(2):
                    dve.tensor_scalar(gsel[:, k, :], m.gates[:, 1, D:2 * D],
                                      m.const[0:B, bass.ds(C_ID + 2 * r + k, 1)], None,
                                      ALU.mult).then_inc(S["gsel"], 1)
                dve.wait_ge(S["rs"], r + 1)
                dve.wait_ge(S["st"], Q * r + Q)
                for q in range(Q):
                    dve.tensor_scalar(xn[:, q, :], m.x_res[:, r * Q + q, :], mv[:, q, 0:1], rstd[:, q:q + 1],
                                      ALU.subtract, ALU.mult).then_inc(S["xn"], 1)
                dve.wait_ge(S["rms"], r + 1)
                dve.scalar_tensor_tensor(hf[:], hT[:].rearrange("p s t -> p (s t)"), m.gate1[:, E1:E1 + 1], rrms[:],
                                         ALU.mult, ALU.mult).then_inc(S["hf"], 1)
                dve.wait_ge(S["back_ps"], r + 1)
                dve.wait_ge(S["gate"], r + 1)
                for k in range(2):
                    tick(dve.tensor_tensor(gh[:, 2 * k:2 * k + 2, :],
                                           ps[2][:, k * L:(k + 1) * L].rearrange("p (c d) -> p c d", c=NCH),
                                           gate[:, k:k + 1, :].broadcast_to([P, NCH, D]), ALU.mult))
                settle(r)
                xs = m.x_res[:, bass.ds(r * Q, Q), :]
                tick(dve.tensor_tensor(xs, xs, gh[:], ALU.add))
                dve.wait_ge(S["lg_ps"], r + 1)
                lg = ps[4][:, 0:Q * E1].rearrange("p (q e) -> p q e", q=Q)
                tick(dve.tensor_reduce(mx[:], lg, AX, ALU.max))
                settle(r)
                dve.tensor_tensor(sh[:], lg, mx[:].unsqueeze(2).broadcast_to([P, Q, E1]),
                                  ALU.subtract).then_inc(S["sh"], 1)
                dve.wait_ge(S["ex"], r + 1)
                pause(dve, S["v_passed"])
                for q in range(Q):
                    tick(dve.max(top[:, q, :], ex[:, q, :]))
                settle(r)
                pause(dve, S["v_passed"])
                for q in range(Q):
                    tick(dve.max_index(idx[:, q, :], top[:, q, :], ex[:, q, :]))
                tick(dve.tensor_tensor(den[:], top[:, :, 0], top[:, :, 1], ALU.add))
                settle(r)
                tick(dve.tensor_copy(m.expert[:, bass.ds(r * Q, Q), :], idx[:, :, 0:TOPK]))
                tick(dve.reciprocal(rden[:], den[:]))
                settle(r)
                tick(dve.tensor_tensor(m.weight[:, bass.ds(r * Q, Q), :], top[:, :, 0:TOPK],
                                       rden[:].unsqueeze(2).broadcast_to([P, Q, TOPK]), ALU.mult))
                settle(r)
                ends()

        @block.scalar
        def _(act):
            act.preload_act_table_set(EXPLN)
            with act.Fori(0, PAIRS, 1) as r:
                tick, settle, ends = ticker(act, S["a_own"], ROUTER_ACT)
                act.wait_ge(S["st"], Q * r + Q)
                tick(act.activation(lnv[:], mv[:, :, 1], ACT.Ln, bias=m.eps[:, 0:1]))
                settle(r)
                act.activation(rstd[:], lnv[:], ACT.Exp, scale=-0.5).then_inc(S["rs"], 1)
                act.wait_ge(S["gate_ps"], r + 1)
                act.activation(gate[:], ps[3][:, 0:2 * D].rearrange("p (s d) -> p s d", s=2),
                               ACT.Copy).then_inc(S["gate"], 1)
                act.wait_ge(S["xT"], r + 1)
                for k in range(2):
                    act.activation(hT[:, k, :], ps[0][:, k * L:(k + 1) * L], ACT.Identity,
                                   bias=m.modT[:, 1, 2, bass.ds(2 * r + k, 1)],
                                   scale=m.modT[:, 1, 3, bass.ds(2 * r + k, 1)]).then_inc(S["h"], 1)
                act.wait_ge(S["h"], 2 * r + 2)
                act.activation(sq[:], hT[:].rearrange("p s t -> p (s t)"), ACT.Square).then_inc(S["sq"], 1)
                act.wait_ge(S["ms_ps"], r + 1)
                tick(act.activation(lrms[:], ps[1][:, :], ACT.Ln, bias=m.eps[:, 1:2]))
                settle(r)
                act.activation(rrms[:], lrms[:], ACT.Exp, scale=-0.5).then_inc(S["rms"], 1)
                act.wait_ge(S["sh"], r + 1)
                act.activation(ex[:], sh[:], ACT.Exp).then_inc(S["ex"], 1)
                act.wait_ge(S["rows_ps"], r + 1)
                act.wait_ge(S["stored"], 16 * r)
                act.activation(rows[:], ps[5][:, :].rearrange("p (q d) -> p q d", q=Q), ACT.Copy)\
                   .then_inc(S["rows"], 1)
                ends()

        @block.sync
        def _(sp):
            with sp.Fori(0, PAIRS, 1) as r:
                sp.wait_ge(S["rows"], r + 1)
                sp.dma_start(m.hf_rows[bass.ds(r * Q * P, Q * P), :].rearrange("(q p) d -> p q d", p=P),
                             rows[:]).then_inc(S["stored"], 16)
            sp.wait_ge(S["stored"], 16 * PAIRS)

        @block.tensor
        def _(pe):
            with pe.Fori(0, PAIRS, 1) as r:
                pe.wait_ge(S["gsel"], 2 * r + 2)
                pe.matmul(ps[3][:, 0:2 * D], m.ones16[:], gsel[:].rearrange("p s d -> p (s d)"), start=True,
                          stop=True).then_inc(S["gate_ps"], 1)
                pe.wait_ge(S["xn"], Q * r + Q)
                for q in range(Q):
                    mm = pe.transpose(ps[0][:, q * P:(q + 1) * P], xn[:, q, :], ident)
                mm.then_inc(S["xT"], 1)
                pe.wait_ge(S["h"], 2 * r + 2)
                for k in range(2):
                    for c in range(NCH):
                        q = k * NCH + c
                        mm = pe.transpose(ps[2][:, q * D:(q + 1) * D], hT[:, k, c * P:(c + 1) * P], ident)
                mm.then_inc(S["back_ps"], 1)
                pe.wait_ge(S["sq"], r + 1)
                pe.matmul(ps[1][:, :], m.ones128[:], sq[:], start=True, stop=True).then_inc(S["ms_ps"], 1)
                pe.wait_ge(S["hf"], r + 1)
                for q in range(Q):
                    mm = pe.matmul(ps[4][:, q * E1:(q + 1) * E1], hf[:, q * P:(q + 1) * P], m.gate1[:, 0:E1],
                                   start=True, stop=True)
                mm.then_inc(S["lg_ps"], 1)
                for q in range(Q):
                    mm = pe.transpose(ps[5][:, q * P:(q + 1) * P], hf[:, q * P:(q + 1) * P], ident)
                mm.then_inc(S["rows_ps"], 1)


ROUTER_DVE, ROUTER_ACT = 20, 2


def slots_phase(nc, d, m, ps):
    with ExitStack() as ctx:
        sem = semaphores(nc, ctx, "m_")

        def sb(n, s, dt=F32):
            return ctx.enter_context(nc.sbuf_tensor("m_" + n, s, dt))

        NT = TILES * E1
        hot = sb("hot", [P, TOPK, TILES, E1])
        cnt = sb("cnt", [P, TILES, E1])
        before = sb("before", [P, P])
        incl = sb("incl", [P, E1, TILES])
        tot = sb("tot", [P, E1, TILES])
        run = sb("run", [P, E1, TILES])
        more = sb("more", [P, E1, TILES])
        full = sb("full", [P, E1])
        ntile, ctile, base, zeros = (sb(n, [P, E1]) for n in ("ntile", "ctile", "base", "zeros"))
        addr = sb("addr", [P, TILES, E1])
        pick = sb("pick", [P, TOPK, TILES, E1])
        slot = sb("slot", [P, TOPK, TILES])
        slot_i, lo_i, hi_i = (sb(n, [P, TOPK, TILES], U32) for n in ("slot_i", "lo_i", "hi_i"))
        lo, hi = sb("lo", [P, TOPK, TILES]), sb("hi", [P, TOPK, TILES])
        cmp = sb("cmp", [P, MOE_TILES, E1])
        etile = sb("etile", [P, MOE_TILES])
        hot_lo = sb("hot_lo", [P, 4, P])
        hot_hi = sb("hot_hi", [P, 4, MOE_TILES])
        idm, off, fil = (sb(n, [P, MOE_TILES]) for n in ("idm", "off", "fil"))
        tok_i = sb("tok_i", [P, MOE_TILES], U32)
        own, s_cnt, s_ps, s_map = sem("own"), sem("cnt"), sem("ps"), sem("map")
        s_hot = [sem(f"hot{i}") for i in range(4)]
        s_used = [sem(f"used{i}") for i in range(4)]
        block = ctx.enter_context(nc.Block())

        @block.tensor
        def _(pe):
            pe.wait_ge(s_cnt, 1)
            flat = cnt[:].rearrange("p t e -> p (t e)")
            pe.matmul(ps[0][:, 0:NT], before[:], flat, start=True, stop=True)
            pe.matmul(ps[1][:, 0:NT], m.ones128[:], flat, start=True, stop=True).then_inc(s_ps, 1)
            for i in range(4):
                pe.wait_ge(s_hot[i], 1)
                pe.matmul(ps[2][:, 0:MOE_TILES], hot_lo[:, i, :], hot_hi[:, i, :], start=(i == 0),
                          stop=False).then_inc(s_used[i], 1)
            with pe.Fori(1, ASSIGN // 4 - 1, 1) as r:
                for i in range(4):
                    pe.wait_ge(s_hot[i], r + 1)
                    pe.matmul(ps[2][:, 0:MOE_TILES], hot_lo[:, i, :], hot_hi[:, i, :], start=False,
                              stop=False).then_inc(s_used[i], 1)
            for i in range(4):
                pe.wait_ge(s_hot[i], ASSIGN // 4)
                mm = pe.matmul(ps[2][:, 0:MOE_TILES], hot_lo[:, i, :], hot_hi[:, i, :], start=False, stop=(i == 3))
            mm.then_inc(s_map, 1)

        @block.vector
        def _(dve):
            tick, settle, _ = ticker(dve, own)
            iota8 = m.const[:, C_IOTA8:C_IOTA8 + E1]
            for k in range(TOPK):
                tick(dve.tensor_tensor(hot[:, k], m.expert[:, :, k:k + 1].broadcast_to([P, TILES, E1]),
                                       iota8.unsqueeze(1).broadcast_to([P, TILES, E1]), ALU.is_equal))
            tick(dve.tensor_tensor(before[:], m.const[:, C_TRI:C_TRI + P], m.const[:, C_ID:C_ID + P], ALU.subtract))
            tick(dve.memset(zeros[:], 0.0))
            tick(dve.memset(run[:], 1.0))
            settle()
            tick(dve.memset(run[:, :, 0:1], 0.0))
            dve.tensor_tensor(cnt[:], hot[:, 0], hot[:, 1], ALU.add).then_inc(s_cnt, 1)
            dve.wait_ge(s_ps, 1)
            tick(dve.tensor_copy(tot[:], ps[1][:, 0:NT].rearrange("p (t e) -> p e t", e=E1)))
            settle()
            flat = lambda a: a[:].rearrange("p e t -> p (e t)")
            tick(dve.tensor_tensor_scan(flat(incl), flat(run), flat(tot), 0.0, ALU.mult, ALU.add))
            settle()
            tick(dve.tensor_scalar(full[:], incl[:, :, TILES - 1], 1.0, None, ALU.add))
            tick(dve.tensor_tensor(tot[:], incl[:], tot[:], ALU.subtract))
            settle()
            tick(dve.tensor_tensor(more[:], full[:].unsqueeze(2).broadcast_to([P, E1, TILES]),
                                   m.const[:, C_IOTA:C_IOTA + TILES].unsqueeze(1).broadcast_to([P, E1, TILES]),
                                   ALU.is_gt))
            settle()
            tick(dve.tensor_reduce(ntile[:], more[:], AX, ALU.add))
            settle()
            tick(dve.tensor_tensor_scan(ctile[:], ntile[:], zeros[:], 0.0, ALU.add, ALU.add))
            settle()
            tick(dve.tensor_tensor(base[:], ctile[:], ntile[:], ALU.subtract))
            settle()
            tick(dve.tensor_tensor(tot[:], tot[:], base[:].unsqueeze(2).broadcast_to([P, E1, TILES]), ALU.add))
            settle()
            tick(dve.scalar_tensor_tensor(addr[:].rearrange("p t e -> p e t"), tot[:], float(P),
                                          ps[0][:, 0:NT].rearrange("p (t e) -> p e t", e=E1), ALU.mult, ALU.add))
            settle()
            for k in range(TOPK):
                tick(dve.tensor_tensor(pick[:, k], hot[:, k], addr[:], ALU.mult))
            settle()
            tick(dve.tensor_reduce(slot[:], pick[:], AX, ALU.add))
            tick(dve.tensor_tensor(cmp[:], ctile[:].unsqueeze(1).broadcast_to([P, MOE_TILES, E1]),
                                   m.const[:, C_T72:C_T72 + MOE_TILES].unsqueeze(2).broadcast_to([P, MOE_TILES, E1]),
                                   ALU.is_le))
            settle()
            tick(dve.tensor_reduce(etile[:], cmp[:], AX, ALU.add))
            tick(dve.tensor_copy(slot_i[:], slot[:]))
            settle()
            tick(dve.tensor_scalar(m.etile[:], etile[:], float(E1 - 1), None, ALU.min))
            tick(dve.tensor_scalar(lo_i[:], slot_i[:], P - 1, None, ALU.bitwise_and))
            tick(dve.tensor_scalar(hi_i[:], slot_i[:], 7, None, ALU.logical_shift_right))
            settle()
            tick(dve.tensor_copy(lo[:], lo_i[:]))
            tick(dve.tensor_copy(hi[:], hi_i[:]))
            settle()
            lo_f, hi_f = (a[:].rearrange("p k t -> p (k t)") for a in (lo, hi))
            with dve.Fori(0, ASSIGN // 4, 1) as r:
                for i in range(4):
                    a = bass.ds(4 * r + i, 1)
                    dve.wait_ge(s_used[i], r)
                    dve.tensor_scalar(hot_lo[:, i, :], m.const[:, C_I128:C_I128 + P], lo_f[:, a], None,
                                      ALU.is_equal)
                    dve.tensor_scalar(hot_hi[:, i, :], m.const[:, C_T72:C_T72 + MOE_TILES], hi_f[:, a],
                                      m.const[:, bass.ds(C_VAL + 4 * r + i, 1)], ALU.is_equal,
                                      ALU.mult).then_inc(s_hot[i], 1)
            dve.wait_ge(s_map, 1)
            pad = m.const[:, C_PAD:C_PAD + MOE_TILES]
            tick(dve.tensor_scalar(idm[:], ps[2][:, 0:MOE_TILES], -1.0, None, ALU.add))
            settle()
            tick(dve.tensor_scalar(fil[:], idm[:], 0.0, None, ALU.is_ge))
            tick(dve.tensor_tensor(off[:], idm[:], pad, ALU.subtract))
            settle()
            tick(dve.tensor_tensor(off[:], off[:], fil[:], ALU.mult))
            tick(dve.tensor_scalar(idm[:], idm[:], 0.0, None, ALU.max))
            settle()
            tick(dve.tensor_tensor(m.to_row[:], off[:], pad, ALU.add))
            tick(dve.tensor_copy(tok_i[:], idm[:]))
            settle()
            tick(dve.tensor_scalar(m.from_row[:], tok_i[:], 1, None, ALU.logical_shift_right))
            settle()


def moe_phase(nc, d, m, ps):
    with ExitStack() as ctx:
        new = semaphores(nc, ctx, "x_")
        passed = new("passed")

        def sem(n):
            return [new(f"{n}{k}") for k in range(2)]

        def sb(n, s, dt=F32):
            return ctx.enter_context(nc.sbuf_tensor("x_" + n, s, dt))

        xT = sb("xT", [P, 2, P])
        a = sb("a", [P, 2, I1])
        h = sb("h", [P, 2, I1])
        hT = sb("hT", [IC, 2, NIC, P])
        y0, y1 = sb("y0", [P, D]), sb("y1", [P, D])
        y = (y0, y1)
        src0, src1 = sb("src0", [P, 1], U32), sb("src1", [P, 1], U32)
        dst0, dst1 = sb("dst0", [P, 1], U32), sb("dst1", [P, 1], U32)
        xg0, xg1 = sb("xg0", [P, D]), sb("xg1", [P, D])
        src, dst, xg = (src0, src1), (dst0, dst1), (xg0, xg1)
        names = "src rows xT_ps xT ag_ps a h hT_ps hT y_ps y dst sent".split()
        S = {n: sem(n) for n in names}
        ident = m.const[:, C_ID:C_ID + P]
        block = ctx.enter_context(nc.Block())
        R = MOE_TILES // 2

        @block.gpsimd
        def _(pool):
            def fetch(r, k):
                pool.wait_ge(S["xT_ps"][k], r)
                pool.tensor_copy(src[k][:], m.from_row[:, bass.ds(2 * r + k, 1)]).then_inc(S["src"][k], 1)
                pool.wait_ge(S["src"][k], r + 1)
                pause(pool, passed)
                pool.indirect_dma_start(xg[k][:], None, m.hf_rows[:, :],
                                        bass.IndirectOffsetOnAxis(ap=src[k][:, 0:1], axis=0)).then_inc(S["rows"][k], 16)

            def send(r, k):
                pool.wait_ge(S["sent"][k], 16 * r)
                pool.tensor_copy(dst[k][:], m.to_row[:, bass.ds(2 * r + k, 1)]).then_inc(S["dst"][k], 1)
                pool.wait_ge(S["dst"][k], r + 1)
                pool.wait_ge(S["y"][k], r + 1)
                pause(pool, passed)
                pool.indirect_dma_start(m.y_rows[:, :], bass.IndirectOffsetOnAxis(ap=dst[k][:, 0:1], axis=0),
                                        y[k][:], None).then_inc(S["sent"][k], 16)

            fetch(0, 0)
            fetch(0, 1)
            with pool.Fori(0, R - 1, 1) as r:
                for k in range(2):
                    fetch(r + 1, k)
                    send(r, k)
            for k in range(2):
                send(R - 1, k)
            for k in range(2):
                pool.wait_ge(S["sent"][k], 16 * R)

        @block.tensor
        def _(pe):
            def first(r, k):
                pe.wait_ge(S["rows"][k], 16 * (r + 1))
                pe.wait_ge(S["y"][k], r)
                pe.transpose(ps[4 + k][:, 0:P], xg[k][:], ident).then_inc(S["xT_ps"][k], 1)
                expert = pe.value_load(m.etile[0:1, bass.ds(2 * r + k, 1)], min_val=0, max_val=E1 - 1)
                pe.wait_ge(S["xT"][k], r + 1)
                pe.wait_ge(S["h"][k], r)
                for i in range(2):
                    mm = pe.matmul(ps[2 * k + i][:, 0:I1], xT[:, k, :],
                                   m.w13[:, bass.ds(expert * 2 + i, 1), :].rearrange("p e i -> p (e i)"),
                                   start=True, stop=True)
                mm.then_inc(S["ag_ps"][k], 1)
                return expert

            def second(r, k, expert):
                pe.wait_ge(S["h"][k], r + 1)
                pe.wait_ge(S["hT"][k], r)
                for i in range(NIC):
                    mm = pe.transpose(ps[6 + k][0:IC, i * P:(i + 1) * P], h[:, k, i * IC:(i + 1) * IC], ident)
                mm.then_inc(S["hT_ps"][k], 1)

            def third(r, k, expert):
                pe.wait_ge(S["hT"][k], r + 1)
                for i in range(NIC):
                    mm = pe.matmul(ps[4 + k][:, 0:D], hT[:, k, i, :],
                                   m.w2d[:, bass.ds(expert * NIC + i, 1), :].rearrange("p e d -> p (e d)"),
                                   start=(i == 0), stop=(i == NIC - 1))
                mm.then_inc(S["y_ps"][k], 1)

            with pe.Fori(0, R, 1) as r:
                e0 = first(r, 0)
                e1 = first(r, 1)
                second(r, 0, e0)
                second(r, 1, e1)
                third(r, 0, e0)
                third(r, 1, e1)

        @block.scalar
        def _(act):
            with act.Fori(0, R, 1) as r:
                for k in range(2):
                    act.wait_ge(S["xT_ps"][k], r + 1)
                    act.activation(xT[:, k, :], ps[4 + k][:, 0:P], ACT.Copy).then_inc(S["xT"][k], 1)
                for k in range(2):
                    act.wait_ge(S["ag_ps"][k], r + 1)
                    act.wait_ge(S["h"][k], r)
                    act.activation(a[:, k, :], ps[2 * k][:, 0:I1], ACT.Silu).then_inc(S["a"][k], 1)
                for k in range(2):
                    act.wait_ge(S["hT_ps"][k], r + 1)
                    act.wait_ge(S["y_ps"][k], r)
                    act.activation(hT[:, k], ps[6 + k][0:IC, :].rearrange("p (i t) -> p i t", i=NIC),
                                   ACT.Copy).then_inc(S["hT"][k], 1)

        @block.vector
        def _(dve):
            with dve.Fori(0, R, 1) as r:
                for k in range(2):
                    dve.wait_ge(S["a"][k], r + 1)
                    dve.wait_ge(S["hT_ps"][k], r)
                    dve.tensor_tensor(h[:, k, :], a[:, k, :], ps[2 * k + 1][:, 0:I1], ALU.mult).then_inc(S["h"][k], 1)
                for k in range(2):
                    dve.wait_ge(S["y_ps"][k], r + 1)
                    dve.wait_ge(S["sent"][k], 16 * r)
                    dve.tensor_copy(y[k][:], ps[4 + k][:, 0:D]).then_inc(S["y"][k], 1)


def output_phase(nc, d, m, ps):
    with ExitStack() as ctx:
        new = semaphores(nc, ctx, "o_")

        def sem(n):
            return [new(f"{n}{k}") for k in range(2)]

        def sb(n, s, dt=F32):
            return ctx.enter_context(nc.sbuf_tensor("o_" + n, s, dt))

        Q = 2 * NCH
        yr = sb("yr", [P, 2, Q, TOPK, D])
        wy = sb("wy", [P, 2, Q, TOPK, D])
        sm = sb("sm", [P, 2, Q, D])
        o = sb("o", [P, 2, Q, D])
        gsel, gate = sb("gsel", [B, 2, 2, D]), sb("gate", [P, 2, 2, D])
        names = "loaded wy sum gsel gate_ps gate gated o stored".split()
        S = {n: sem(n) for n in names}
        block = ctx.enter_context(nc.Block())

        @block.sync
        def _(sp):
            with sp.Fori(0, PAIRS // 2, 1) as r:
                for k in range(2):
                    sp.wait_ge(S["wy"][k], r)
                    sp.dma_start(yr[:, k].rearrange("p q k d -> p q (k d)"),
                                 m.y_rows[bass.ds((2 * r + k) * Q * P * TOPK, Q * P * TOPK), :].rearrange(
                                     "(q p k) d -> p q (k d)", p=P, k=TOPK)).then_inc(S["loaded"][k], 16)

        @block.scalar
        def _(act):
            with act.Fori(0, PAIRS // 2, 1) as r:
                for k in range(2):
                    act.wait_ge(S["gate_ps"][k], r + 1)
                    act.wait_ge(S["gated"][k], r)
                    act.activation(gate[:, k], ps[k][:, 0:2 * D].rearrange("p (s d) -> p s d", s=2),
                                   ACT.Copy).then_inc(S["gate"][k], 1)
                    act.wait_ge(S["o"][k], r + 1)
                    act.dma_start(m.out[bass.ds((2 * r + k) * 2, 2)].rearrange("b (c t) d -> t (b c) d", t=P),
                                  o[:, k]).then_inc(S["stored"][k], 16)
            for k in range(2):
                act.wait_ge(S["stored"][k], 16 * PAIRS // 2)

        @block.tensor
        def _(pe):
            with pe.Fori(0, PAIRS // 2, 1) as r:
                for k in range(2):
                    pe.wait_ge(S["gsel"][k], 2 * r + 2)
                    pe.wait_ge(S["gate"][k], r)
                    pe.matmul(ps[k][:, 0:2 * D], m.ones16[:], gsel[:, k].rearrange("p s d -> p (s d)"), start=True,
                              stop=True).then_inc(S["gate_ps"][k], 1)

        @block.vector
        def _(dve):
            with dve.Fori(0, PAIRS // 2, 1) as r:
                for k in range(2):
                    dve.wait_ge(S["gate_ps"][k], r)
                    for s in range(2):
                        dve.tensor_scalar(gsel[:, k, s, :], m.gates[:, 1, D:2 * D],
                                          m.const[0:B, bass.ds(C_ID + 4 * r + 2 * k + s, 1)], None,
                                          ALU.mult).then_inc(S["gsel"][k], 1)
                for k in range(2):
                    tiles = bass.ds((2 * r + k) * Q, Q)
                    dve.wait_ge(S["loaded"][k], 16 * (r + 1))
                    dve.tensor_tensor(wy[:, k], yr[:, k],
                                      m.weight[:, tiles, :].unsqueeze(3).broadcast_to([P, Q, TOPK, D]),
                                      ALU.mult).then_inc(S["wy"][k], 1)
                    dve.wait_ge(S["wy"][k], r + 1)
                    dve.tensor_tensor(sm[:, k], wy[:, k, :, 0, :], wy[:, k, :, 1, :], ALU.add)\
                       .then_inc(S["sum"][k], 1)
                    dve.wait_ge(S["sum"][k], r + 1)
                    dve.wait_ge(S["gate"][k], r + 1)
                    dve.tensor_tensor(wy[:, k, :, 0, :].rearrange("p (s c) d -> p s c d", s=2),
                                      sm[:, k].rearrange("p (s c) d -> p s c d", s=2),
                                      gate[:, k].unsqueeze(2).broadcast_to([P, 2, NCH, D]), ALU.mult)\
                       .then_inc(S["gated"][k], 1)
                    dve.wait_ge(S["gated"][k], r + 1)
                    dve.wait_ge(S["stored"][k], 16 * r)
                    dve.tensor_tensor(o[:, k], wy[:, k, :, 0, :], m.x_res[:, tiles, :], ALU.add)\
                       .then_inc(S["o"][k], 1)


LAYER0 = [attention_phase, route_phase, gather_phase, expert_phase, combine_phase]
LAYER1 = [scan_phase, router_phase, slots_phase, moe_phase, output_phase]


def build(nc, d, out, phases=99):
    with ExitStack() as ctx:
        def sb(n, s, dt=F32):
            return ctx.enter_context(nc.sbuf_tensor(n, s, dt))

        m = Mem()
        m.out = out
        m.const = sb("const", [P, C_END])
        m.x_res = sb("x_res", [P, TILES, D])
        m.silu_c = sb("silu_c", [P, 2, B])
        m.modT = sb("modT", [P, 2, 4, B])
        m.gates = sb("gates", [B, 2, 3 * D])
        m.eps = sb("eps", [P, 3])
        m.ones16 = sb("ones16", [B, P])
        m.ones128 = sb("ones128", [P, P])
        m.wq, m.wk, m.wv, m.wo = (sb(n, [P, D])[:] for n in ("wq", "wk", "wv", "wo"))
        m.gate0 = sb("gate0", [P, E0])[:]
        m.gn = sb("gn", [P, 2])[:]
        m.w_in = sb("w_in", [P, 2 * DI + 104])[:]
        m.bcol = sb("bcol", [P, NH, 7 + NST])[:]
        m.gate1 = sb("gate1", [P, E1 + 1])[:]
        m.w_outT = sb("w_outT", [P, NH, D])[:]
        m.wdt = sb("wdt", [P, DI])
        ps = [ctx.enter_context(nc.psum_tensor(f"bank{i}", [P, 512], F32)) for i in range(8)]
        setup_phase(nc, d, m, ps)
        with ExitStack() as layer:
            def sb(n, s, dt=F32):
                return layer.enter_context(nc.sbuf_tensor(n, s, dt))

            m.probs = sb("probs", [P, NCH, B * E0])
            m.places = sb("places", [P, NCH, B * E0])
            m.xn2 = sb("xn2", [P, TILES, D])
            m.xin = sb("xin", [P, E0, B * CAP])
            m.yT = sb("yT", [P, E0, B * CAP])
            for ph in LAYER0[:max(phases - 1, 0)]:
                ph(nc, d, m, ps)
        with ExitStack() as layer:
            def sb(n, s, dt=F32):
                return layer.enter_context(nc.sbuf_tensor(n, s, dt))

            m.w13 = sb("w13", [P, E1 * 2, I1])
            m.w2d = sb("w2d", [IC, E1 * NIC, D])
            m.expert, m.weight = sb("expert", [P, TILES, TOPK]), sb("weight", [P, TILES, TOPK])
            m.etile = sb("etile", [P, MOE_TILES], U32)
            m.from_row, m.to_row = sb("from_row", [P, MOE_TILES], U32), sb("to_row", [P, MOE_TILES], U32)
            m.hf_rows = nc.dram_tensor("hf_rows", (B * L, D), F32).ap()
            m.y_rows = nc.dram_tensor("y_rows", (B * L * TOPK + MOE_TILES * P, D), F32).ap()
            for ph in LAYER1[:max(phases - 6, 0)]:
                ph(nc, d, m, ps)
        if phases < 11:
            s_out = ctx.enter_context(nc.semaphore("stored"))
            with nc.Block() as block:
                @block.sync
                def _(sp):
                    for i in range(4):
                        sp.dma_start(out[4 * i:4 * i + 4].rearrange("b (c t) d -> t (b c) d", t=P),
                                     m.x_res[:, 8 * i:8 * i + 8, :]).then_inc(s_out, 16)
                    sp.wait_ge(s_out, 64)


def lay_out(i):
    f = lambda a: np.ascontiguousarray(np.asarray(a))
    win = f(i["L1_attn_W_in"])
    bc, dt = win[2 * DI:2 * DI + 2 * NST], win[2 * DI + 2 * NST:]
    half = lambda a: f(a).reshape(NH, P, -1).transpose(1, 0, 2)
    return {
        "x": f(i["L0_attn_x"]),
        "const": constants(),
        "cT": f(np.stack([f(i["L0_c"]).T, f(i["L1_c"]).T], 1)),
        "wmod": f(np.stack([f(i["L0_wmod"]), f(i["L1_wmod"])], 1)),
        "lnrow": f(np.broadcast_to(np.stack([f(i["L1_attn_ln_g"]), f(i["L1_attn_ln_b"])])[None], (B, 2, D))),
        "wqT": f(f(i["L0_attn_Wq"]).T), "wkT": f(f(i["L0_attn_Wk"]).T),
        "wvT": f(f(i["L0_attn_Wv"]).T), "woT": f(f(i["L0_attn_Wo"]).T),
        "gate0": f(i["L0_ffn_gate_w"]),
        "gn": f(np.stack([f(i["L0_attn_gn_weight"]), f(i["L0_attn_gn_bias"])], 1)),
        "w1": f(i["L0_ffn_w1"]), "w2": f(i["L0_ffn_w2"]),
        "winT": f(np.concatenate([win[:2 * DI], bc, bc, bc, dt]).T),
        "cols": f(np.concatenate([half(i["L1_attn_conv_w"]), half(i["L1_attn_conv_b"]), half(i["L1_attn_b_dt"]),
                                  half(i["L1_attn_D"]), half(i["L1_attn_A_log"])], 2)),
        "gate1T": f(np.concatenate([f(i["L1_ffn_gate_w"]).T, f(i["L1_ffn_rms_weight"])[:, None]], 1)),
        "woutT": f(f(i["L1_attn_W_out"]).T.reshape(NH, P, D).transpose(1, 0, 2)),
        "wdtT": f(f(i["L1_attn_W_dt"]).T),
        "w13": f(np.stack([f(i["L1_ffn_w1"]).transpose(2, 0, 1), f(i["L1_ffn_w3"]).transpose(2, 0, 1)], 2).reshape(P, E1 * 2, I1)),
        "w2d": f(f(i["L1_ffn_w2"]).transpose(2, 0, 1).reshape(NIC, IC, E1, D).transpose(1, 2, 0, 3).reshape(IC, E1 * NIC, D)),
    }


def kernel(**inputs):
    import concourse.bacc as bacc
    from concourse.bass_utils import run_bass_kernel_spmd

    nc = bacc.Bacc("TRN2", target_bir_lowering=False, num_devices=1)
    arrays = lay_out(inputs)
    d = {n: nc.dram_tensor("in_" + n, a.shape, mybir.dt.from_np(a.dtype), kind="ExternalInput").ap() for n, a in arrays.items()}
    out = nc.dram_tensor("out", (B, L, D), F32, kind="ExternalOutput").ap()
    build(nc, d, out)
    return run_bass_kernel_spmd(nc, [{"in_" + n: a for n, a in arrays.items()}], core_ids=[0]).results[0]["out"]
```

```python
from contextlib import ExitStack

import numpy as np

import concourse.bass as bass
from concourse import mybir

F32 = mybir.dt.float32
BF16 = mybir.dt.bfloat16
U32 = mybir.dt.uint32
ALU = mybir.AluOpType
ACT = mybir.ActivationFunctionType
AX = mybir.AxisListType.X

P = 128
B, L, D = 16, 256, 128
NCH = L // P
PAIRS = B // 2
TILES = B * NCH
HEADS, DH = 8, 16
E0, CAP, H0 = 8, 64, 512
HC0 = H0 // P
DI, NST, KCONV, RDT = 256, 16, 4, 8
NH = DI // P
E1, I1, TOPK = 8, 448, 2
IC, NIC = 112, I1 // 112
LN_EPS, RMS_EPS = 1e-5, 1e-6
EXPLN = "natural_log_exp_and_others"

C_DEC, C_INV, C_INVT, C_TRI, C_BLK, C_AVG, C_ID = 0, 256, 512, 640, 768, 896, 1024
C_PAR, C_IOTA, C_IOTA8, C_REP = 1152, 1154, 1218, 1226
C_T72, C_I128, C_VAL, C_PAD, C_END = 1258, 1330, 1458, 1522, 1594


def constants():
    gam = (1.0 - np.exp(np.linspace(np.log(1 / 32), np.log(1 / 512), HEADS)).astype(np.float32)).astype(np.float64)
    p = np.arange(P)
    g = gam[p // DH]
    t = np.arange(L)
    c = np.zeros((P, C_END), np.float32)
    c[:, C_DEC:C_DEC + L] = g[:, None] ** t
    c[:, C_INV:C_INV + L] = g[:, None] ** -t.astype(np.float64)
    c[:, C_INVT:C_INVT + P] = g[None, :] ** -p[:, None].astype(np.float64)
    c[:, C_TRI:C_TRI + P] = p[:, None] <= p[None, :]
    same = p[:, None] // DH == p[None, :] // DH
    c[:, C_BLK:C_BLK + P] = same
    c[:, C_AVG:C_AVG + P] = same / DH
    c[:, C_ID:C_ID + P] = np.eye(P)
    c[:, C_PAR] = (p // DH) % 2 == 0
    c[:, C_PAR + 1] = (p // DH) % 2 == 1
    c[:, C_IOTA:C_IOTA + CAP] = np.arange(1, CAP + 1)
    c[:, C_IOTA8:C_IOTA8 + E1] = np.arange(E1)
    c[:, C_REP:C_REP + 32] = p[:, None] % 32 == np.arange(32)[None, :]
    tiles = np.arange(72)
    c[:, C_T72:C_T72 + 72] = tiles
    c[:, C_I128:C_I128 + P] = p
    rank, tile = np.divmod(np.arange(B * L * TOPK // P), TILES)
    c[:, C_VAL:C_VAL + 64] = 1 + TOPK * (P * tile[None, :] + p[:, None]) + rank[None, :]
    c[:, C_PAD:C_PAD + 72] = B * L * TOPK + P * tiles[None, :] + p[:, None]
    return c


def ticker(eng, sem, per_round=0):
    n = [0]

    def tick(ins):
        ins.then_inc(sem, 1)
        n[0] += 1

    def settle(rnd=0):
        eng.wait_ge(sem, rnd * per_round + n[0])

    def ends():
        assert n[0] == per_round, (sem, n[0], per_round)

    return tick, settle, ends


def pause(eng, passed):
    eng.sem_inc(passed, 1)


def semaphores(nc, ctx, prefix=""):
    taken = []

    def clear():
        nc.clear_and_free_semaphores(taken)
        nc.all_engine_barrier()

    def sem(n):
        taken.append(nc.alloc_semaphore(name=prefix + n))
        return taken[-1]

    ctx.callback(clear)
    return sem


class Mem:
    pass


def setup_phase(nc, d, m, ps):
    with ExitStack() as ctx:
        sem = semaphores(nc, ctx)

        def sb(n, s, dt=F32):
            return ctx.enter_context(nc.sbuf_tensor(n, s, dt))

        cT = sb("cT", [P, 2, B])
        wmod = sb("wmod", [P, 2, 6 * D])
        lnrow = sb("lnrow", [B, 2, D])
        sgn = sb("sgn", [B, 2, 2 * D])
        mag = sb("mag", [B, 2, 2 * D])
        s_c, s_w, s_x, s_sc, s_mod, s_row = (sem("ld_c"), sem("ld_mod"), sem("ld_x"), sem("silu_c"),
                                             sem("mod_ps"), sem("v_own0"))
        block = ctx.enter_context(nc.Block())
        BIG = [(m.x_res[:, 8 * i:8 * i + 8, :],
                d["x"][4 * i:4 * i + 4].rearrange("b (c t) d -> t (b c) d", t=P)) for i in range(4)]
        SMALL = [(m.wq, d["wqT"]), (m.wk, d["wkT"]), (m.wv, d["wvT"]), (m.wo, d["woT"]), (m.gate0, d["gate0"]),
                 (m.gn, d["gn"]), (m.w_in, d["winT"]), (m.bcol, d["cols"]), (m.gate1, d["gate1T"]),
                 (m.w_outT, d["woutT"]), (m.wdt[96:96 + RDT, :], d["wdtT"])]

        @block.sync
        def _(sp):
            sp.dma_start(cT[:], d["cT"]).then_inc(s_c, 16)
            sp.dma_start(lnrow[:], d["lnrow"]).then_inc(s_c, 16)
            sp.dma_start(wmod[:], d["wmod"]).then_inc(s_w, 16)
            sp.dma_start(m.const[:], d["const"]).then_inc(s_w, 16)
            for dst, src in BIG:
                sp.dma_start(dst, src).then_inc(s_x, 16)
            for dst, src in SMALL:
                sp.dma_start(dst if dst is not m.wdt else dst, src).then_inc(s_x, 16)
            sp.wait_ge(s_x, 16 * (len(BIG) + len(SMALL)))

        @block.scalar
        def _(act):
            act.wait_ge(s_c, 32)
            act.activation(m.silu_c[:], cT[:], ACT.Silu).then_inc(s_sc, 1)

        @block.tensor
        def _(pe):
            pe.wait_ge(s_sc, 1)
            pe.wait_ge(s_w, 32)
            for ly in range(2):
                for k, w in enumerate((0, 1, 3, 4)):
                    pe.matmul(ps[ly][:, k * B:(k + 1) * B], wmod[:, ly, w * D:(w + 1) * D], m.silu_c[:, ly, :],
                              start=True, stop=True)
                for k, w in enumerate((2, 5)):
                    mm = pe.matmul(ps[2 + ly][0:B, k * D:(k + 1) * D], m.silu_c[:, ly, :],
                                   wmod[:, ly, w * D:(w + 1) * D], start=True, stop=True)
            mm.then_inc(s_mod, 1)

        @block.vector
        def _(dve):
            tick, settle, _ = ticker(dve, s_row)
            tick(dve.memset(m.eps[:, 0:1], LN_EPS))
            tick(dve.memset(m.eps[:, 1:2], RMS_EPS))
            tick(dve.memset(m.eps[:, 2:3], 1.0))
            tick(dve.memset(m.ones16[:], 1.0))
            tick(dve.memset(m.ones128[:], 1.0 / D))
            dve.wait_ge(s_mod, 1)
            for ly in range(2):
                for k in range(4):
                    tick(dve.tensor_scalar(m.modT[:, ly, k, :], ps[ly][:, k * B:(k + 1) * B],
                                           float(k % 2), None, ALU.add))
                rows = ps[2 + ly][0:B, 0:2 * D]
                tick(dve.tensor_scalar(sgn[:, ly, :], rows, 0.0, 2.0, ALU.is_ge, ALU.mult))
            settle()
            tick(dve.tensor_scalar(sgn[:], sgn[:], -1.0, None, ALU.add))
            settle()
            for ly in range(2):
                tick(dve.tensor_tensor(mag[:, ly, :], sgn[:, ly, :], ps[2 + ly][0:B, 0:2 * D], ALU.mult))
            settle()
            for ly in range(2):
                tick(dve.scalar_tensor_tensor(m.gates[:, ly, 0:2 * D], mag[:, ly, :], 0.25, sgn[:, ly, :],
                                              ALU.max, ALU.mult))
            settle()
            dve.wait_ge(s_c, 32)
            tick(dve.tensor_tensor(m.gates[:, 1, 2 * D:3 * D], m.gates[:, 1, 0:D], lnrow[:, 1, :], ALU.mult))
            settle()
            tick(dve.tensor_tensor(m.gates[:, 1, 0:D], m.gates[:, 1, 0:D], lnrow[:, 0, :], ALU.mult))
            settle()




def attention_phase(nc, d, m, ps):
    with ExitStack() as ctx:
        sem = semaphores(nc, ctx)

        def sb(n, s, dt=F32):
            return ctx.enter_context(nc.sbuf_tensor(n, s, dt))

        Q = 2 * NCH
        stats, mv = sb("stats", [P, Q, 6]), sb("mv", [P, Q, 2])
        lnv, rstd = sb("lnv", [P, Q]), sb("rstd", [P, Q])
        xn = sb("xn", [P, Q, D])
        hT = sb("hT", [P, 2, L])
        qm = sb("qm", [P, 2, 2, L])
        kd = sb("kd", [P, 2, L])
        kt0 = sb("kt0", [P, 2, D])
        v0 = sb("v0", [P, 2, D])
        vp = sb("vp", [P, 2, Q, D])
        state = sb("state", [P, 2, D])
        prob = sb("prob", [P, 2, 4, 2 * NCH, P])
        gst, gmv = sb("gst", [P, 2, 6]), sb("gmv", [P, 2, 2])
        gin, gm = sb("gin", [P, 2, 2]), sb("gm", [P, 2, 2])
        gvar, glnv, gr = sb("gvar", [P, 2]), sb("glnv", [P, 2]), sb("gr", [P, 2])
        gsc, gbi = sb("gsc", [P, 2]), sb("gbi", [P, 2])
        ynT = sb("ynT", [P, 2, L])
        gsel = sb("gsel", [B, 2, 2 * D])
        gate = sb("gate", [P, 2, 2 * D])
        att = sb("att", [P, Q, D])
        xstats, xmv = sb("xstats", [P, Q, 6]), sb("xmv", [P, Q, 2])
        xlnv, xrstd = sb("xlnv", [P, Q]), sb("xrstd", [P, Q])
        xb = sb("xb", [P, Q, D])
        h2T = sb("h2T", [P, 2, L])
        mx = sb("mx", [P, Q])
        sh = sb("sh", [P, Q, E0])
        ex = sb("ex", [P, Q, E0])
        sm = sb("sm", [P, Q])
        rs = sb("rs", [P, Q])

        names = ("v_head v_tail v_passed a_head a_tail ln_stats ln_rstd xn_ready xn_T h_ready proj_ps qk_ready v_sb "
                 "v_zero state_ps state_sb score_ps score_sb y_ps gn_in gn_ps gn_var gn_rstd gn_aff yn_ready "
                 "out_ps gsel_ready gate_ps gate_sb x_stats x_rstd x_norm x_T h2_ready rt_ps rt_shift rt_exp x_kept").split()
        S = {n: sem("a1_" + n) for n in names}
        ident = m.const[:, C_ID:C_ID + P]
        block = ctx.enter_context(nc.Block())
        bT, bY, bK, bQ, bV = ps[0:5]
        bS = (bT, bK, bQ, bV)
        bR, bG, bO = ps[5:8]
        pairs_of = lambda t: t[:, :].rearrange("p (s t) -> p s t", s=2)

        def rounds(eng, body):
            body(0, None)
            with eng.Fori(0, PAIRS - 1, 1) as r:
                body(r + 1, r)
            body(None, PAIRS - 1)

        @block.vector
        def _(dve):
            dve.memset(vp[:], 0.0).then_inc(S["v_zero"], 1)

            def body(a, b):
                head, settle_head, end_head = ticker(dve, S["v_head"], A1_HEAD)
                tail, settle_tail, end_tail = ticker(dve, S["v_tail"], A1_TAIL)

                def statistics(tick, settle, rnd, st, out):
                    pause(dve, S["v_passed"])
                    for q in range(Q):
                        tick(dve.bn_stats(st[:, q, :], m.x_res[:, rnd * Q + q, :]))
                    settle(rnd)
                    pause(dve, S["v_passed"])
                    for q in range(Q):
                        ins = dve.bn_aggr(out[:, q, :], st[:, q, :])
                        if q < Q - 1:
                            tick(ins)
                    return ins

                def masks(k):
                    tri = m.const[:, C_TRI:C_TRI + P].unsqueeze(1).broadcast_to([P, 4, P])
                    for j in range(4):
                        dve.wait_ge(S["score_ps"], a * 8 + k * 4 + j + 1)
                        dve.tensor_tensor(prob[:, k, j], bS[j][:, :].rearrange("p (a t) -> p a t", a=4), tri,
                                          ALU.mult).then_inc(S["score_sb"], 1)

                if a is not None:
                    statistics(head, settle_head, a, stats, mv).then_inc(S["ln_stats"], 1)
                if b is not None:
                    dve.wait_ge(S["y_ps"], b + 1)
                    pause(dve, S["v_passed"])
                    for k in range(2):
                        tail(dve.bn_stats(gst[:, k, :], bR[:, k * L:(k + 1) * L]))
                    settle_tail(b)
                    pause(dve, S["v_passed"])
                    for k in range(2):
                        tail(dve.bn_aggr(gmv[:, k, :], gst[:, k, :]))
                    settle_tail(b)
                    tail(dve.tensor_tensor(gin[:, :, 1], gmv[:, :, 0], gmv[:, :, 0], ALU.mult))
                    tail(dve.tensor_copy(gin[:, :, 0], gmv[:, :, 0]))
                    settle_tail(b)
                    dve.tensor_tensor(gin[:, :, 1], gin[:, :, 1], gmv[:, :, 1], ALU.add).then_inc(S["gn_in"], 1)
                if a is not None:
                    dve.wait_ge(S["ln_rstd"], a + 1)
                    dve.wait_ge(S["ln_stats"], a + 1)
                    for q in range(Q):
                        dve.tensor_scalar(xn[:, q, :], m.x_res[:, a * Q + q, :], mv[:, q, 0:1], rstd[:, q:q + 1],
                                          ALU.subtract, ALU.mult).then_inc(S["xn_ready"], 1)
                if b is not None:
                    for k in range(2):
                        dve.tensor_scalar(gsel[:, k, :], m.gates[:, 0, 0:2 * D],
                                          m.const[0:B, bass.ds(C_ID + 2 * b + k, 1)], None,
                                          ALU.mult).then_inc(S["gsel_ready"], 1)
                    dve.wait_ge(S["gn_ps"], b + 1)
                    tail(dve.tensor_copy(gm[:], bO[:, 0:4].rearrange("p (s k) -> p s k", s=2)))
                    settle_tail(b)
                    tail(dve.tensor_tensor(gvar[:], gm[:, :, 0], gm[:, :, 0], ALU.mult))
                    settle_tail(b)
                    tail(dve.tensor_tensor(gvar[:], gm[:, :, 1], gvar[:], ALU.subtract))
                    settle_tail(b)
                    dve.tensor_scalar(gvar[:], gvar[:], 0.0, None, ALU.max).then_inc(S["gn_var"], 1)
                    dve.wait_ge(S["gn_rstd"], b + 1)
                    tail(dve.tensor_scalar(gsc[:], gr[:], m.gn[:, 0:1], None, ALU.mult))
                    settle_tail(b)
                    tail(dve.tensor_tensor(gbi[:], gm[:, :, 0], gsc[:], ALU.mult))
                    settle_tail(b)
                    dve.tensor_scalar(gbi[:], gbi[:], -1.0, m.gn[:, 1:2], ALU.mult, ALU.add).then_inc(S["gn_aff"], 1)
                if a is not None:
                    dve.wait_ge(S["proj_ps"], a + 1)
                    dec = m.const[:, C_DEC:C_DEC + L].unsqueeze(1).broadcast_to([P, 2, L])
                    inv = m.const[:, C_INV:C_INV + L].unsqueeze(1).broadcast_to([P, 2, L])
                    invt = m.const[:, C_INVT:C_INVT + D].unsqueeze(1).broadcast_to([P, 2, D])
                    dve.tensor_tensor(kt0[:], bY[:, 0:2 * D].rearrange("p (s d) -> p s d", s=2), invt,
                                      ALU.mult).then_inc(S["qk_ready"], 1)
                    dve.tensor_tensor(kd[:], pairs_of(bK), inv, ALU.mult).then_inc(S["qk_ready"], 1)
                    for k in range(2):
                        dve.scalar_tensor_tensor(qm[:, k], pairs_of(bQ), m.const[:, C_PAR + k:C_PAR + k + 1], dec,
                                                 ALU.mult, ALU.mult).then_inc(S["qk_ready"], 1)
                if b is not None:
                    dve.wait_ge(S["out_ps"], b + 1)
                    dve.wait_ge(S["gate_sb"], b + 1)
                    for k in range(2):
                        tail(dve.tensor_tensor(att[:, 2 * k:2 * k + 2, :],
                                               bO[:, k * L:(k + 1) * L].rearrange("p (c d) -> p c d", c=2),
                                               gate[:, k, 0:D].unsqueeze(1).broadcast_to([P, NCH, D]), ALU.mult))
                    settle_tail(b)
                    tail(dve.tensor_tensor(m.x_res[:, bass.ds(b * Q, Q), :], att[:], m.x_res[:, bass.ds(b * Q, Q), :],
                                           ALU.add))
                    settle_tail(b)
                    statistics(tail, settle_tail, b, xstats, xmv).then_inc(S["x_stats"], 1)
                if a is not None:
                    dve.wait_ge(S["state_ps"], a + 1)
                    blk = m.const[:, C_BLK:C_BLK + D].unsqueeze(1).broadcast_to([P, 2, D])
                    dve.tensor_tensor(state[:], bY[:, 2 * D:4 * D].rearrange("p (s d) -> p s d", s=2), blk,
                                      ALU.mult).then_inc(S["state_sb"], 1)
                    masks(0)
                if b is not None:
                    dve.wait_ge(S["x_rstd"], b + 1)
                    dve.wait_ge(S["x_stats"], b + 1)
                    for q in range(Q):
                        dve.tensor_scalar(xb[:, q, :], m.x_res[:, b * Q + q, :], xmv[:, q, 0:1],
                                          xrstd[:, q:q + 1], ALU.subtract, ALU.mult).then_inc(S["x_norm"], 1)
                if a is not None:
                    masks(1)
                if b is not None:
                    dve.wait_ge(S["rt_ps"], b + 1)
                    lg = bG[:, 0:Q * E0].rearrange("p (q e) -> p q e", q=Q)
                    tail(dve.tensor_reduce(mx[:], lg, AX, ALU.max))
                    settle_tail(b)
                    dve.tensor_tensor(sh[:], lg, mx[:].unsqueeze(2).broadcast_to([P, Q, E0]),
                                      ALU.subtract).then_inc(S["rt_shift"], 1)
                    dve.wait_ge(S["rt_exp"], b + 1)
                    tail(dve.tensor_reduce(sm[:], ex[:], AX, ALU.add))
                    settle_tail(b)
                    tail(dve.reciprocal(rs[:], sm[:]))
                    settle_tail(b)
                    for q in range(Q):
                        tail(dve.tensor_scalar(m.probs[:, q % NCH, bass.ds(b * 2 * E0 + (q // NCH) * E0, E0)],
                                               ex[:, q, :], rs[:, q:q + 1], None, ALU.mult))
                    settle_tail(b)
                    dve.wait_ge(S["x_kept"], b + 1)
                    end_tail()
                if a is not None:
                    end_head()

            rounds(dve, body)

        @block.gpsimd
        def _(pool):
            def body(a, b):
                if b is not None:
                    pool.wait_ge(S["x_norm"], (b + 1) * Q)
                    pool.tensor_copy(m.xn2[:, bass.ds(b * Q, Q), :], xb[:]).then_inc(S["x_kept"], 1)

            rounds(pool, body)
            pool.wait_ge(S["x_kept"], PAIRS)

        @block.scalar
        def _(act):
            act.preload_act_table_set(EXPLN)
            act.wait_ge(S["v_zero"], 1)

            def body(a, b):
                head, settle_head, _ = ticker(act, S["a_head"], 1)
                tail, settle_tail, end_tail = ticker(act, S["a_tail"], 2)

                def rsqrt(tick, settle, rnd, out, tmp, var):
                    tick(act.activation(tmp, var, ACT.Ln, bias=m.eps[:, 0:1]))
                    settle(rnd)
                    return act.activation(out, tmp, ACT.Exp, scale=-0.5)

                if a is not None:
                    act.wait_ge(S["ln_stats"], a + 1)
                    rsqrt(head, settle_head, a, rstd[:], lnv[:], mv[:, :, 1]).then_inc(S["ln_rstd"], 1)
                if b is not None:
                    act.wait_ge(S["gate_ps"], b + 1)
                    act.activation(gate[:], bG[:, :].rearrange("p (s d) -> p s d", s=2),
                                   ACT.Copy).then_inc(S["gate_sb"], 1)
                if a is not None:
                    act.wait_ge(S["xn_T"], a + 1)
                    for k in range(2):
                        act.activation(hT[:, k, :], bT[:, k * L:(k + 1) * L], ACT.Identity,
                                       bias=m.modT[:, 0, 0, bass.ds(2 * a + k, 1)],
                                       scale=m.modT[:, 0, 1, bass.ds(2 * a + k, 1)]).then_inc(S["h_ready"], 1)
                if b is not None:
                    act.wait_ge(S["gn_var"], b + 1)
                    rsqrt(tail, settle_tail, b, gr[:], glnv[:], gvar[:]).then_inc(S["gn_rstd"], 1)
                    act.wait_ge(S["gn_aff"], b + 1)
                    for k in range(2):
                        act.activation(ynT[:, k, :], bR[:, k * L:(k + 1) * L], ACT.Identity, bias=gbi[:, k:k + 1],
                                       scale=gsc[:, k:k + 1]).then_inc(S["yn_ready"], 1)
                if a is not None:
                    act.wait_ge(S["proj_ps"], a + 1)
                    act.activation(v0[:], bV[:, :].rearrange("p (s c d) -> p s c d", s=2, c=NCH)[:, :, 0, :],
                                   ACT.Copy).then_inc(S["v_sb"], 1)
                    heads = lambda t: t.rearrange("p (g a d) -> p g a d", a=2, d=DH)
                    for k in range(2):
                        act.activation(heads(vp[:, k].rearrange("p q d -> p (q d)"))[:, :, k, :],
                                       heads(bV[:, :])[:, :, k, :], ACT.Copy).then_inc(S["v_sb"], 1)
                if b is not None:
                    act.wait_ge(S["x_stats"], b + 1)
                    rsqrt(tail, settle_tail, b, xrstd[:], xlnv[:], xmv[:, :, 1]).then_inc(S["x_rstd"], 1)
                    act.wait_ge(S["x_T"], b + 1)
                    for k in range(2):
                        act.activation(h2T[:, k, :], bG[:, k * L:(k + 1) * L], ACT.Identity,
                                       bias=m.modT[:, 0, 2, bass.ds(2 * b + k, 1)],
                                       scale=m.modT[:, 0, 3, bass.ds(2 * b + k, 1)]).then_inc(S["h2_ready"], 1)
                    act.wait_ge(S["rt_shift"], b + 1)
                    act.activation(ex[:], sh[:], ACT.Exp).then_inc(S["rt_exp"], 1)
                    end_tail()

            rounds(act, body)

        @block.tensor
        def _(pe):
            flat = lambda t: t.rearrange("p s t -> p (s t)")

            def body(a, b):
                def scores(k):
                    for j in range(4):
                        if k == 1:
                            pe.wait_ge(S["score_sb"], a * 8 + j + 1)
                        for c in range(NCH):
                            rows = slice(32 * j, 32 * j + 32)
                            mm = pe.matmul(bS[j][:, c * 2 * P:(c + 1) * 2 * P].rearrange("p (a t) -> p a t", a=2),
                                           kd[rows, k, c * P:(c + 1) * P], qm[rows, :, k, c * P:(c + 1) * P],
                                           start=True, stop=True)
                        mm.then_inc(S["score_ps"], 1)

                if a is not None:
                    pe.wait_ge(S["xn_ready"], (a + 1) * Q)
                    for q in range(Q):
                        mm = pe.transpose(bT[:, q * P:(q + 1) * P], xn[:, q, :], ident)
                    mm.then_inc(S["xn_T"], 1)
                if b is not None:
                    pe.wait_ge(S["gn_in"], b + 1)
                    pe.matmul(bO[:, 0:4], m.const[:, C_AVG:C_AVG + P], gin[:].rearrange("p s k -> p (s k)"),
                              start=True, stop=True).then_inc(S["gn_ps"], 1)
                    pe.wait_ge(S["gsel_ready"], (b + 1) * 2)
                    pe.matmul(bG[:, :], m.ones16[:], gsel[:].rearrange("p s d -> p (s d)"), start=True,
                              stop=True).then_inc(S["gate_ps"], 1)
                if a is not None:
                    pe.wait_ge(S["h_ready"], (a + 1) * 2)
                    for k in range(2):
                        pe.matmul(bY[:, k * D:(k + 1) * D], hT[:, k, 0:P], m.wk, start=True, stop=True)
                    hf = flat(hT[:])
                    pe.matmul(bK[:, :], m.wk, hf, start=True, stop=True)
                    pe.matmul(bQ[:, :], m.wq, hf, start=True, stop=True)
                    for q in range(Q):
                        mm = pe.matmul(bV[:, q * D:(q + 1) * D], hf[:, q * P:(q + 1) * P], m.wv, start=True, stop=True)
                    mm.then_inc(S["proj_ps"], 1)
                if b is not None:
                    pe.wait_ge(S["yn_ready"], (b + 1) * 2)
                    yf = flat(ynT[:])
                    for q in range(Q):
                        mm = pe.matmul(bO[:, q * D:(q + 1) * D], yf[:, q * P:(q + 1) * P], m.wo, start=True, stop=True)
                    mm.then_inc(S["out_ps"], 1)
                if a is not None:
                    pe.wait_ge(S["v_sb"], 3 * a + 3)
                    pe.wait_ge(S["qk_ready"], a * 4 + 1)
                    for k in range(2):
                        mm = pe.matmul(bY[:, (2 + k) * D:(3 + k) * D], kt0[:, k, :], v0[:, k, :],
                                       start=True, stop=True)
                    mm.then_inc(S["state_ps"], 1)
                    pe.wait_ge(S["qk_ready"], (a + 1) * 4)
                    scores(0)
                if b is not None:
                    pe.wait_ge(S["x_norm"], (b + 1) * Q)
                    pe.wait_ge(S["gate_sb"], b + 1)
                    for q in range(Q):
                        mm = pe.transpose(bG[:, q * P:(q + 1) * P], xb[:, q, :], ident)
                    mm.then_inc(S["x_T"], 1)
                if a is not None:
                    scores(1)
                if b is not None:
                    pe.wait_ge(S["h2_ready"], (b + 1) * 2)
                    hf = flat(h2T[:])
                    for q in range(Q):
                        mm = pe.matmul(bG[:, q * E0:(q + 1) * E0], hf[:, q * P:(q + 1) * P], m.gate0, start=True,
                                       stop=True)
                    mm.then_inc(S["rt_ps"], 1)
                if a is not None:
                    pe.wait_ge(S["state_sb"], a + 1)
                    for k in range(2):
                        pe.wait_ge(S["score_sb"], a * 8 + 4 * k + 4)
                        for par in range(2):
                            pe.matmul(bR[:, k * L + P:(k + 1) * L], state[:, k, :], qm[:, par, k, P:L],
                                      start=(par == 0), stop=False, skip_group_check=True)
                        for c in (1, 0):
                            for j in range(4):
                                for par in range(2):
                                    mm = pe.matmul(bR[32 * j:32 * j + 32, k * L + c * P:k * L + (c + 1) * P],
                                                   vp[:, par, k * NCH + c, 32 * j:32 * j + 32],
                                                   prob[:, k, j, 2 * c + par, :], start=(c == 0 and par == 0),
                                                   stop=(par == 1), skip_group_check=True)
                    mm.then_inc(S["y_ps"], 1)

            rounds(pe, body)


A1_HEAD, A1_TAIL = 7, 28


def route_phase(nc, d, m, ps):
    with ExitStack() as ctx:
        sem = semaphores(nc, ctx)

        def sb(n, s, dt=F32):
            return ctx.enter_context(nc.sbuf_tensor(n, s, dt))

        left = sb("left", [P, L])
        top8 = sb("top8", [P, 8])
        zeros = sb("zeros", [P, L])
        taken = sb("taken", [P, L])
        place = sb("place", [P, L])
        listed = sb("listed", [P, L])
        s_in, s_own, s_out, s_back = sem("rt_in"), sem("rt_own"), sem("rt_out"), sem("rt_back")
        ident = m.const[:, C_ID:C_ID + P]
        block = ctx.enter_context(nc.Block())

        @block.tensor
        def _(pe):
            for c in range(NCH):
                mm = pe.transpose(ps[0][:, c * P:(c + 1) * P], m.probs[:, c, :], ident)
            mm.then_inc(s_in, 1)
            pe.wait_ge(s_out, 1)
            for c in range(NCH):
                mm = pe.transpose(ps[1][:, c * P:(c + 1) * P], listed[:, c * P:(c + 1) * P], ident)
            mm.then_inc(s_back, 1)

        @block.vector
        def _(dve):
            tick, settle, _ = ticker(dve, s_own)
            tick(dve.memset(zeros[:], 0.0))
            dve.wait_ge(s_in, 1)
            tick(dve.tensor_copy(left[:], ps[0][:, 0:L]))
            settle()
            for _ in range(CAP // 8):
                tick(dve.max(top8[:], left[:]))
                settle()
                tick(dve.match_replace(left[:], top8[:], left[:], -1.0))
                settle()
            tick(dve.tensor_scalar(taken[:], left[:], 0.0, None, ALU.is_lt))
            settle()
            tick(dve.tensor_tensor_scan(place[:], taken[:], zeros[:], 0.0, ALU.add, ALU.add))
            settle()
            dve.tensor_tensor(listed[:], place[:], taken[:], ALU.mult).then_inc(s_out, 1)
            dve.wait_ge(s_back, 1)
            tick(dve.tensor_copy(m.places[:], ps[1][:, 0:L].rearrange("p (c n) -> p c n", c=NCH)))
            settle()


def one_hot(dve, out, places, iota, c, first):
    return dve.tensor_tensor(out, places[:, c, bass.ds(first, E0)].unsqueeze(2).broadcast_to([P, E0, CAP]),
                             iota.unsqueeze(1).broadcast_to([P, E0, CAP]), ALU.is_equal)


def gather_phase(nc, d, m, ps):
    with ExitStack() as ctx:
        new = semaphores(nc, ctx, "")

        def sem(n):
            return [new(f"{n}{k}") for k in range(2)]

        def sb(n, s, dt=F32):
            return ctx.enter_context(nc.sbuf_tensor(n, s, dt))

        pick = sb("pick", [P, 2, NCH, E0, CAP])
        xst = sb("xst", [P, 2, NCH, D])
        picked, staged, product, taken = sem("g_picked"), sem("g_staged"), sem("g_product"), sem("g_taken")
        iota = m.const[:, C_IOTA:C_IOTA + CAP]
        block = ctx.enter_context(nc.Block())

        @block.vector
        def _(dve):
            with dve.Fori(0, PAIRS, 1) as r:
                for k in range(2):
                    dve.wait_ge(product[k], r)
                    for c in range(NCH):
                        one_hot(dve, pick[:, k, c], m.places, iota, c, r * 2 * E0 + k * E0).then_inc(picked[k], 1)

        @block.gpsimd
        def _(pool):
            with pool.Fori(0, PAIRS, 1) as r:
                for k in range(2):
                    pool.wait_ge(product[k], r)
                    pool.tensor_copy(xst[:, k], m.xn2[:, bass.ds(r * 2 * NCH + k * NCH, NCH), :]).then_inc(staged[k], 1)

        @block.tensor
        def _(pe):
            with pe.Fori(0, PAIRS, 1) as r:
                for k in range(2):
                    pe.wait_ge(staged[k], r + 1)
                    pe.wait_ge(taken[k], r)
                    for c in range(NCH):
                        pe.wait_ge(picked[k], 2 * r + c + 1)
                        mm = pe.matmul(ps[k][:, :], xst[:, k, c, :], pick[:, k, c].rearrange("p e s -> p (e s)"),
                                       start=(c == 0), stop=(c == NCH - 1))
                    mm.then_inc(product[k], 1)

        @block.scalar
        def _(act):
            with act.Fori(0, PAIRS, 1) as r:
                for k in range(2):
                    act.wait_ge(product[k], r + 1)
                    seq = bass.ds(2 * r + k, 1)
                    act.activation(m.xin[:, :, bass.ds(2 * r * CAP + k * CAP, CAP)],
                                   ps[k][:, :].rearrange("p (e s) -> p e s", e=E0), ACT.Identity,
                                   bias=m.modT[:, 0, 2, seq], scale=m.modT[:, 0, 3, seq]).then_inc(taken[k], 1)


def expert_phase(nc, d, m, ps):
    N = B * CAP // 2
    with ExitStack() as ctx:
        sem = semaphores(nc, ctx)

        def sb(n, s, dt=F32):
            return ctx.enter_context(nc.sbuf_tensor(n, s, dt))

        w1 = sb("w1", [P, 2, H0])
        w2 = sb("w2", [P, 2, HC0, D])
        g = sb("g", [P, 2, HC0, N])
        loaded = [sem(f"e_loaded{k}") for k in range(2)]
        hidden = [sem(f"e_hidden{h}") for h in range(HC0)]
        gelued = [sem(f"e_gelued{h}") for h in range(HC0)]
        result = [[sem(f"e_result{k}{a}") for a in range(2)] for k in range(2)]
        kept = [sem(f"e_kept{a}") for a in range(2)]
        block = ctx.enter_context(nc.Block())

        @block.sync
        def _(sp):
            with sp.Fori(0, E0 // 2, 1) as r:
                for k in range(2):
                    sp.wait_ge(result[k][1], r)
                    sp.dma_start(w1[:, k, :], d["w1"][bass.ds(2 * r + k, 1), :, :].rearrange(
                        "e p h -> (e p) h")).then_inc(loaded[k], 16)
                    sp.dma_start(w2[:, k], d["w2"][bass.ds(2 * r + k, 1), :, :].rearrange(
                        "e (h p) c -> p (e h) c", p=P)).then_inc(loaded[k], 16)

        @block.tensor
        def _(pe):
            with pe.Fori(0, E0 // 2, 1) as r:
                for k in range(2):
                    pe.wait_ge(loaded[k], 32 * (r + 1))
                    for a in range(2):
                        for h in range(HC0):
                            pe.wait_ge(gelued[h], 4 * r + 2 * k + a)
                            pe.matmul(ps[h][:, :], w1[:, k, h * P:(h + 1) * P],
                                      m.xin[:, 2 * r + k, a * N:(a + 1) * N], start=True,
                                      stop=True).then_inc(hidden[h], 1)
                    for a in range(2):
                        pe.wait_ge(kept[a], 2 * r + k)
                        for h in range(HC0):
                            pe.wait_ge(gelued[h], 4 * r + 2 * k + a + 1)
                            mm = pe.matmul(ps[4 + a][:, :], w2[:, k, h, :], g[:, a, h, :], start=(h == 0),
                                           stop=(h == HC0 - 1))
                        mm.then_inc(result[k][a], 1)

        @block.scalar
        def _(act):
            with act.Fori(0, E0 // 2, 1) as r:
                for k in range(2):
                    for a in range(2):
                        act.wait_ge(result[1 - k][a], r + k)
                        for h in range(HC0):
                            act.wait_ge(hidden[h], 4 * r + 2 * k + a + 1)
                            act.activation(g[:, a, h, :], ps[h][:, :], ACT.Gelu).then_inc(gelued[h], 1)

        @block.vector
        def _(dve):
            with dve.Fori(0, E0 // 2, 1) as r:
                for k in range(2):
                    for a in range(2):
                        dve.wait_ge(result[k][a], r + 1)
                        dve.tensor_copy(m.yT[:, 2 * r + k, a * N:(a + 1) * N], ps[4 + a][:, :]).then_inc(kept[a], 1)


def combine_phase(nc, d, m, ps):
    with ExitStack() as ctx:
        sem = semaphores(nc, ctx)

        def sb(n, s, dt=F32):
            return ctx.enter_context(nc.sbuf_tensor(n, s, dt))

        hot = sb("hot", [P, 2, NCH, E0, CAP])
        pick = sb("pickw", [P, 2, NCH, E0, CAP])
        pickT = sb("pickT", [P, 2, E0 // 2, L])
        yst = sb("yst", [P, 2, E0, CAP])
        ysl = sb("ysl", [P, 2, E0 // 2, D])
        gsel = sb("gsel2", [B, 2, D])
        gate = sb("gate2", [P, 2, D])
        out = sb("moe0", [P, 2, NCH, D])
        names = "hot pick yst pickT_ps pickT y_ps ysl gsel gate_ps gate out_ps prod sum".split()
        S = {n: [sem(f"c_{n}{k}") for k in range(2)] for n in names}
        ident = m.const[:, C_ID:C_ID + P]
        iota = m.const[:, C_IOTA:C_IOTA + CAP]
        block = ctx.enter_context(nc.Block())

        @block.gpsimd
        def _(pool):
            with pool.Fori(0, PAIRS, 1) as r:
                for k in range(2):
                    pool.wait_ge(S["y_ps"][k], r)
                    pool.tensor_copy(yst[:, k], m.yT[:, :, bass.ds(2 * r * CAP + k * CAP, CAP)]).then_inc(S["yst"][k], 1)

        @block.vector
        def _(dve):
            with dve.Fori(0, PAIRS, 1) as r:
                for k in range(2):
                    dve.wait_ge(S["pickT_ps"][k], r)
                    for c in range(NCH):
                        one_hot(dve, hot[:, k, c], m.places, iota, c, r * 2 * E0 + k * E0).then_inc(S["hot"][k], 1)
                    for c in range(NCH):
                        dve.wait_ge(S["hot"][k], 2 * r + c + 1)
                        dve.tensor_tensor(pick[:, k, c], hot[:, k, c],
                                          m.probs[:, c, bass.ds(r * 2 * E0 + k * E0, E0)].unsqueeze(2).broadcast_to(
                                              [P, E0, CAP]), ALU.mult).then_inc(S["pick"][k], 1)
                    if k == 0:
                        dve.wait_ge(S["gate_ps"][0], r)
                        for s in range(2):
                            dve.tensor_scalar(gsel[:, s, :], m.gates[:, 0, D:2 * D],
                                              m.const[0:B, bass.ds(C_ID + 2 * r + s, 1)], None,
                                              ALU.mult).then_inc(S["gsel"][0], 1)
                for k in range(2):
                    dve.wait_ge(S["y_ps"][k], r + 1)
                    dve.tensor_copy(ysl[:, k], ps[4 + k][:, :].rearrange("p (a d) -> p a d", d=D)).then_inc(S["ysl"][k], 1)
                dve.wait_ge(S["gate"][0], r + 1)
                for k in range(2):
                    dve.wait_ge(S["out_ps"][k], r + 1)
                    dve.tensor_tensor(out[:, k], ps[4 + k][:, 0:L].rearrange("p (c d) -> p c d", c=NCH),
                                      gate[:, k, :].unsqueeze(1).broadcast_to([P, NCH, D]),
                                      ALU.mult).then_inc(S["prod"][k], 1)
                    dve.wait_ge(S["prod"][k], r + 1)
                    xs = m.x_res[:, bass.ds(r * 2 * NCH + k * NCH, NCH), :]
                    dve.tensor_tensor(xs, out[:, k], xs, ALU.add).then_inc(S["sum"][k], 1)

        @block.tensor
        def _(pe):
            with pe.Fori(0, PAIRS, 1) as r:
                for k in range(2):
                    pe.wait_ge(S["pickT"][k], 2 * r)
                    for c in range(NCH):
                        pe.wait_ge(S["pick"][k], 2 * r + c + 1)
                        for a in range(E0 // 2):
                            mm = pe.transpose(ps[2 * k + a // 2][:, (a % 2) * L + c * P:(a % 2) * L + (c + 1) * P],
                                              pick[:, k, c, 2 * a:2 * a + 2, :].rearrange("p e s -> p (e s)"), ident)
                    mm.then_inc(S["pickT_ps"][k], 1)
                    pe.wait_ge(S["yst"][k], r + 1)
                    pe.wait_ge(S["prod"][k], r)
                    for a in range(E0 // 2):
                        mm = pe.transpose(ps[4 + k][:, a * P:(a + 1) * P],
                                          yst[:, k, 2 * a:2 * a + 2, :].rearrange("p e s -> p (e s)"), ident)
                    mm.then_inc(S["y_ps"][k], 1)
                pe.wait_ge(S["gsel"][0], 2 * r + 2)
                pe.wait_ge(S["gate"][0], r)
                pe.matmul(ps[7][:, 0:2 * D], m.ones16[:], gsel[:].rearrange("p s d -> p (s d)"), start=True,
                          stop=True).then_inc(S["gate_ps"][0], 1)
                for k in range(2):
                    pe.wait_ge(S["ysl"][k], r + 1)
                    pe.wait_ge(S["pickT"][k], 2 * r + 2)
                    for c in range(NCH):
                        for a in range(E0 // 2):
                            mm = pe.matmul(ps[4 + k][:, c * D:(c + 1) * D], pickT[:, k, a, c * P:(c + 1) * P],
                                           ysl[:, k, a, :], start=(a == 0), stop=(a == E0 // 2 - 1))
                    mm.then_inc(S["out_ps"][k], 1)

        @block.scalar
        def _(act):
            with act.Fori(0, PAIRS, 1) as r:
                for k in range(2):
                    act.wait_ge(S["out_ps"][k], r)
                    act.wait_ge(S["pickT_ps"][k], r + 1)
                    for a in range(2):
                        act.activation(pickT[:, k, 2 * a:2 * a + 2, :],
                                       ps[2 * k + a][:, :].rearrange("p (a t) -> p a t", a=2),
                                       ACT.Copy).then_inc(S["pickT"][k], 1)
                act.wait_ge(S["gate_ps"][0], r + 1)
                act.wait_ge(S["prod"][1], r)
                act.activation(gate[:], ps[7][:, 0:2 * D].rearrange("p (s d) -> p s d", s=2),
                               ACT.Copy).then_inc(S["gate"][0], 1)


SCAN_J = NST // 2
RING = 4


def scan_phase(nc, d, m, ps):
    with ExitStack() as ctx:
        sem = semaphores(nc, ctx, "s_")

        def sb(n, s, dt=F32):
            return ctx.enter_context(nc.sbuf_tensor("s_" + n, s, dt))

        stats, mv = sb("stats", [P, NCH, 6]), sb("mv", [P, NCH, 2])
        lnv, rstd = sb("lnv", [P, NCH]), sb("rstd", [P, NCH])
        ostats, omv = sb("ostats", [P, NCH, 6]), sb("omv", [P, NCH, 2])
        olnv, orstd = sb("olnv", [P, NCH]), sb("orstd", [P, NCH])
        xn = sb("xn", [P, NCH, D])
        hT = sb("hT", [P, 2, L])
        acc = sb("acc", [P, NH, L])
        u = sb("u", [P, 2, NH, L])
        z = sb("z", [P, 2, NH, L])
        dlow = sb("dlow", [P, L])
        t1 = sb("t1", [P, NH, L])
        soft, e, ebig, cub = (sb(n, [P, NH, L]) for n in ("soft", "e", "ebig", "cub"))
        dt = sb("dt", [P, 2, NH, L])
        dtu = sb("dtu", [P, 2, NH, L])
        bc = sb("bc", [3 * 32, 2, L], BF16)
        r1 = sb("r1", [3 * 32, L])
        mid = sb("mid", [3 * 32, L], BF16)
        spread = sb("spread", [3 * 32, 32, P], BF16)
        aneg = sb("aneg", [P, NH, NST])
        dA = sb("dA", [P, RING, NH, 2, L])
        dbu = sb("dbu", [P, 2, NH, 2, L])
        hs = sb("hs", [P, 2, NH, 2, L])
        hc = sb("hc", [P, 2, NH, 2, L])
        yt, yz = sb("yt", [P, NH, L]), sb("yz", [P, NH, L])
        gsel, gate = sb("gsel", [B, 2, D]), sb("gate", [P, 2, D])
        oh = sb("oh", [P, NCH, D])
        names = ("v_passed p_passed v_pre v_prep v_fin init a_exp "
                 "B_ps C_ps dA_ready dbu_done scanned hc_ready y_part "
                 "e_ready e_bound e_cubic st rs xn xT h xs_ps z_ps conv dlow u_ready z_ready dt_ps t1 abs soft dt_ready dtu_ready "
                 "bc_mid oln bc_ready gsel gate_ps gate "
                 "weights y_read yz out_ps ost ors o_read done").split()
        S = {n: sem(n) for n in names}
        ident = m.const[:, C_ID:C_ID + P]
        bB, bC, bY, bX, bZ, bT = ps[0:2], ps[2:4], ps[4], ps[5], ps[6], ps[7]
        col = lambda h, i: m.bcol[:, h, i:i + 1]
        CONV_B, DT_B, DSKIP, ALOG = 4, 5, 6, 7
        block = ctx.enter_context(nc.Block())

        def sequences(eng, body, last):
            body(0, 0, True, True)
            with eng.Fori(0, PAIRS - 1, 1) as r:
                body(2 * r + 1, 1, False, True)
                body(2 * r + 2, 0, False, True)
            body(B - 1, 1, False, False)
            last(B - 1, 1)

        @block.vector
        def _(dve):
            tick0, settle0, _ = ticker(dve, S["v_pre"])
            tick0(dve.tensor_copy(spread[:], m.const[0:96, C_REP:C_REP + 32].unsqueeze(2).broadcast_to([96, 32, P])))
            tick0(dve.memset(dA[:, :, :, :, 0:1], 0.0))
            dve.wait_ge(S["a_exp"], 1)
            tick0(dve.tensor_scalar(aneg[:], aneg[:], -1.0, None, ALU.mult))
            settle0()
            dve.sem_inc(S["init"], 1)

            def prepare(step, b, k, T):
                tick, settle = T
                if step == 0:
                    for c in range(NCH):
                        tick(dve.bn_stats(stats[:, c, :], m.x_res[:, b * NCH + c, :]))
                    settle(b)
                    pause(dve, S["v_passed"])
                    for c in range(NCH):
                        dve.bn_aggr(mv[:, c, :], stats[:, c, :]).then_inc(S["st"], 1)
                if step == 1:
                    dve.wait_ge(S["rs"], b + 1)
                    dve.wait_ge(S["st"], 2 * b + 2)
                    for c in range(NCH):
                        dve.tensor_scalar(xn[:, c, :], m.x_res[:, b * NCH + c, :], mv[:, c, 0:1], rstd[:, c:c + 1],
                                          ALU.subtract, ALU.mult).then_inc(S["xn"], 1)
                if step == 4:
                    dve.wait_ge(S["xs_ps"], b + 1)
                    for h in range(NH):
                        tick(dve.tensor_scalar(acc[:, h, :], bX[:, h * L:(h + 1) * L], col(h, KCONV - 1),
                                               col(h, CONV_B), ALU.mult, ALU.add))
                    dve.tensor_copy(bc[:, k, :], bT[0:96, 0:L]).then_inc(S["bc_mid"], 1)
                    for s in range(1, KCONV):
                        settle(b)
                        for h in range(NH):
                            ins = dve.scalar_tensor_tensor(acc[:, h, s:], bX[:, h * L:(h + 1) * L - s],
                                                           col(h, KCONV - 1 - s), acc[:, h, s:], ALU.mult, ALU.add)
                            if s < KCONV - 1:
                                tick(ins)
                            else:
                                ins.then_inc(S["conv"], 1)
                        if s == 1:
                            dve.wait_ge(S["bc_mid"], b + 1)
                            tick(dve.tensor_tensor(r1[:], bT[0:96, 0:L], bc[:, k, :], ALU.subtract))
                        if s == 2:
                            tick(dve.tensor_copy(bc[32:64, k, :], r1[32:64, :]))
                            tick(dve.tensor_copy(mid[64:96, :], r1[64:96, :]))
                    dve.tensor_tensor(bc[64:96, k, :], r1[64:96, :], mid[64:96, :], ALU.subtract)\
                        .then_inc(S["bc_ready"], 1)
                if step == 5:
                    dve.wait_ge(S["dt_ps"], b + 1)
                    for h in range(NH):
                        dve.tensor_scalar(t1[:, h, :], bX[:, h * L:(h + 1) * L], col(h, DT_B), None,
                                          ALU.add).then_inc(S["t1"], 1)
                if step == 6:
                    dve.wait_ge(S["e_cubic"], b + 1)
                    tick(dve.tensor_tensor(cub[:], cub[:], e[:], ALU.mult))
                    settle(b)
                    tick(dve.scalar_tensor_tensor(cub[:], cub[:], 1.0, e[:], ALU.add, ALU.mult))
                    settle(b)
                    dve.wait_ge(S["soft"], b + 1)
                    tick(dve.tensor_tensor(cub[:], cub[:], soft[:], ALU.min))
                    settle(b)
                    dve.scalar_tensor_tensor(dt[:, k], t1[:], 0.0, cub[:], ALU.max, ALU.add)\
                        .then_inc(S["dt_ready"], 1)
                    dve.wait_ge(S["dt_ready"], b + 1)
                    dve.wait_ge(S["u_ready"], b + 1)
                    dve.tensor_tensor(dtu[:, k], dt[:, k], u[:, k], ALU.mult).then_inc(S["dtu_ready"], 1)

            def finish(step, b, k, T):
                tick, settle = T
                if step == 0:
                    dve.wait_ge(S["y_part"], 8 * b + 8)
                    for h in range(NH):
                        dve.scalar_tensor_tensor(yt[:, h, :], u[:, k, h, :], col(h, DSKIP), bY[:, h * L:(h + 1) * L],
                                                 ALU.mult, ALU.add).then_inc(S["y_read"], 1)
                    dve.wait_ge(S["y_read"], 2 * b + 2)
                    dve.wait_ge(S["z_ready"], b + 1)
                    dve.tensor_tensor(yz[:], yt[:], z[:, k], ALU.mult).then_inc(S["yz"], 1)
                if step == 2:
                    dve.wait_ge(S["out_ps"], b + 1)
                    for c in range(NCH):
                        tick(dve.bn_stats(ostats[:, c, :], bZ[:, c * D:(c + 1) * D]))
                    settle(b)
                    pause(dve, S["v_passed"])
                    for c in range(NCH):
                        dve.bn_aggr(omv[:, c, :], ostats[:, c, :]).then_inc(S["ost"], 1)
                if step == 3:
                    dve.wait_ge(S["ors"], b + 1)
                    dve.wait_ge(S["ost"], 2 * b + 2)
                    for c in range(NCH):
                        dve.tensor_scalar(oh[:, c, :], bZ[:, c * D:(c + 1) * D], omv[:, c, 0:1], orstd[:, c:c + 1],
                                          ALU.subtract, ALU.mult).then_inc(S["o_read"], 1)
                    dve.wait_ge(S["o_read"], 2 * b + 2)
                    dve.wait_ge(S["gate"], b + 1)
                    tick(dve.tensor_tensor(oh[:], oh[:], gate[:, 0:1, :].broadcast_to([P, NCH, D]), ALU.mult))
                    settle(b)
                    tick(dve.tensor_tensor(oh[:], oh[:], gate[:, 1:2, :].broadcast_to([P, NCH, D]), ALU.add))
                    settle(b)
                    xs = m.x_res[:, bass.ds(b * NCH, NCH), :]
                    dve.tensor_tensor(xs, xs, oh[:], ALU.add).then_inc(S["done"], 1)

            def times_B(b, k, j):
                dve.wait_ge(S["B_ps"], 8 * b + j + 1)
                if j == 0:
                    dve.wait_ge(S["dtu_ready"], b + 1)
                dve.tensor_tensor(dbu[:, j % 2], dtu[:, k].unsqueeze(2).broadcast_to([P, NH, 2, L]),
                                  bB[j % 2][:, :].rearrange("p (n t) -> p n t", n=2).unsqueeze(1).broadcast_to(
                                      [P, NH, 2, L]), ALU.mult).then_inc(S["dbu_done"], 1)

            def recur(b, j):
                flat = lambda a: a.rearrange("p h n t -> p (h n t)")
                dve.wait_ge(S["dbu_done"], 8 * b + j + 1)
                dve.wait_ge(S["dA_ready"], 8 * b + j + 1)
                dve.tensor_tensor_scan(flat(hs[:, j % 2]), flat(dA[:, j % RING]), flat(dbu[:, j % 2]), 0.0,
                                       ALU.mult, ALU.add).then_inc(S["scanned"], 1)

            def times_C(b, j, first):
                dve.wait_ge(S["scanned"], 8 * b + j + 1)
                dve.wait_ge(S["C_ps"], 8 * b + j + 1)
                if not (first and j < 2):
                    dve.wait_ge(S["y_part"], 8 * b + j - 1)
                dve.tensor_tensor(hc[:, j % 2], hs[:, j % 2],
                                  bC[j % 2][:, :].rearrange("p (n t) -> p n t", n=2).unsqueeze(1).broadcast_to(
                                      [P, NH, 2, L]), ALU.mult).then_inc(S["hc_ready"], 1)

            def body(b, k, first, prepares):
                tp, sp_, _ = ticker(dve, S["v_prep"], SCAN_PREP)
                tf, sf, _ = ticker(dve, S["v_fin"], SCAN_FIN)
                for j in range(SCAN_J):
                    recur(b, j)
                    if j + 1 < SCAN_J:
                        times_B(b, k, j + 1)
                    elif prepares:
                        times_B(b + 1, 1 - k, 0)
                    if not first:
                        finish(j, b - 1, 1 - k, (tf, sf))
                    if prepares:
                        prepare(j, b + 1, 1 - k, (tp, sp_))
                    times_C(b, j, first)
                    if j == SCAN_J - 1:
                        if not first:
                            dve.wait_ge(S["gate_ps"], b)
                        dve.tensor_scalar(gsel[:], m.gates[:, 1, :].rearrange("p (a d) -> p a d", a=3)[:, 0:3:2, :],
                                          m.const[0:B, bass.ds(C_ID + b, 1)], None, ALU.mult).then_inc(S["gsel"], 1)

            def last(b, k):
                tf, sf, _ = ticker(dve, S["v_fin"], SCAN_FIN)
                for j in range(SCAN_J):
                    finish(j, b, k, (tf, sf))

            tp, sp_, _ = ticker(dve, S["v_prep"], SCAN_PREP)
            for j in range(SCAN_J):
                prepare(j, 0, 0, (tp, sp_))
            times_B(0, 0, 0)
            sequences(dve, body, last)

        @block.scalar
        def _(act):
            act.activation(aneg[:], m.bcol[:, :, ALOG:], ACT.Exp).then_inc(S["a_exp"], 1)
            act.preload_act_table_set(EXPLN)
            act.wait_ge(S["init"], 1)

            def prepare(step, b, k):
                if step == 0:
                    act.wait_ge(S["st"], 2 * b + 2)
                    act.activation(lnv[:], mv[:, :, 1], ACT.Ln, bias=m.eps[:, 0:1]).then_inc(S["abs"], 1)
                    act.wait_ge(S["abs"], 2 * b + 1)
                    act.activation(rstd[:], lnv[:], ACT.Exp, scale=-0.5).then_inc(S["rs"], 1)
                if step == 2:
                    act.wait_ge(S["xT"], b + 1)
                    act.activation(hT[:, k, :], bT[:, 0:L], ACT.Identity, bias=m.modT[:, 1, 0, bass.ds(b, 1)],
                                   scale=m.modT[:, 1, 1, bass.ds(b, 1)]).then_inc(S["h"], 1)
                if step == 3:
                    act.wait_ge(S["xs_ps"], b + 1)
                    act.activation(dlow[96:96 + RDT, :], bT[96:96 + RDT, 0:L], ACT.Copy).then_inc(S["dlow"], 1)
                if step == 4:
                    act.wait_ge(S["z_ps"], b + 1)
                    act.activation(z[:, k], bZ[:, :].rearrange("p (h t) -> p h t", h=NH), ACT.Silu)\
                       .then_inc(S["z_ready"], 1)
                    act.wait_ge(S["conv"], 2 * b + 2)
                    act.activation(u[:, k], acc[:], ACT.Silu).then_inc(S["u_ready"], 1)
                    act.preload_act_table_set(EXPLN)
                if step == 5:
                    act.wait_ge(S["t1"], 2 * b + 2)
                    act.activation(soft[:], t1[:], ACT.Abs).then_inc(S["abs"], 1)
                    act.wait_ge(S["abs"], 2 * b + 2)
                    act.activation(e[:], soft[:], ACT.Exp, scale=-1.0).then_inc(S["e_ready"], 1)
                    act.wait_ge(S["e_bound"], b + 1)
                    act.activation(soft[:], ebig[:], ACT.Ln, bias=m.eps[:, 2:3]).then_inc(S["soft"], 1)

            def finish(step, b, k):
                if step == 0:
                    act.wait_ge(S["gate_ps"], b + 1)
                    act.activation(gate[:], bT[:, 0:2 * D].rearrange("p (a d) -> p a d", a=2), ACT.Copy)\
                       .then_inc(S["gate"], 1)
                if step == 2:
                    act.wait_ge(S["ost"], 2 * b + 2)
                    act.activation(olnv[:], omv[:, :, 1], ACT.Ln, bias=m.eps[:, 0:1]).then_inc(S["oln"], 1)
                    act.wait_ge(S["oln"], b + 1)
                    act.activation(orstd[:], olnv[:], ACT.Exp, scale=-0.5).then_inc(S["ors"], 1)

            def decays(b, k, j, free):
                if j == 0:
                    act.wait_ge(S["dt_ready"], b + 1)
                if free:
                    act.wait_ge(S["scanned"], 8 * b + j - RING + 1)
                for h in range(NH):
                    for n in range(2):
                        ins = act.activation(dA[:, j % RING, h, n, 1:], dt[:, k, h, 1:], ACT.Exp,
                                             scale=aneg[:, h, 2 * j + n:2 * j + n + 1])
                ins.then_inc(S["dA_ready"], 1)

            def body(b, k, first, prepares):
                for j in range(SCAN_J):
                    if j < RING:
                        decays(b, k, j + RING, True)
                    if not first:
                        finish(j, b - 1, 1 - k)
                    if prepares:
                        prepare(j, b + 1, 1 - k)
                        if j == 6:
                            decays(b + 1, 1 - k, 0, True)
                            decays(b + 1, 1 - k, 1, True)
                        if j == 7:
                            decays(b + 1, 1 - k, 2, True)
                            decays(b + 1, 1 - k, 3, True)

            def last(b, k):
                for j in range(SCAN_J):
                    finish(j, b, k)

            for j in range(SCAN_J):
                prepare(j, 0, 0)
            for j in range(RING):
                decays(0, 0, j, False)
            sequences(act, body, last)

        @block.sync
        def _(sp):
            sp.dma_start(m.w13[:], d["w13"]).then_inc(S["weights"], 16)
            sp.dma_start(m.w2d[:], d["w2d"]).then_inc(S["weights"], 16)
            sp.wait_ge(S["weights"], 32)

        @block.gpsimd
        def _(pool):
            with pool.Fori(0, B, 1) as b:
                pool.wait_ge(S["e_ready"], b + 1)
                pause(pool, S["p_passed"])
                pool.tensor_scalar(ebig[:], e[:], SMALL_E, None, ALU.max).then_inc(S["e_bound"], 1)
                pool.tensor_scalar(cub[:], e[:], 1.0 / 3, -0.5, ALU.mult, ALU.add).then_inc(S["e_cubic"], 1)

        @block.tensor
        def _(pe):
            pe.wait_ge(S["init"], 1)

            def prepare(step, b, k):
                if step == 2:
                    pe.wait_ge(S["xn"], 2 * b + 2)
                    if not (isinstance(b, int) and b == 0):
                        pe.wait_ge(S["gate"], b - 1)
                    for c in range(NCH):
                        mm = pe.transpose(bT[:, c * P:(c + 1) * P], xn[:, c, :], ident)
                    mm.then_inc(S["xT"], 1)
                if step == 3:
                    pe.wait_ge(S["h"], b + 1)
                    for h in range(NH):
                        pe.matmul(bX[:, h * L:(h + 1) * L], m.w_in[:, h * P:(h + 1) * P], hT[:, k, :],
                                  start=True, stop=True)
                    pe.matmul(bT[0:104, 0:L], m.w_in[:, 2 * DI:2 * DI + 104], hT[:, k, :], start=True,
                              stop=True).then_inc(S["xs_ps"], 1)
                if step == 4:
                    if not (isinstance(b, int) and b == 0):
                        pe.wait_ge(S["o_read"], 2 * b - 2)
                    for h in range(NH):
                        mm = pe.matmul(bZ[:, h * L:(h + 1) * L], m.w_in[:, DI + h * P:DI + (h + 1) * P], hT[:, k, :],
                                       start=True, stop=True)
                    mm.then_inc(S["z_ps"], 1)
                if step == 5:
                    pe.wait_ge(S["dlow"], b + 1)
                    pe.wait_ge(S["conv"], 2 * b + 2)
                    for h in range(NH):
                        mm = pe.matmul(bX[:, h * L:(h + 1) * L], m.wdt[96:96 + RDT, h * P:(h + 1) * P],
                                       dlow[96:96 + RDT, :], start=True, stop=True)
                    mm.then_inc(S["dt_ps"], 1)

            def finish(step, b, k):
                if step == 0:
                    pe.wait_ge(S["gsel"], b + 1)
                    pe.matmul(bT[:, 0:2 * D], m.ones16[:], gsel[:].rearrange("p a d -> p (a d)"), start=True,
                              stop=True).then_inc(S["gate_ps"], 1)
                if step == 1:
                    pe.wait_ge(S["yz"], b + 1)
                    for c in range(NCH):
                        o = bZ[:, c * D:(c + 1) * D]
                        for h in range(NH):
                            pe.matmul(o, yz[:, h, c * P:(c + 1) * P], m.w_outT[:, h, :], start=(h == 0), stop=False)
                        mm = pe.matmul(o, hT[:, k, c * P:(c + 1) * P], ident, start=False, stop=True)
                    mm.then_inc(S["out_ps"], 1)

            def rows(bank, b, k, j, first_row, ready):
                for n in range(2):
                    mm = pe.matmul(bank[:, n * L:(n + 1) * L], spread[:, first_row + 2 * j + n, :], bc[:, k, :],
                                   start=True, stop=True)
                mm.then_inc(ready, 1)

            def B_rows(b, k, j, first):
                if j == 0:
                    pe.wait_ge(S["bc_ready"], b + 1)
                if not (first and j < 2):
                    pe.wait_ge(S["dbu_done"], 8 * b + j - 1)
                rows(bB[j % 2], b, k, j, 0, S["B_ps"])

            def C_rows(b, k, j, first):
                if not (first and j < 2):
                    pe.wait_ge(S["hc_ready"], 8 * b + j - 1)
                rows(bC[j % 2], b, k, j, NST, S["C_ps"])

            def sum_states(b, j, first):
                pe.wait_ge(S["hc_ready"], 8 * b + j + 1)
                if j == 0 and not first:
                    pe.wait_ge(S["y_read"], 2 * b)
                for n in range(2):
                    mm = pe.matmul(bY[:, :].rearrange("p (h t) -> p h t", h=NH), ident, hc[:, j % 2, :, n, :],
                                   start=(j == 0 and n == 0), stop=(j == SCAN_J - 1 and n == 1))
                mm.then_inc(S["y_part"], 1)

            def body(b, k, first, prepares):
                for j in range(SCAN_J):
                    if j + 1 < SCAN_J:
                        B_rows(b, k, j + 1, first)
                    elif prepares:
                        B_rows(b + 1, 1 - k, 0, False)
                    C_rows(b, k, j, first)
                    if j > 0:
                        sum_states(b, j - 1, first)
                    elif not first:
                        sum_states(b - 1, SCAN_J - 1, False)
                    if not first:
                        finish(j, b - 1, 1 - k)
                    if prepares:
                        prepare(j, b + 1, 1 - k)

            def last(b, k):
                sum_states(b, SCAN_J - 1, False)
                for j in range(SCAN_J):
                    finish(j, b, k)

            for j in range(SCAN_J):
                prepare(j, 0, 0)
            B_rows(0, 0, 0, True)
            sequences(pe, body, last)


SCAN_PREP, SCAN_FIN = 14, 4
SMALL_E = 2.0 ** -6


MAX_TILES = (B * L * TOPK + E1 * (P - 1)) // P
MOE_TILES = MAX_TILES + MAX_TILES % 2
ASSIGN = TILES * TOPK


def router_phase(nc, d, m, ps):
    with ExitStack() as ctx:
        sem = semaphores(nc, ctx, "r_")

        def sb(n, s, dt=F32):
            return ctx.enter_context(nc.sbuf_tensor("r_" + n, s, dt))

        Q = 2 * NCH
        stats, mv = sb("stats", [P, Q, 6]), sb("mv", [P, Q, 2])
        lnv, rstd = sb("lnv", [P, Q]), sb("rstd", [P, Q])
        xn = sb("xn", [P, Q, D])
        hT = sb("hT", [P, 2, L])
        sq = sb("sq", [P, 2 * L])
        lrms, rrms = sb("lrms", [P, 2 * L]), sb("rrms", [P, 2 * L])
        hf = sb("hf", [P, 2 * L])
        rows = sb("rows", [P, Q, D])
        gsel, gate = sb("gsel", [B, 2, D]), sb("gate", [P, 2, D])
        gh = sb("gh", [P, Q, D])
        mx, sh, ex = sb("mx", [P, Q]), sb("sh", [P, Q, E1]), sb("ex", [P, Q, E1])
        top = sb("top", [P, Q, 8])
        idx = sb("idx", [P, Q, 8], U32)
        den, rden = sb("den", [P, Q]), sb("rden", [P, Q])
        names = ("v_own v_passed a_own st rs xn xT h sq ms_ps rms hf lg_ps sh ex gsel gate_ps gate back_ps rows_ps rows "
                 "stored").split()
        S = {n: sem(n) for n in names}
        ident = m.const[:, C_ID:C_ID + P]
        block = ctx.enter_context(nc.Block())

        @block.vector
        def _(dve):
            with dve.Fori(0, PAIRS, 1) as r:
                tick, settle, ends = ticker(dve, S["v_own"], ROUTER_DVE)
                for q in range(Q):
                    tick(dve.bn_stats(stats[:, q, :], m.x_res[:, r * Q + q, :]))
                settle(r)
                pause(dve, S["v_passed"])
                for q in range(Q):
                    dve.bn_aggr(mv[:, q, :], stats[:, q, :]).then_inc(S["st"], 1)
                for k in range(2):
                    dve.tensor_scalar(gsel[:, k, :], m.gates[:, 1, D:2 * D],
                                      m.const[0:B, bass.ds(C_ID + 2 * r + k, 1)], None,
                                      ALU.mult).then_inc(S["gsel"], 1)
                dve.wait_ge(S["rs"], r + 1)
                dve.wait_ge(S["st"], Q * r + Q)
                for q in range(Q):
                    dve.tensor_scalar(xn[:, q, :], m.x_res[:, r * Q + q, :], mv[:, q, 0:1], rstd[:, q:q + 1],
                                      ALU.subtract, ALU.mult).then_inc(S["xn"], 1)
                dve.wait_ge(S["rms"], r + 1)
                dve.scalar_tensor_tensor(hf[:], hT[:].rearrange("p s t -> p (s t)"), m.gate1[:, E1:E1 + 1], rrms[:],
                                         ALU.mult, ALU.mult).then_inc(S["hf"], 1)
                dve.wait_ge(S["back_ps"], r + 1)
                dve.wait_ge(S["gate"], r + 1)
                for k in range(2):
                    tick(dve.tensor_tensor(gh[:, 2 * k:2 * k + 2, :],
                                           ps[2][:, k * L:(k + 1) * L].rearrange("p (c d) -> p c d", c=NCH),
                                           gate[:, k:k + 1, :].broadcast_to([P, NCH, D]), ALU.mult))
                settle(r)
                xs = m.x_res[:, bass.ds(r * Q, Q), :]
                tick(dve.tensor_tensor(xs, xs, gh[:], ALU.add))
                dve.wait_ge(S["lg_ps"], r + 1)
                lg = ps[4][:, 0:Q * E1].rearrange("p (q e) -> p q e", q=Q)
                tick(dve.tensor_reduce(mx[:], lg, AX, ALU.max))
                settle(r)
                dve.tensor_tensor(sh[:], lg, mx[:].unsqueeze(2).broadcast_to([P, Q, E1]),
                                  ALU.subtract).then_inc(S["sh"], 1)
                dve.wait_ge(S["ex"], r + 1)
                pause(dve, S["v_passed"])
                for q in range(Q):
                    tick(dve.max(top[:, q, :], ex[:, q, :]))
                settle(r)
                pause(dve, S["v_passed"])
                for q in range(Q):
                    tick(dve.max_index(idx[:, q, :], top[:, q, :], ex[:, q, :]))
                tick(dve.tensor_tensor(den[:], top[:, :, 0], top[:, :, 1], ALU.add))
                settle(r)
                tick(dve.tensor_copy(m.expert[:, bass.ds(r * Q, Q), :], idx[:, :, 0:TOPK]))
                tick(dve.reciprocal(rden[:], den[:]))
                settle(r)
                tick(dve.tensor_tensor(m.weight[:, bass.ds(r * Q, Q), :], top[:, :, 0:TOPK],
                                       rden[:].unsqueeze(2).broadcast_to([P, Q, TOPK]), ALU.mult))
                settle(r)
                ends()

        @block.scalar
        def _(act):
            act.preload_act_table_set(EXPLN)
            with act.Fori(0, PAIRS, 1) as r:
                tick, settle, ends = ticker(act, S["a_own"], ROUTER_ACT)
                act.wait_ge(S["st"], Q * r + Q)
                tick(act.activation(lnv[:], mv[:, :, 1], ACT.Ln, bias=m.eps[:, 0:1]))
                settle(r)
                act.activation(rstd[:], lnv[:], ACT.Exp, scale=-0.5).then_inc(S["rs"], 1)
                act.wait_ge(S["gate_ps"], r + 1)
                act.activation(gate[:], ps[3][:, 0:2 * D].rearrange("p (s d) -> p s d", s=2),
                               ACT.Copy).then_inc(S["gate"], 1)
                act.wait_ge(S["xT"], r + 1)
                for k in range(2):
                    act.activation(hT[:, k, :], ps[0][:, k * L:(k + 1) * L], ACT.Identity,
                                   bias=m.modT[:, 1, 2, bass.ds(2 * r + k, 1)],
                                   scale=m.modT[:, 1, 3, bass.ds(2 * r + k, 1)]).then_inc(S["h"], 1)
                act.wait_ge(S["h"], 2 * r + 2)
                act.activation(sq[:], hT[:].rearrange("p s t -> p (s t)"), ACT.Square).then_inc(S["sq"], 1)
                act.wait_ge(S["ms_ps"], r + 1)
                tick(act.activation(lrms[:], ps[1][:, :], ACT.Ln, bias=m.eps[:, 1:2]))
                settle(r)
                act.activation(rrms[:], lrms[:], ACT.Exp, scale=-0.5).then_inc(S["rms"], 1)
                act.wait_ge(S["sh"], r + 1)
                act.activation(ex[:], sh[:], ACT.Exp).then_inc(S["ex"], 1)
                act.wait_ge(S["rows_ps"], r + 1)
                act.wait_ge(S["stored"], 16 * r)
                act.activation(rows[:], ps[5][:, :].rearrange("p (q d) -> p q d", q=Q), ACT.Copy)\
                   .then_inc(S["rows"], 1)
                ends()

        @block.sync
        def _(sp):
            with sp.Fori(0, PAIRS, 1) as r:
                sp.wait_ge(S["rows"], r + 1)
                sp.dma_start(m.hf_rows[bass.ds(r * Q * P, Q * P), :].rearrange("(q p) d -> p q d", p=P),
                             rows[:]).then_inc(S["stored"], 16)
            sp.wait_ge(S["stored"], 16 * PAIRS)

        @block.tensor
        def _(pe):
            with pe.Fori(0, PAIRS, 1) as r:
                pe.wait_ge(S["gsel"], 2 * r + 2)
                pe.matmul(ps[3][:, 0:2 * D], m.ones16[:], gsel[:].rearrange("p s d -> p (s d)"), start=True,
                          stop=True).then_inc(S["gate_ps"], 1)
                pe.wait_ge(S["xn"], Q * r + Q)
                for q in range(Q):
                    mm = pe.transpose(ps[0][:, q * P:(q + 1) * P], xn[:, q, :], ident)
                mm.then_inc(S["xT"], 1)
                pe.wait_ge(S["h"], 2 * r + 2)
                for k in range(2):
                    for c in range(NCH):
                        q = k * NCH + c
                        mm = pe.transpose(ps[2][:, q * D:(q + 1) * D], hT[:, k, c * P:(c + 1) * P], ident)
                mm.then_inc(S["back_ps"], 1)
                pe.wait_ge(S["sq"], r + 1)
                pe.matmul(ps[1][:, :], m.ones128[:], sq[:], start=True, stop=True).then_inc(S["ms_ps"], 1)
                pe.wait_ge(S["hf"], r + 1)
                for q in range(Q):
                    mm = pe.matmul(ps[4][:, q * E1:(q + 1) * E1], hf[:, q * P:(q + 1) * P], m.gate1[:, 0:E1],
                                   start=True, stop=True)
                mm.then_inc(S["lg_ps"], 1)
                for q in range(Q):
                    mm = pe.transpose(ps[5][:, q * P:(q + 1) * P], hf[:, q * P:(q + 1) * P], ident)
                mm.then_inc(S["rows_ps"], 1)


ROUTER_DVE, ROUTER_ACT = 20, 2


def slots_phase(nc, d, m, ps):
    with ExitStack() as ctx:
        sem = semaphores(nc, ctx, "m_")

        def sb(n, s, dt=F32):
            return ctx.enter_context(nc.sbuf_tensor("m_" + n, s, dt))

        NT = TILES * E1
        hot = sb("hot", [P, TOPK, TILES, E1])
        cnt = sb("cnt", [P, TILES, E1])
        before = sb("before", [P, P])
        incl = sb("incl", [P, E1, TILES])
        tot = sb("tot", [P, E1, TILES])
        run = sb("run", [P, E1, TILES])
        more = sb("more", [P, E1, TILES])
        full = sb("full", [P, E1])
        ntile, ctile, base, zeros = (sb(n, [P, E1]) for n in ("ntile", "ctile", "base", "zeros"))
        addr = sb("addr", [P, TILES, E1])
        pick = sb("pick", [P, TOPK, TILES, E1])
        slot = sb("slot", [P, TOPK, TILES])
        slot_i, lo_i, hi_i = (sb(n, [P, TOPK, TILES], U32) for n in ("slot_i", "lo_i", "hi_i"))
        lo, hi = sb("lo", [P, TOPK, TILES]), sb("hi", [P, TOPK, TILES])
        cmp = sb("cmp", [P, MOE_TILES, E1])
        etile = sb("etile", [P, MOE_TILES])
        hot_lo = sb("hot_lo", [P, 4, P])
        hot_hi = sb("hot_hi", [P, 4, MOE_TILES])
        idm, off, fil = (sb(n, [P, MOE_TILES]) for n in ("idm", "off", "fil"))
        tok_i = sb("tok_i", [P, MOE_TILES], U32)
        own, s_cnt, s_ps, s_map = sem("own"), sem("cnt"), sem("ps"), sem("map")
        s_hot = [sem(f"hot{i}") for i in range(4)]
        s_used = [sem(f"used{i}") for i in range(4)]
        block = ctx.enter_context(nc.Block())

        @block.tensor
        def _(pe):
            pe.wait_ge(s_cnt, 1)
            flat = cnt[:].rearrange("p t e -> p (t e)")
            pe.matmul(ps[0][:, 0:NT], before[:], flat, start=True, stop=True)
            pe.matmul(ps[1][:, 0:NT], m.ones128[:], flat, start=True, stop=True).then_inc(s_ps, 1)
            for i in range(4):
                pe.wait_ge(s_hot[i], 1)
                pe.matmul(ps[2][:, 0:MOE_TILES], hot_lo[:, i, :], hot_hi[:, i, :], start=(i == 0),
                          stop=False).then_inc(s_used[i], 1)
            with pe.Fori(1, ASSIGN // 4 - 1, 1) as r:
                for i in range(4):
                    pe.wait_ge(s_hot[i], r + 1)
                    pe.matmul(ps[2][:, 0:MOE_TILES], hot_lo[:, i, :], hot_hi[:, i, :], start=False,
                              stop=False).then_inc(s_used[i], 1)
            for i in range(4):
                pe.wait_ge(s_hot[i], ASSIGN // 4)
                mm = pe.matmul(ps[2][:, 0:MOE_TILES], hot_lo[:, i, :], hot_hi[:, i, :], start=False, stop=(i == 3))
            mm.then_inc(s_map, 1)

        @block.vector
        def _(dve):
            tick, settle, _ = ticker(dve, own)
            iota8 = m.const[:, C_IOTA8:C_IOTA8 + E1]
            for k in range(TOPK):
                tick(dve.tensor_tensor(hot[:, k], m.expert[:, :, k:k + 1].broadcast_to([P, TILES, E1]),
                                       iota8.unsqueeze(1).broadcast_to([P, TILES, E1]), ALU.is_equal))
            tick(dve.tensor_tensor(before[:], m.const[:, C_TRI:C_TRI + P], m.const[:, C_ID:C_ID + P], ALU.subtract))
            tick(dve.memset(zeros[:], 0.0))
            tick(dve.memset(run[:], 1.0))
            settle()
            tick(dve.memset(run[:, :, 0:1], 0.0))
            dve.tensor_tensor(cnt[:], hot[:, 0], hot[:, 1], ALU.add).then_inc(s_cnt, 1)
            dve.wait_ge(s_ps, 1)
            tick(dve.tensor_copy(tot[:], ps[1][:, 0:NT].rearrange("p (t e) -> p e t", e=E1)))
            settle()
            flat = lambda a: a[:].rearrange("p e t -> p (e t)")
            tick(dve.tensor_tensor_scan(flat(incl), flat(run), flat(tot), 0.0, ALU.mult, ALU.add))
            settle()
            tick(dve.tensor_scalar(full[:], incl[:, :, TILES - 1], 1.0, None, ALU.add))
            tick(dve.tensor_tensor(tot[:], incl[:], tot[:], ALU.subtract))
            settle()
            tick(dve.tensor_tensor(more[:], full[:].unsqueeze(2).broadcast_to([P, E1, TILES]),
                                   m.const[:, C_IOTA:C_IOTA + TILES].unsqueeze(1).broadcast_to([P, E1, TILES]),
                                   ALU.is_gt))
            settle()
            tick(dve.tensor_reduce(ntile[:], more[:], AX, ALU.add))
            settle()
            tick(dve.tensor_tensor_scan(ctile[:], ntile[:], zeros[:], 0.0, ALU.add, ALU.add))
            settle()
            tick(dve.tensor_tensor(base[:], ctile[:], ntile[:], ALU.subtract))
            settle()
            tick(dve.tensor_tensor(tot[:], tot[:], base[:].unsqueeze(2).broadcast_to([P, E1, TILES]), ALU.add))
            settle()
            tick(dve.scalar_tensor_tensor(addr[:].rearrange("p t e -> p e t"), tot[:], float(P),
                                          ps[0][:, 0:NT].rearrange("p (t e) -> p e t", e=E1), ALU.mult, ALU.add))
            settle()
            for k in range(TOPK):
                tick(dve.tensor_tensor(pick[:, k], hot[:, k], addr[:], ALU.mult))
            settle()
            tick(dve.tensor_reduce(slot[:], pick[:], AX, ALU.add))
            tick(dve.tensor_tensor(cmp[:], ctile[:].unsqueeze(1).broadcast_to([P, MOE_TILES, E1]),
                                   m.const[:, C_T72:C_T72 + MOE_TILES].unsqueeze(2).broadcast_to([P, MOE_TILES, E1]),
                                   ALU.is_le))
            settle()
            tick(dve.tensor_reduce(etile[:], cmp[:], AX, ALU.add))
            tick(dve.tensor_copy(slot_i[:], slot[:]))
            settle()
            tick(dve.tensor_scalar(m.etile[:], etile[:], float(E1 - 1), None, ALU.min))
            tick(dve.tensor_scalar(lo_i[:], slot_i[:], P - 1, None, ALU.bitwise_and))
            tick(dve.tensor_scalar(hi_i[:], slot_i[:], 7, None, ALU.logical_shift_right))
            settle()
            tick(dve.tensor_copy(lo[:], lo_i[:]))
            tick(dve.tensor_copy(hi[:], hi_i[:]))
            settle()
            lo_f, hi_f = (a[:].rearrange("p k t -> p (k t)") for a in (lo, hi))
            with dve.Fori(0, ASSIGN // 4, 1) as r:
                for i in range(4):
                    a = bass.ds(4 * r + i, 1)
                    dve.wait_ge(s_used[i], r)
                    dve.tensor_scalar(hot_lo[:, i, :], m.const[:, C_I128:C_I128 + P], lo_f[:, a], None,
                                      ALU.is_equal)
                    dve.tensor_scalar(hot_hi[:, i, :], m.const[:, C_T72:C_T72 + MOE_TILES], hi_f[:, a],
                                      m.const[:, bass.ds(C_VAL + 4 * r + i, 1)], ALU.is_equal,
                                      ALU.mult).then_inc(s_hot[i], 1)
            dve.wait_ge(s_map, 1)
            pad = m.const[:, C_PAD:C_PAD + MOE_TILES]
            tick(dve.tensor_scalar(idm[:], ps[2][:, 0:MOE_TILES], -1.0, None, ALU.add))
            settle()
            tick(dve.tensor_scalar(fil[:], idm[:], 0.0, None, ALU.is_ge))
            tick(dve.tensor_tensor(off[:], idm[:], pad, ALU.subtract))
            settle()
            tick(dve.tensor_tensor(off[:], off[:], fil[:], ALU.mult))
            tick(dve.tensor_scalar(idm[:], idm[:], 0.0, None, ALU.max))
            settle()
            tick(dve.tensor_tensor(m.to_row[:], off[:], pad, ALU.add))
            tick(dve.tensor_copy(tok_i[:], idm[:]))
            settle()
            tick(dve.tensor_scalar(m.from_row[:], tok_i[:], 1, None, ALU.logical_shift_right))
            settle()


def moe_phase(nc, d, m, ps):
    with ExitStack() as ctx:
        new = semaphores(nc, ctx, "x_")
        passed = new("passed")

        def sem(n):
            return [new(f"{n}{k}") for k in range(2)]

        def sb(n, s, dt=F32):
            return ctx.enter_context(nc.sbuf_tensor("x_" + n, s, dt))

        xT = sb("xT", [P, 2, P])
        a = sb("a", [P, 2, I1])
        h = sb("h", [P, 2, I1])
        hT = sb("hT", [IC, 2, NIC, P])
        y = (sb("y0", [P, D]), sb("y1", [P, D]))
        src = (sb("src0", [P, 1], U32), sb("src1", [P, 1], U32))
        dst = (sb("dst0", [P, 1], U32), sb("dst1", [P, 1], U32))
        xg = (sb("xg0", [P, D]), sb("xg1", [P, D]))
        names = "src rows xT_ps xT ag_ps a h hT_ps hT y_ps y y_free dst sent".split()
        S = {n: sem(n) for n in names}
        FREE = "h hT y_ps hT_ps y y_free".split()
        ident = m.const[:, C_ID:C_ID + P]
        block = ctx.enter_context(nc.Block())
        R = MOE_TILES // 2

        def steps(eng, step):
            step(None, (0, 0), None, None)
            step((0, 0), (0, 1), None, None)
            step((0, 1), (1, 0), (0, 0), None)
            with eng.Fori(0, R - 2, 1) as r:
                step((r + 1, 0), (r + 1, 1), (r, 1), (r, 0))
                step((r + 1, 1), (r + 2, 0), (r + 1, 0), (r, 1))
            step((R - 1, 0), (R - 1, 1), (R - 2, 1), (R - 2, 0))
            step((R - 1, 1), None, (R - 1, 0), (R - 2, 1))
            step(None, None, (R - 1, 1), (R - 1, 0))
            step(None, None, None, (R - 1, 1))

        @block.gpsimd
        def _(pool):
            for n in FREE:
                for k in range(2):
                    pool.sem_inc(S[n][k], 1)

            def fetch(r, k, used=True):
                if used:
                    pool.wait_ge(S["xT_ps"][k], r)
                pool.tensor_copy(src[k][:], m.from_row[:, bass.ds(2 * r + k, 1)]).then_inc(S["src"][k], 1)
                pool.wait_ge(S["src"][k], r + 1)
                pause(pool, passed)
                pool.indirect_dma_start(xg[k][:], None, m.hf_rows[:, :],
                                        bass.IndirectOffsetOnAxis(ap=src[k][:, 0:1], axis=0)).then_inc(S["rows"][k], 16)

            def send(r, k):
                pool.wait_ge(S["y"][k], r + 2)
                pool.tensor_copy(dst[k][:], m.to_row[:, bass.ds(2 * r + k, 1)]).then_inc(S["dst"][k], 1)
                pool.wait_ge(S["dst"][k], r + 1)
                pause(pool, passed)
                pool.indirect_dma_start(m.y_rows[:, :], bass.IndirectOffsetOnAxis(ap=dst[k][:, 0:1], axis=0),
                                        y[k][:], None).then_inc(S["sent"][k], 16)

            for r in range(3):
                for k in range(2):
                    fetch(r, k, used=(r > 0))
            with pool.Fori(0, R - 3, 1) as r:
                for k in range(2):
                    fetch(r + 3, k)
                    send(r, k)
            for r in range(R - 3, R):
                for k in range(2):
                    send(r, k)

        @block.sync
        def _(sp):
            with sp.Fori(0, R, 1) as r:
                for k in range(2):
                    sp.wait_ge(S["sent"][k], 16 * (r + 1))
                    sp.sem_inc(S["y_free"][k], 1)

        @block.tensor
        def _(pe):
            def expert(r, k):
                return pe.value_load(m.etile[0:1, bass.ds(2 * r + k, 1)], min_val=0, max_val=E1 - 1)

            def step(now, after, before, last):
                if now is not None:
                    r, k = now
                    e = expert(r, k)
                    pe.wait_ge(S["xT"][k], r + 1)
                    pe.wait_ge(S["h"][k], r + 1)
                    for i in range(2):
                        mm = pe.matmul(ps[2 * k + i][:, 0:I1], xT[:, k, :],
                                       m.w13[:, bass.ds(e * 2 + i, 1), :].rearrange("p e i -> p (e i)"),
                                       start=True, stop=True)
                    mm.then_inc(S["ag_ps"][k], 1)
                if last is not None:
                    e = expert(*last)
                if after is not None:
                    r, k = after
                    pe.wait_ge(S["rows"][k], 16 * (r + 1))
                    pe.transpose(ps[4][:, 0:P], xg[k][:], ident).then_inc(S["xT_ps"][k], 1)
                if before is not None:
                    r, k = before
                    pe.wait_ge(S["h"][k], r + 2)
                    pe.wait_ge(S["hT"][k], r + 1)
                    for i in range(NIC):
                        mm = pe.transpose(ps[6 + k][0:IC, i * P:(i + 1) * P], h[:, k, i * IC:(i + 1) * IC], ident)
                    mm.then_inc(S["hT_ps"][k], 1)
                if last is not None:
                    r, k = last
                    pe.wait_ge(S["hT"][k], r + 2)
                    pe.wait_ge(S["y"][1 - k], r + k + 1)
                    for i in range(NIC):
                        mm = pe.matmul(ps[5][:, 0:D], hT[:, k, i, :],
                                       m.w2d[:, bass.ds(e * NIC + i, 1), :].rearrange("p e d -> p (e d)"),
                                       start=(i == 0), stop=(i == NIC - 1))
                    mm.then_inc(S["y_ps"][k], 1)

            steps(pe, step)

        @block.scalar
        def _(act):
            act.preload_act_table_set("silu_and_others")

            def step(now, after, before, last):
                if now is not None:
                    r, k = now
                    act.wait_ge(S["ag_ps"][k], r + 1)
                    act.wait_ge(S["h"][k], r + 1)
                    act.activation(a[:, k, :], ps[2 * k][:, 0:I1], ACT.Silu).then_inc(S["a"][k], 1)
                if after is not None:
                    r, k = after
                    act.wait_ge(S["xT_ps"][k], r + 1)
                    act.activation(xT[:, k, :], ps[4][:, 0:P], ACT.Copy).then_inc(S["xT"][k], 1)
                if before is not None:
                    r, k = before
                    act.wait_ge(S["hT_ps"][k], r + 2)
                    act.wait_ge(S["y_ps"][k], r + 1)
                    act.activation(hT[:, k], ps[6 + k][0:IC, :].rearrange("p (i t) -> p i t", i=NIC),
                                   ACT.Copy).then_inc(S["hT"][k], 1)

            steps(act, step)

        @block.vector
        def _(dve):
            def step(now, after, before, last):
                if now is not None:
                    r, k = now
                    dve.wait_ge(S["a"][k], r + 1)
                    dve.wait_ge(S["hT_ps"][k], r + 1)
                    dve.tensor_tensor(h[:, k, :], a[:, k, :], ps[2 * k + 1][:, 0:I1], ALU.mult).then_inc(S["h"][k], 1)
                if last is not None:
                    r, k = last
                    dve.wait_ge(S["y_ps"][k], r + 2)
                    dve.wait_ge(S["y_free"][k], r + 1)
                    dve.tensor_copy(y[k][:], ps[5][:, 0:D]).then_inc(S["y"][k], 1)

            steps(dve, step)


def output_phase(nc, d, m, ps):
    with ExitStack() as ctx:
        new = semaphores(nc, ctx, "o_")

        def sem(n):
            return [new(f"{n}{k}") for k in range(2)]

        def sb(n, s, dt=F32):
            return ctx.enter_context(nc.sbuf_tensor("o_" + n, s, dt))

        Q = 2 * NCH
        yr = sb("yr", [P, 2, Q, TOPK, D])
        wy = sb("wy", [P, 2, Q, TOPK, D])
        sm = sb("sm", [P, 2, Q, D])
        o = sb("o", [P, 2, Q, D])
        gsel, gate = sb("gsel", [B, 2, 2, D]), sb("gate", [P, 2, 2, D])
        names = "loaded wy sum gsel gate_ps gate gated o stored".split()
        S = {n: sem(n) for n in names}
        block = ctx.enter_context(nc.Block())

        @block.sync
        def _(sp):
            with sp.Fori(0, PAIRS // 2, 1) as r:
                for k in range(2):
                    sp.wait_ge(S["wy"][k], r)
                    sp.dma_start(yr[:, k].rearrange("p q k d -> p q (k d)"),
                                 m.y_rows[bass.ds((2 * r + k) * Q * P * TOPK, Q * P * TOPK), :].rearrange(
                                     "(q p k) d -> p q (k d)", p=P, k=TOPK)).then_inc(S["loaded"][k], 16)

        @block.scalar
        def _(act):
            with act.Fori(0, PAIRS // 2, 1) as r:
                for k in range(2):
                    act.wait_ge(S["gate_ps"][k], r + 1)
                    act.wait_ge(S["gated"][k], r)
                    act.activation(gate[:, k], ps[k][:, 0:2 * D].rearrange("p (s d) -> p s d", s=2),
                                   ACT.Copy).then_inc(S["gate"][k], 1)
                    act.wait_ge(S["o"][k], r + 1)
                    act.dma_start(m.out[bass.ds((2 * r + k) * 2, 2)].rearrange("b (c t) d -> t (b c) d", t=P),
                                  o[:, k]).then_inc(S["stored"][k], 16)
            for k in range(2):
                act.wait_ge(S["stored"][k], 16 * PAIRS // 2)

        @block.tensor
        def _(pe):
            with pe.Fori(0, PAIRS // 2, 1) as r:
                for k in range(2):
                    pe.wait_ge(S["gsel"][k], 2 * r + 2)
                    pe.wait_ge(S["gate"][k], r)
                    pe.matmul(ps[k][:, 0:2 * D], m.ones16[:], gsel[:, k].rearrange("p s d -> p (s d)"), start=True,
                              stop=True).then_inc(S["gate_ps"][k], 1)

        @block.vector
        def _(dve):
            with dve.Fori(0, PAIRS // 2, 1) as r:
                for k in range(2):
                    dve.wait_ge(S["gate_ps"][k], r)
                    for s in range(2):
                        dve.tensor_scalar(gsel[:, k, s, :], m.gates[:, 1, D:2 * D],
                                          m.const[0:B, bass.ds(C_ID + 4 * r + 2 * k + s, 1)], None,
                                          ALU.mult).then_inc(S["gsel"][k], 1)
                for k in range(2):
                    tiles = bass.ds((2 * r + k) * Q, Q)
                    dve.wait_ge(S["loaded"][k], 16 * (r + 1))
                    dve.tensor_tensor(wy[:, k], yr[:, k],
                                      m.weight[:, tiles, :].unsqueeze(3).broadcast_to([P, Q, TOPK, D]),
                                      ALU.mult).then_inc(S["wy"][k], 1)
                    dve.wait_ge(S["wy"][k], r + 1)
                    dve.tensor_tensor(sm[:, k], wy[:, k, :, 0, :], wy[:, k, :, 1, :], ALU.add)\
                       .then_inc(S["sum"][k], 1)
                    dve.wait_ge(S["sum"][k], r + 1)
                    dve.wait_ge(S["gate"][k], r + 1)
                    dve.tensor_tensor(wy[:, k, :, 0, :].rearrange("p (s c) d -> p s c d", s=2),
                                      sm[:, k].rearrange("p (s c) d -> p s c d", s=2),
                                      gate[:, k].unsqueeze(2).broadcast_to([P, 2, NCH, D]), ALU.mult)\
                       .then_inc(S["gated"][k], 1)
                    dve.wait_ge(S["gated"][k], r + 1)
                    dve.wait_ge(S["stored"][k], 16 * r)
                    dve.tensor_tensor(o[:, k], wy[:, k, :, 0, :], m.x_res[:, tiles, :], ALU.add)\
                       .then_inc(S["o"][k], 1)


LAYER0 = [attention_phase, route_phase, gather_phase, expert_phase, combine_phase]
LAYER1 = [scan_phase, router_phase, slots_phase, moe_phase, output_phase]


def build(nc, d, out, phases=99):
    with ExitStack() as ctx:
        def sb(n, s, dt=F32):
            return ctx.enter_context(nc.sbuf_tensor(n, s, dt))

        m = Mem()
        m.out = out
        m.const = sb("const", [P, C_END])
        m.x_res = sb("x_res", [P, TILES, D])
        m.silu_c = sb("silu_c", [P, 2, B])
        m.modT = sb("modT", [P, 2, 4, B])
        m.gates = sb("gates", [B, 2, 3 * D])
        m.eps = sb("eps", [P, 3])
        m.ones16 = sb("ones16", [B, P])
        m.ones128 = sb("ones128", [P, P])
        m.wq, m.wk, m.wv, m.wo = (sb(n, [P, D])[:] for n in ("wq", "wk", "wv", "wo"))
        m.gate0 = sb("gate0", [P, E0])[:]
        m.gn = sb("gn", [P, 2])[:]
        m.w_in = sb("w_in", [P, 2 * DI + 104])[:]
        m.bcol = sb("bcol", [P, NH, 7 + NST])[:]
        m.gate1 = sb("gate1", [P, E1 + 1])[:]
        m.w_outT = sb("w_outT", [P, NH, D])[:]
        m.wdt = sb("wdt", [P, DI])
        ps = [ctx.enter_context(nc.psum_tensor(f"bank{i}", [P, 512], F32)) for i in range(8)]
        setup_phase(nc, d, m, ps)
        with ExitStack() as layer:
            def sb(n, s, dt=F32):
                return layer.enter_context(nc.sbuf_tensor(n, s, dt))

            m.probs = sb("probs", [P, NCH, B * E0])
            m.places = sb("places", [P, NCH, B * E0])
            m.xn2 = sb("xn2", [P, TILES, D])
            m.xin = sb("xin", [P, E0, B * CAP])
            m.yT = sb("yT", [P, E0, B * CAP])
            for ph in LAYER0[:max(phases - 1, 0)]:
                ph(nc, d, m, ps)
        with ExitStack() as layer:
            def sb(n, s, dt=F32):
                return layer.enter_context(nc.sbuf_tensor(n, s, dt))

            m.w13 = sb("w13", [P, E1 * 2, I1])
            m.w2d = sb("w2d", [IC, E1 * NIC, D])
            m.expert, m.weight = sb("expert", [P, TILES, TOPK]), sb("weight", [P, TILES, TOPK])
            m.etile = sb("etile", [P, MOE_TILES], U32)
            m.from_row, m.to_row = sb("from_row", [P, MOE_TILES], U32), sb("to_row", [P, MOE_TILES], U32)
            m.hf_rows = nc.dram_tensor("hf_rows", (B * L, D), F32).ap()
            m.y_rows = nc.dram_tensor("y_rows", (B * L * TOPK + MOE_TILES * P, D), F32).ap()
            for ph in LAYER1[:max(phases - 6, 0)]:
                ph(nc, d, m, ps)
        if phases < 11:
            s_out = ctx.enter_context(nc.semaphore("stored"))
            with nc.Block() as block:
                @block.sync
                def _(sp):
                    for i in range(4):
                        sp.dma_start(out[4 * i:4 * i + 4].rearrange("b (c t) d -> t (b c) d", t=P),
                                     m.x_res[:, 8 * i:8 * i + 8, :]).then_inc(s_out, 16)
                    sp.wait_ge(s_out, 64)


def lay_out(i):
    f = lambda a: np.ascontiguousarray(np.asarray(a))
    win = f(i["L1_attn_W_in"])
    bc, dt = win[2 * DI:2 * DI + 2 * NST], win[2 * DI + 2 * NST:]
    half = lambda a: f(a).reshape(NH, P, -1).transpose(1, 0, 2)
    return {
        "x": f(i["L0_attn_x"]),
        "const": constants(),
        "cT": f(np.stack([f(i["L0_c"]).T, f(i["L1_c"]).T], 1)),
        "wmod": f(np.stack([f(i["L0_wmod"]), f(i["L1_wmod"])], 1)),
        "lnrow": f(np.broadcast_to(np.stack([f(i["L1_attn_ln_g"]), f(i["L1_attn_ln_b"])])[None], (B, 2, D))),
        "wqT": f(f(i["L0_attn_Wq"]).T), "wkT": f(f(i["L0_attn_Wk"]).T),
        "wvT": f(f(i["L0_attn_Wv"]).T), "woT": f(f(i["L0_attn_Wo"]).T),
        "gate0": f(i["L0_ffn_gate_w"]),
        "gn": f(np.stack([f(i["L0_attn_gn_weight"]), f(i["L0_attn_gn_bias"])], 1)),
        "w1": f(i["L0_ffn_w1"]), "w2": f(i["L0_ffn_w2"]),
        "winT": f(np.concatenate([win[:2 * DI], bc, bc, bc, dt]).T),
        "cols": f(np.concatenate([half(i["L1_attn_conv_w"]), half(i["L1_attn_conv_b"]), half(i["L1_attn_b_dt"]),
                                  half(i["L1_attn_D"]), half(i["L1_attn_A_log"])], 2)),
        "gate1T": f(np.concatenate([f(i["L1_ffn_gate_w"]).T, f(i["L1_ffn_rms_weight"])[:, None]], 1)),
        "woutT": f(f(i["L1_attn_W_out"]).T.reshape(NH, P, D).transpose(1, 0, 2)),
        "wdtT": f(f(i["L1_attn_W_dt"]).T),
        "w13": f(np.stack([f(i["L1_ffn_w1"]).transpose(2, 0, 1), f(i["L1_ffn_w3"]).transpose(2, 0, 1)], 2).reshape(P, E1 * 2, I1)),
        "w2d": f(f(i["L1_ffn_w2"]).transpose(2, 0, 1).reshape(NIC, IC, E1, D).transpose(1, 2, 0, 3).reshape(IC, E1 * NIC, D)),
    }


def kernel(**inputs):
    import concourse.bacc as bacc
    from concourse.bass_utils import run_bass_kernel_spmd

    nc = bacc.Bacc("TRN2", target_bir_lowering=False, num_devices=1)
    arrays = lay_out(inputs)
    d = {n: nc.dram_tensor("in_" + n, a.shape, mybir.dt.from_np(a.dtype), kind="ExternalInput").ap() for n, a in arrays.items()}
    out = nc.dram_tensor("out", (B, L, D), F32, kind="ExternalOutput").ap()
    build(nc, d, out)
    return run_bass_kernel_spmd(nc, [{"in_" + n: a for n, a in arrays.items()}], core_ids=[0]).results[0]["out"]
```

```python
from contextlib import ExitStack

import numpy as np

import concourse.bass as bass
from concourse import mybir

F32 = mybir.dt.float32
BF16 = mybir.dt.bfloat16
U32 = mybir.dt.uint32
ALU = mybir.AluOpType
ACT = mybir.ActivationFunctionType
AX = mybir.AxisListType.X

P = 128
B, L, D = 16, 256, 128
NCH = L // P
PAIRS = B // 2
TILES = B * NCH
HEADS, DH = 8, 16
E0, CAP, H0 = 8, 64, 512
HC0 = H0 // P
DI, NST, KCONV, RDT = 256, 16, 4, 8
NH = DI // P
E1, I1, TOPK = 8, 448, 2
IC, NIC = 112, I1 // 112
LN_EPS, RMS_EPS = 1e-5, 1e-6
SMALL_E = 2.0 ** -6
EXPLN = "natural_log_exp_and_others"

C_DEC, C_INV, C_INVT, C_TRI, C_BLK, C_AVG, C_ID = 0, 256, 512, 640, 768, 896, 1024
C_PAR, C_IOTA, C_IOTA8, C_REP = 1152, 1154, 1218, 1226
C_T72, C_I128, C_VAL, C_PAD, C_END = 1258, 1330, 1458, 1522, 1594


def constants():
    gam = (1.0 - np.exp(np.linspace(np.log(1 / 32), np.log(1 / 512), HEADS)).astype(np.float32)).astype(np.float64)
    p = np.arange(P)
    g = gam[p // DH]
    t = np.arange(L)
    c = np.zeros((P, C_END), np.float32)
    c[:, C_DEC:C_DEC + L] = g[:, None] ** t
    c[:, C_INV:C_INV + L] = g[:, None] ** -t.astype(np.float64)
    c[:, C_INVT:C_INVT + P] = g[None, :] ** -p[:, None].astype(np.float64)
    c[:, C_TRI:C_TRI + P] = p[:, None] <= p[None, :]
    same = p[:, None] // DH == p[None, :] // DH
    c[:, C_BLK:C_BLK + P] = same
    c[:, C_AVG:C_AVG + P] = same / DH
    c[:, C_ID:C_ID + P] = np.eye(P)
    c[:, C_PAR] = (p // DH) % 2 == 0
    c[:, C_PAR + 1] = (p // DH) % 2 == 1
    c[:, C_IOTA:C_IOTA + CAP] = np.arange(1, CAP + 1)
    c[:, C_IOTA8:C_IOTA8 + E1] = np.arange(E1)
    c[:, C_REP:C_REP + 32] = p[:, None] % 32 == np.arange(32)[None, :]
    tiles = np.arange(72)
    c[:, C_T72:C_T72 + 72] = tiles
    c[:, C_I128:C_I128 + P] = p
    rank, tile = np.divmod(np.arange(B * L * TOPK // P), TILES)
    c[:, C_VAL:C_VAL + 64] = 1 + TOPK * (P * tile[None, :] + p[:, None]) + rank[None, :]
    c[:, C_PAD:C_PAD + 72] = B * L * TOPK + P * tiles[None, :] + p[:, None]
    return c


def ticker(eng, sem, per_round=0):
    n = [0]

    def tick(ins):
        ins.then_inc(sem, 1)
        n[0] += 1

    def settle(rnd=0):
        eng.wait_ge(sem, rnd * per_round + n[0])

    def ends():
        assert n[0] == per_round, (sem, n[0], per_round)

    return tick, settle, ends


def pause(eng, passed):
    eng.sem_inc(passed, 1)


def semaphores(nc, ctx, prefix=""):
    taken = []

    def clear():
        nc.clear_and_free_semaphores(taken)
        nc.all_engine_barrier()

    def sem(n):
        taken.append(nc.alloc_semaphore(name=prefix + n))
        return taken[-1]

    ctx.callback(clear)
    return sem


class Mem:
    pass


def setup_phase(nc, d, m, ps):
    with ExitStack() as ctx:
        sem = semaphores(nc, ctx)

        def sb(n, s, dt=F32):
            return ctx.enter_context(nc.sbuf_tensor(n, s, dt))

        cT = sb("cT", [P, 2, B])
        wmod = sb("wmod", [P, 2, 6 * D])
        lnrow = sb("lnrow", [B, 2, D])
        sgn = sb("sgn", [B, 2, 2 * D])
        mag = sb("mag", [B, 2, 2 * D])
        s_c, s_w, s_x, s_sc, s_mod, s_row = (sem("ld_c"), sem("ld_mod"), sem("ld_x"), sem("silu_c"),
                                             sem("mod_ps"), sem("v_own0"))
        block = ctx.enter_context(nc.Block())
        BIG = [(m.x_res[:, 8 * i:8 * i + 8, :],
                d["x"][4 * i:4 * i + 4].rearrange("b (c t) d -> t (b c) d", t=P)) for i in range(4)]
        SMALL = [(m.wq, d["wqT"]), (m.wk, d["wkT"]), (m.wv, d["wvT"]), (m.wo, d["woT"]), (m.gate0, d["gate0"]),
                 (m.gn, d["gn"]), (m.w_in, d["winT"]), (m.bcol, d["cols"]), (m.gate1, d["gate1T"]),
                 (m.w_outT, d["woutT"]), (m.wdt[96:96 + RDT, :], d["wdtT"])]

        @block.sync
        def _(sp):
            sp.dma_start(cT[:], d["cT"]).then_inc(s_c, 16)
            sp.dma_start(lnrow[:], d["lnrow"]).then_inc(s_c, 16)
            sp.dma_start(wmod[:], d["wmod"]).then_inc(s_w, 16)
            sp.dma_start(m.const[:], d["const"]).then_inc(s_w, 16)
            for dst, src in BIG:
                sp.dma_start(dst, src).then_inc(s_x, 16)
            for dst, src in SMALL:
                sp.dma_start(dst if dst is not m.wdt else dst, src).then_inc(s_x, 16)
            sp.wait_ge(s_x, 16 * (len(BIG) + len(SMALL)))

        @block.scalar
        def _(act):
            act.wait_ge(s_c, 32)
            act.activation(m.silu_c[:], cT[:], ACT.Silu).then_inc(s_sc, 1)

        @block.tensor
        def _(pe):
            pe.wait_ge(s_sc, 1)
            pe.wait_ge(s_w, 32)
            for ly in range(2):
                for k, w in enumerate((0, 1, 3, 4)):
                    pe.matmul(ps[ly][:, k * B:(k + 1) * B], wmod[:, ly, w * D:(w + 1) * D], m.silu_c[:, ly, :],
                              start=True, stop=True)
                for k, w in enumerate((2, 5)):
                    mm = pe.matmul(ps[2 + ly][0:B, k * D:(k + 1) * D], m.silu_c[:, ly, :],
                                   wmod[:, ly, w * D:(w + 1) * D], start=True, stop=True)
            mm.then_inc(s_mod, 1)

        @block.vector
        def _(dve):
            tick, settle, _ = ticker(dve, s_row)
            tick(dve.memset(m.eps[:, 0:1], LN_EPS))
            tick(dve.memset(m.eps[:, 1:2], RMS_EPS))
            tick(dve.memset(m.eps[:, 2:3], 1.0 + SMALL_E))
            tick(dve.memset(m.eps[:, 3:4], -SMALL_E))
            tick(dve.memset(m.eps[:, 4:5], -0.5))
            tick(dve.memset(m.ones16[:], 1.0))
            tick(dve.memset(m.ones128[:], 1.0 / D))
            dve.wait_ge(s_mod, 1)
            for ly in range(2):
                for k in range(4):
                    tick(dve.tensor_scalar(m.modT[:, ly, k, :], ps[ly][:, k * B:(k + 1) * B],
                                           float(k % 2), None, ALU.add))
                rows = ps[2 + ly][0:B, 0:2 * D]
                tick(dve.tensor_scalar(sgn[:, ly, :], rows, 0.0, 2.0, ALU.is_ge, ALU.mult))
            settle()
            tick(dve.tensor_scalar(sgn[:], sgn[:], -1.0, None, ALU.add))
            settle()
            for ly in range(2):
                tick(dve.tensor_tensor(mag[:, ly, :], sgn[:, ly, :], ps[2 + ly][0:B, 0:2 * D], ALU.mult))
            settle()
            for ly in range(2):
                tick(dve.scalar_tensor_tensor(m.gates[:, ly, 0:2 * D], mag[:, ly, :], 0.25, sgn[:, ly, :],
                                              ALU.max, ALU.mult))
            settle()
            dve.wait_ge(s_c, 32)
            tick(dve.tensor_tensor(m.gates[:, 1, 2 * D:3 * D], m.gates[:, 1, 0:D], lnrow[:, 1, :], ALU.mult))
            settle()
            tick(dve.tensor_tensor(m.gates[:, 1, 0:D], m.gates[:, 1, 0:D], lnrow[:, 0, :], ALU.mult))
            settle()




def attention_phase(nc, d, m, ps):
    with ExitStack() as ctx:
        sem = semaphores(nc, ctx)

        def sb(n, s, dt=F32):
            return ctx.enter_context(nc.sbuf_tensor(n, s, dt))

        Q = 2 * NCH
        stats, mv = sb("stats", [P, Q, 6]), sb("mv", [P, Q, 2])
        lnv, rstd = sb("lnv", [P, Q]), sb("rstd", [P, Q])
        xn = sb("xn", [P, Q, D])
        hT = sb("hT", [P, 2, L])
        qm = sb("qm", [P, 2, 2, L])
        kd = sb("kd", [P, 2, L])
        kt0 = sb("kt0", [P, 2, D])
        v0 = sb("v0", [P, 2, D])
        vp = sb("vp", [P, 2, Q, D])
        state = sb("state", [P, 2, D])
        prob = sb("prob", [P, 2, 4, 2 * NCH, P])
        gst, gmv = sb("gst", [P, 2, 6]), sb("gmv", [P, 2, 2])
        gin, gm = sb("gin", [P, 2, 2]), sb("gm", [P, 2, 2])
        gvar, glnv, gr = sb("gvar", [P, 2]), sb("glnv", [P, 2]), sb("gr", [P, 2])
        gsc, gbi = sb("gsc", [P, 2]), sb("gbi", [P, 2])
        ynT = sb("ynT", [P, 2, L])
        gsel = sb("gsel", [B, 2, 2 * D])
        gate = sb("gate", [P, 2, 2 * D])
        att = sb("att", [P, Q, D])
        xstats, xmv = sb("xstats", [P, Q, 6]), sb("xmv", [P, Q, 2])
        xlnv, xrstd = sb("xlnv", [P, Q]), sb("xrstd", [P, Q])
        xb = sb("xb", [P, Q, D])
        h2T = sb("h2T", [P, 2, L])
        mx = sb("mx", [P, Q])
        sh = sb("sh", [P, Q, E0])
        ex = sb("ex", [P, Q, E0])
        sm = sb("sm", [P, Q])
        rs = sb("rs", [P, Q])

        names = ("v_head v_tail v_passed a_head a_tail ln_stats ln_rstd xn_ready xn_T h_ready proj_ps qk_ready v_sb "
                 "v_zero state_ps state_sb score_ps score_sb y_ps gn_in gn_ps gn_var gn_rstd gn_aff yn_ready "
                 "out_ps gsel_ready gate_ps gate_sb x_stats x_rstd x_norm x_T h2_ready rt_ps rt_shift rt_exp "
                 "x_kept").split()
        S = {n: sem("a1_" + n) for n in names}
        ident = m.const[:, C_ID:C_ID + P]
        block = ctx.enter_context(nc.Block())
        bT, bY, bK, bQ, bV = ps[0:5]
        bS = (bT, bK, bQ, bV)
        bR, bG, bO = ps[5:8]
        pairs_of = lambda t: t[:, :].rearrange("p (s t) -> p s t", s=2)

        def rounds(eng, body):
            body(0, None, None)
            body(1, 0, None)
            with eng.Fori(0, PAIRS - 2, 1) as r:
                body(r + 2, r + 1, r)
            body(None, PAIRS - 1, PAIRS - 2)
            body(None, None, PAIRS - 1)

        @block.vector
        def _(dve):
            dve.memset(vp[:], 0.0).then_inc(S["v_zero"], 1)

            def body(n, a, b):
                head, settle_head, end_head = ticker(dve, S["v_head"], A1_HEAD)
                tail, settle_tail, end_tail = ticker(dve, S["v_tail"], A1_TAIL)

                def statistics(tick, settle, rnd, st, out):
                    pause(dve, S["v_passed"])
                    for q in range(Q):
                        tick(dve.bn_stats(st[:, q, :], m.x_res[:, rnd * Q + q, :]))
                    settle(rnd)
                    pause(dve, S["v_passed"])
                    for q in range(Q):
                        ins = dve.bn_aggr(out[:, q, :], st[:, q, :])
                        if q < Q - 1:
                            tick(ins)
                    return ins

                def masks(k):
                    tri = m.const[:, C_TRI:C_TRI + P].unsqueeze(1).broadcast_to([P, 4, P])
                    for j in range(4):
                        dve.wait_ge(S["score_ps"], a * 8 + k * 4 + j + 1)
                        dve.tensor_tensor(prob[:, k, j], bS[j][:, :].rearrange("p (a t) -> p a t", a=4), tri,
                                          ALU.mult).then_inc(S["score_sb"], 1)

                if b is not None:
                    dve.wait_ge(S["y_ps"], b + 1)
                    pause(dve, S["v_passed"])
                    for k in range(2):
                        tail(dve.bn_stats(gst[:, k, :], bR[:, k * L:(k + 1) * L]))
                    settle_tail(b)
                    pause(dve, S["v_passed"])
                    for k in range(2):
                        tail(dve.bn_aggr(gmv[:, k, :], gst[:, k, :]))
                    settle_tail(b)
                    tail(dve.tensor_tensor(gin[:, :, 1], gmv[:, :, 0], gmv[:, :, 0], ALU.mult))
                    tail(dve.tensor_copy(gin[:, :, 0], gmv[:, :, 0]))
                    settle_tail(b)
                    dve.tensor_tensor(gin[:, :, 1], gin[:, :, 1], gmv[:, :, 1], ALU.add).then_inc(S["gn_in"], 1)
                if b is not None:
                    for k in range(2):
                        dve.tensor_scalar(gsel[:, k, :], m.gates[:, 0, 0:2 * D],
                                          m.const[0:B, bass.ds(C_ID + 2 * b + k, 1)], None,
                                          ALU.mult).then_inc(S["gsel_ready"], 1)
                    dve.wait_ge(S["gn_ps"], b + 1)
                    tail(dve.tensor_copy(gm[:], bO[:, 0:4].rearrange("p (s k) -> p s k", s=2)))
                    settle_tail(b)
                    tail(dve.tensor_tensor(gvar[:], gm[:, :, 0], gm[:, :, 0], ALU.mult))
                    settle_tail(b)
                    tail(dve.tensor_tensor(gvar[:], gm[:, :, 1], gvar[:], ALU.subtract))
                    settle_tail(b)
                    dve.tensor_scalar(gvar[:], gvar[:], 0.0, None, ALU.max).then_inc(S["gn_var"], 1)
                    dve.wait_ge(S["gn_rstd"], b + 1)
                    tail(dve.tensor_scalar(gsc[:], gr[:], m.gn[:, 0:1], None, ALU.mult))
                    settle_tail(b)
                    tail(dve.tensor_tensor(gbi[:], gm[:, :, 0], gsc[:], ALU.mult))
                    settle_tail(b)
                    dve.tensor_scalar(gbi[:], gbi[:], -1.0, m.gn[:, 1:2], ALU.mult, ALU.add).then_inc(S["gn_aff"], 1)
                if a is not None:
                    dve.wait_ge(S["proj_ps"], a + 1)
                    dec = m.const[:, C_DEC:C_DEC + L].unsqueeze(1).broadcast_to([P, 2, L])
                    inv = m.const[:, C_INV:C_INV + L].unsqueeze(1).broadcast_to([P, 2, L])
                    invt = m.const[:, C_INVT:C_INVT + D].unsqueeze(1).broadcast_to([P, 2, D])
                    dve.tensor_tensor(kt0[:], bY[:, 0:2 * D].rearrange("p (s d) -> p s d", s=2), invt,
                                      ALU.mult).then_inc(S["qk_ready"], 1)
                    dve.tensor_tensor(kd[:], pairs_of(bK), inv, ALU.mult).then_inc(S["qk_ready"], 1)
                    for k in range(2):
                        dve.scalar_tensor_tensor(qm[:, k], pairs_of(bQ), m.const[:, C_PAR + k:C_PAR + k + 1], dec,
                                                 ALU.mult, ALU.mult).then_inc(S["qk_ready"], 1)
                    dve.wait_ge(S["state_ps"], a + 1)
                    blk = m.const[:, C_BLK:C_BLK + D].unsqueeze(1).broadcast_to([P, 2, D])
                    dve.tensor_tensor(state[:], bY[:, 2 * D:4 * D].rearrange("p (s d) -> p s d", s=2), blk,
                                      ALU.mult).then_inc(S["state_sb"], 1)
                    masks(0)
                if b is not None:
                    dve.wait_ge(S["out_ps"], b + 1)
                    dve.wait_ge(S["gate_sb"], b + 1)
                    for k in range(2):
                        tail(dve.tensor_tensor(att[:, 2 * k:2 * k + 2, :],
                                               bO[:, k * L:(k + 1) * L].rearrange("p (c d) -> p c d", c=2),
                                               gate[:, k, 0:D].unsqueeze(1).broadcast_to([P, NCH, D]), ALU.mult))
                    settle_tail(b)
                    tail(dve.tensor_tensor(m.x_res[:, bass.ds(b * Q, Q), :], att[:], m.x_res[:, bass.ds(b * Q, Q), :],
                                           ALU.add))
                    settle_tail(b)
                    statistics(tail, settle_tail, b, xstats, xmv).then_inc(S["x_stats"], 1)
                if a is not None:
                    masks(1)
                if b is not None:
                    dve.wait_ge(S["x_rstd"], b + 1)
                    dve.wait_ge(S["x_stats"], b + 1)
                    for q in range(Q):
                        dve.tensor_scalar(xb[:, q, :], m.x_res[:, b * Q + q, :], xmv[:, q, 0:1],
                                          xrstd[:, q:q + 1], ALU.subtract, ALU.mult).then_inc(S["x_norm"], 1)
                if n is not None:
                    statistics(head, settle_head, n, stats, mv).then_inc(S["ln_stats"], 1)
                    if a is not None:
                        dve.wait_ge(S["xn_T"], n)
                    dve.wait_ge(S["ln_rstd"], n + 1)
                    dve.wait_ge(S["ln_stats"], n + 1)
                    for q in range(Q):
                        dve.tensor_scalar(xn[:, q, :], m.x_res[:, n * Q + q, :], mv[:, q, 0:1], rstd[:, q:q + 1],
                                          ALU.subtract, ALU.mult).then_inc(S["xn_ready"], 1)
                    end_head()
                if b is not None:
                    dve.wait_ge(S["rt_ps"], b + 1)
                    lg = bG[:, 0:Q * E0].rearrange("p (q e) -> p q e", q=Q)
                    tail(dve.tensor_reduce(mx[:], lg, AX, ALU.max))
                    settle_tail(b)
                    dve.tensor_tensor(sh[:], lg, mx[:].unsqueeze(2).broadcast_to([P, Q, E0]),
                                      ALU.subtract).then_inc(S["rt_shift"], 1)
                    dve.wait_ge(S["rt_exp"], b + 1)
                    tail(dve.tensor_reduce(sm[:], ex[:], AX, ALU.add))
                    settle_tail(b)
                    tail(dve.reciprocal(rs[:], sm[:]))
                    settle_tail(b)
                    for q in range(Q):
                        tail(dve.tensor_scalar(m.probs[:, q % NCH, bass.ds(b * 2 * E0 + (q // NCH) * E0, E0)],
                                               ex[:, q, :], rs[:, q:q + 1], None, ALU.mult))
                    settle_tail(b)
                    dve.wait_ge(S["x_kept"], b + 1)
                    end_tail()

            rounds(dve, body)

        @block.gpsimd
        def _(pool):
            def body(n, a, b):
                if b is not None:
                    pool.wait_ge(S["x_norm"], (b + 1) * Q)
                    pool.tensor_copy(m.xn2[:, bass.ds(b * Q, Q), :], xb[:]).then_inc(S["x_kept"], 1)

            rounds(pool, body)
            pool.wait_ge(S["x_kept"], PAIRS)

        @block.scalar
        def _(act):
            act.preload_act_table_set(EXPLN)
            act.wait_ge(S["v_zero"], 1)

            def body(n, a, b):
                head, settle_head, _ = ticker(act, S["a_head"], 1)
                tail, settle_tail, end_tail = ticker(act, S["a_tail"], 2)

                def rsqrt(tick, settle, rnd, out, tmp, var):
                    tick(act.activation(tmp, var, ACT.Ln, bias=m.eps[:, 0:1]))
                    settle(rnd)
                    return act.activation(out, tmp, ACT.Exp, scale=-0.5)

                if a is not None:
                    act.wait_ge(S["xn_T"], a + 1)
                    for k in range(2):
                        act.activation(hT[:, k, :], bT[:, k * L:(k + 1) * L], ACT.Identity,
                                       bias=m.modT[:, 0, 0, bass.ds(2 * a + k, 1)],
                                       scale=m.modT[:, 0, 1, bass.ds(2 * a + k, 1)]).then_inc(S["h_ready"], 1)
                if b is not None:
                    act.wait_ge(S["gate_ps"], b + 1)
                    act.activation(gate[:], bG[:, :].rearrange("p (s d) -> p s d", s=2),
                                   ACT.Copy).then_inc(S["gate_sb"], 1)
                if b is not None:
                    act.wait_ge(S["gn_var"], b + 1)
                    rsqrt(tail, settle_tail, b, gr[:], glnv[:], gvar[:]).then_inc(S["gn_rstd"], 1)
                    act.wait_ge(S["gn_aff"], b + 1)
                    for k in range(2):
                        act.activation(ynT[:, k, :], bR[:, k * L:(k + 1) * L], ACT.Identity, bias=gbi[:, k:k + 1],
                                       scale=gsc[:, k:k + 1]).then_inc(S["yn_ready"], 1)
                if a is not None:
                    act.wait_ge(S["proj_ps"], a + 1)
                    act.activation(v0[:], bV[:, :].rearrange("p (s c d) -> p s c d", s=2, c=NCH)[:, :, 0, :],
                                   ACT.Copy).then_inc(S["v_sb"], 1)
                    heads = lambda t: t.rearrange("p (g a d) -> p g a d", a=2, d=DH)
                    for k in range(2):
                        act.activation(heads(vp[:, k].rearrange("p q d -> p (q d)"))[:, :, k, :],
                                       heads(bV[:, :])[:, :, k, :], ACT.Copy).then_inc(S["v_sb"], 1)
                if b is not None:
                    act.wait_ge(S["x_stats"], b + 1)
                    rsqrt(tail, settle_tail, b, xrstd[:], xlnv[:], xmv[:, :, 1]).then_inc(S["x_rstd"], 1)
                    act.wait_ge(S["x_T"], b + 1)
                    for k in range(2):
                        act.activation(h2T[:, k, :], bG[:, k * L:(k + 1) * L], ACT.Identity,
                                       bias=m.modT[:, 0, 2, bass.ds(2 * b + k, 1)],
                                       scale=m.modT[:, 0, 3, bass.ds(2 * b + k, 1)]).then_inc(S["h2_ready"], 1)
                if n is not None:
                    act.wait_ge(S["ln_stats"], n + 1)
                    rsqrt(head, settle_head, n, rstd[:], lnv[:], mv[:, :, 1]).then_inc(S["ln_rstd"], 1)
                if b is not None:
                    act.wait_ge(S["rt_shift"], b + 1)
                    act.activation(ex[:], sh[:], ACT.Exp).then_inc(S["rt_exp"], 1)
                    end_tail()

            rounds(act, body)

        @block.tensor
        def _(pe):
            flat = lambda t: t.rearrange("p s t -> p (s t)")

            def body(n, a, b):
                def scores(k):
                    for j in range(4):
                        if k == 1:
                            pe.wait_ge(S["score_sb"], a * 8 + j + 1)
                        for c in range(NCH):
                            rows = slice(32 * j, 32 * j + 32)
                            mm = pe.matmul(bS[j][:, c * 2 * P:(c + 1) * 2 * P].rearrange("p (a t) -> p a t", a=2),
                                           kd[rows, k, c * P:(c + 1) * P], qm[rows, :, k, c * P:(c + 1) * P],
                                           start=True, stop=True)
                        mm.then_inc(S["score_ps"], 1)

                def result(k):
                    pe.wait_ge(S["score_sb"], a * 8 + 4 * k + 4)
                    for par in range(2):
                        pe.matmul(bR[:, k * L + P:(k + 1) * L], state[:, k, :], qm[:, par, k, P:L],
                                  start=(par == 0), stop=False, skip_group_check=True)
                    for c in (1, 0):
                        for j in range(4):
                            for par in range(2):
                                mm = pe.matmul(bR[32 * j:32 * j + 32, k * L + c * P:k * L + (c + 1) * P],
                                               vp[:, par, k * NCH + c, 32 * j:32 * j + 32],
                                               prob[:, k, j, 2 * c + par, :], start=(c == 0 and par == 0),
                                               stop=(par == 1), skip_group_check=True)
                    if k == 1:
                        mm.then_inc(S["y_ps"], 1)

                if a is not None:
                    pe.wait_ge(S["xn_ready"], (a + 1) * Q)
                    for q in range(Q):
                        mm = pe.transpose(bT[:, q * P:(q + 1) * P], xn[:, q, :], ident)
                    mm.then_inc(S["xn_T"], 1)
                if b is not None:
                    pe.wait_ge(S["gn_in"], b + 1)
                    pe.matmul(bO[:, 0:4], m.const[:, C_AVG:C_AVG + P], gin[:].rearrange("p s k -> p (s k)"),
                              start=True, stop=True).then_inc(S["gn_ps"], 1)
                    pe.wait_ge(S["gsel_ready"], (b + 1) * 2)
                    pe.matmul(bG[:, :], m.ones16[:], gsel[:].rearrange("p s d -> p (s d)"), start=True,
                              stop=True).then_inc(S["gate_ps"], 1)
                if a is not None:
                    pe.wait_ge(S["h_ready"], (a + 1) * 2)
                    for k in range(2):
                        pe.matmul(bY[:, k * D:(k + 1) * D], hT[:, k, 0:P], m.wk, start=True, stop=True)
                    hf = flat(hT[:])
                    pe.matmul(bK[:, :], m.wk, hf, start=True, stop=True)
                    pe.matmul(bQ[:, :], m.wq, hf, start=True, stop=True)
                    for q in range(Q):
                        mm = pe.matmul(bV[:, q * D:(q + 1) * D], hf[:, q * P:(q + 1) * P], m.wv, start=True, stop=True)
                    mm.then_inc(S["proj_ps"], 1)
                if b is not None:
                    pe.wait_ge(S["yn_ready"], (b + 1) * 2)
                    yf = flat(ynT[:])
                    for q in range(Q):
                        mm = pe.matmul(bO[:, q * D:(q + 1) * D], yf[:, q * P:(q + 1) * P], m.wo, start=True, stop=True)
                    mm.then_inc(S["out_ps"], 1)
                if a is not None:
                    pe.wait_ge(S["v_sb"], 3 * a + 3)
                    pe.wait_ge(S["qk_ready"], a * 4 + 1)
                    for k in range(2):
                        mm = pe.matmul(bY[:, (2 + k) * D:(3 + k) * D], kt0[:, k, :], v0[:, k, :],
                                       start=True, stop=True)
                    mm.then_inc(S["state_ps"], 1)
                    pe.wait_ge(S["qk_ready"], (a + 1) * 4)
                    scores(0)
                    scores(1)
                if b is not None:
                    pe.wait_ge(S["x_norm"], (b + 1) * Q)
                    pe.wait_ge(S["gate_sb"], b + 1)
                    for q in range(Q):
                        mm = pe.transpose(bG[:, q * P:(q + 1) * P], xb[:, q, :], ident)
                    mm.then_inc(S["x_T"], 1)
                if a is not None:
                    pe.wait_ge(S["state_sb"], a + 1)
                    result(0)
                if b is not None:
                    pe.wait_ge(S["h2_ready"], (b + 1) * 2)
                    hf = flat(h2T[:])
                    for q in range(Q):
                        mm = pe.matmul(bG[:, q * E0:(q + 1) * E0], hf[:, q * P:(q + 1) * P], m.gate0, start=True,
                                       stop=True)
                    mm.then_inc(S["rt_ps"], 1)
                if a is not None:
                    result(1)

            rounds(pe, body)


A1_HEAD, A1_TAIL = 7, 28


def route_phase(nc, d, m, ps):
    with ExitStack() as ctx:
        sem = semaphores(nc, ctx)

        def sb(n, s, dt=F32):
            return ctx.enter_context(nc.sbuf_tensor(n, s, dt))

        left = sb("left", [P, L])
        top8 = sb("top8", [P, 8])
        zeros = sb("zeros", [P, L])
        taken = sb("taken", [P, L])
        place = sb("place", [P, L])
        listed = sb("listed", [P, L])
        s_in, s_own, s_out, s_back = sem("rt_in"), sem("rt_own"), sem("rt_out"), sem("rt_back")
        ident = m.const[:, C_ID:C_ID + P]
        block = ctx.enter_context(nc.Block())

        @block.tensor
        def _(pe):
            for c in range(NCH):
                mm = pe.transpose(ps[0][:, c * P:(c + 1) * P], m.probs[:, c, :], ident)
            mm.then_inc(s_in, 1)
            pe.wait_ge(s_out, 1)
            for c in range(NCH):
                mm = pe.transpose(ps[1][:, c * P:(c + 1) * P], listed[:, c * P:(c + 1) * P], ident)
            mm.then_inc(s_back, 1)

        @block.vector
        def _(dve):
            tick, settle, _ = ticker(dve, s_own)
            tick(dve.memset(zeros[:], 0.0))
            dve.wait_ge(s_in, 1)
            tick(dve.tensor_copy(left[:], ps[0][:, 0:L]))
            settle()
            for _ in range(CAP // 8):
                tick(dve.max(top8[:], left[:]))
                settle()
                tick(dve.match_replace(left[:], top8[:], left[:], -1.0))
                settle()
            tick(dve.tensor_scalar(taken[:], left[:], 0.0, None, ALU.is_lt))
            settle()
            tick(dve.tensor_tensor_scan(place[:], taken[:], zeros[:], 0.0, ALU.add, ALU.add))
            settle()
            dve.tensor_tensor(listed[:], place[:], taken[:], ALU.mult).then_inc(s_out, 1)
            dve.wait_ge(s_back, 1)
            tick(dve.tensor_copy(m.places[:], ps[1][:, 0:L].rearrange("p (c n) -> p c n", c=NCH)))
            settle()


def one_hot(dve, out, places, iota, c, first):
    return dve.tensor_tensor(out, places[:, c, bass.ds(first, E0)].unsqueeze(2).broadcast_to([P, E0, CAP]),
                             iota.unsqueeze(1).broadcast_to([P, E0, CAP]), ALU.is_equal)


def gather_phase(nc, d, m, ps):
    with ExitStack() as ctx:
        new = semaphores(nc, ctx, "")

        def sem(n):
            return [new(f"{n}{k}") for k in range(2)]

        def sb(n, s, dt=F32):
            return ctx.enter_context(nc.sbuf_tensor(n, s, dt))

        pick = sb("pick", [P, 2, NCH, E0, CAP])
        xst = sb("xst", [P, 2, NCH, D])
        picked, staged, product, taken = sem("g_picked"), sem("g_staged"), sem("g_product"), sem("g_taken")
        iota = m.const[:, C_IOTA:C_IOTA + CAP]
        block = ctx.enter_context(nc.Block())

        @block.vector
        def _(dve):
            with dve.Fori(0, PAIRS, 1) as r:
                for k in range(2):
                    dve.wait_ge(product[k], r + 1)
                    for c in range(NCH):
                        one_hot(dve, pick[:, k, c], m.places, iota, c, r * 2 * E0 + k * E0).then_inc(picked[k], 1)

        @block.gpsimd
        def _(pool):
            for k in range(2):
                pool.sem_inc(product[k], 1)
                pool.sem_inc(taken[k], 1)
            with pool.Fori(0, PAIRS, 1) as r:
                for k in range(2):
                    pool.wait_ge(product[k], r + 1)
                    pool.tensor_copy(xst[:, k], m.xn2[:, bass.ds(r * 2 * NCH + k * NCH, NCH), :]).then_inc(staged[k], 1)

        @block.tensor
        def _(pe):
            with pe.Fori(0, PAIRS, 1) as r:
                for k in range(2):
                    pe.wait_ge(staged[k], r + 1)
                    pe.wait_ge(taken[k], r + 1)
                    for c in range(NCH):
                        pe.wait_ge(picked[k], 2 * r + c + 1)
                        mm = pe.matmul(ps[k][:, :], xst[:, k, c, :], pick[:, k, c].rearrange("p e s -> p (e s)"),
                                       start=(c == 0), stop=(c == NCH - 1))
                    mm.then_inc(product[k], 1)

        @block.scalar
        def _(act):
            with act.Fori(0, PAIRS, 1) as r:
                for k in range(2):
                    act.wait_ge(product[k], r + 2)
                    seq = bass.ds(2 * r + k, 1)
                    act.activation(m.xin[:, :, bass.ds(2 * r * CAP + k * CAP, CAP)],
                                   ps[k][:, :].rearrange("p (e s) -> p e s", e=E0), ACT.Identity,
                                   bias=m.modT[:, 0, 2, seq], scale=m.modT[:, 0, 3, seq]).then_inc(taken[k], 1)


def expert_phase(nc, d, m, ps):
    N = B * CAP // 2
    with ExitStack() as ctx:
        sem = semaphores(nc, ctx)

        def sb(n, s, dt=F32):
            return ctx.enter_context(nc.sbuf_tensor(n, s, dt))

        w1 = sb("w1", [P, 2, H0])
        w2 = sb("w2", [P, 2, HC0, D])
        g = sb("g", [P, 2, HC0, N])
        loaded = [sem(f"e_loaded{k}") for k in range(2)]
        hidden = [sem(f"e_hidden{h}") for h in range(HC0)]
        gelued = [sem(f"e_gelued{h}") for h in range(HC0)]
        result = [[sem(f"e_result{k}{a}") for a in range(2)] for k in range(2)]
        kept = [sem(f"e_kept{a}") for a in range(2)]
        block = ctx.enter_context(nc.Block())

        @block.gpsimd
        def _(pool):
            for free in (*result[0], *result[1], *gelued, *kept):
                pool.sem_inc(free, 1)

        @block.sync
        def _(sp):
            with sp.Fori(0, E0 // 2, 1) as r:
                for k in range(2):
                    sp.wait_ge(result[k][1], r + 1)
                    sp.dma_start(w1[:, k, :], d["w1"][bass.ds(2 * r + k, 1), :, :].rearrange(
                        "e p h -> (e p) h")).then_inc(loaded[k], 16)
                    sp.dma_start(w2[:, k], d["w2"][bass.ds(2 * r + k, 1), :, :].rearrange(
                        "e (h p) c -> p (e h) c", p=P)).then_inc(loaded[k], 16)

        @block.tensor
        def _(pe):
            with pe.Fori(0, E0 // 2, 1) as r:
                for k in range(2):
                    pe.wait_ge(loaded[k], 32 * (r + 1))
                    for a in range(2):
                        for h in range(HC0):
                            pe.wait_ge(gelued[h], 4 * r + 2 * k + a + 1)
                            pe.matmul(ps[h][:, :], w1[:, k, h * P:(h + 1) * P],
                                      m.xin[:, 2 * r + k, a * N:(a + 1) * N], start=True,
                                      stop=True).then_inc(hidden[h], 1)
                    for a in range(2):
                        pe.wait_ge(kept[a], 2 * r + k + 1)
                        for h in range(HC0):
                            pe.wait_ge(gelued[h], 4 * r + 2 * k + a + 2)
                            mm = pe.matmul(ps[4 + a][:, :], w2[:, k, h, :], g[:, a, h, :], start=(h == 0),
                                           stop=(h == HC0 - 1))
                        mm.then_inc(result[k][a], 1)

        @block.scalar
        def _(act):
            act.preload_act_table_set("gelu_and_others")
            with act.Fori(0, E0 // 2, 1) as r:
                for k in range(2):
                    for a in range(2):
                        act.wait_ge(result[1 - k][a], r + k + 1)
                        for h in range(HC0):
                            act.wait_ge(hidden[h], 4 * r + 2 * k + a + 1)
                            act.activation(g[:, a, h, :], ps[h][:, :], ACT.Gelu).then_inc(gelued[h], 1)

        @block.vector
        def _(dve):
            with dve.Fori(0, E0 // 2, 1) as r:
                for k in range(2):
                    for a in range(2):
                        dve.wait_ge(result[k][a], r + 2)
                        dve.tensor_copy(m.yT[:, 2 * r + k, a * N:(a + 1) * N], ps[4 + a][:, :]).then_inc(kept[a], 1)


def combine_phase(nc, d, m, ps):
    with ExitStack() as ctx:
        sem = semaphores(nc, ctx)

        def sb(n, s, dt=F32):
            return ctx.enter_context(nc.sbuf_tensor(n, s, dt))

        hot = sb("hot", [P, 2, NCH, E0, CAP])
        pick = sb("pickw", [P, 2, NCH, E0, CAP])
        pickT = sb("pickT", [P, 2, E0 // 2, L])
        yst = sb("yst", [P, 2, E0, CAP])
        ysl = sb("ysl", [P, 2, E0 // 2, D])
        gsel = sb("gsel2", [B, 2, D])
        gate = sb("gate2", [P, 2, D])
        out = sb("moe0", [P, 2, NCH, D])
        names = "hot pick yst pickT_ps pickT y_ps ysl prod".split()
        S = {n: [sem(f"c_{n}{k}") for k in range(2)] for n in names}
        s_gsel, s_gate_ps, s_gate, s_out, s_sum = (sem("c_" + n) for n in ("gsel", "gate_ps", "gate", "out_ps", "sum"))
        ident = m.const[:, C_ID:C_ID + P]
        iota = m.const[:, C_IOTA:C_IOTA + CAP]
        block = ctx.enter_context(nc.Block())

        def rounds(eng, body):
            body(0, None)
            with eng.Fori(0, PAIRS - 1, 1) as r:
                body(r + 1, r)
            body(None, PAIRS - 1)

        @block.gpsimd
        def _(pool):
            for k in range(2):
                pool.sem_inc(S["prod"][k], 1)

            def body(a, b):
                if a is None:
                    return
                for k in range(2):
                    if b is not None:
                        pool.wait_ge(S["y_ps"][k], a)
                    pool.tensor_copy(yst[:, k], m.yT[:, :, bass.ds(2 * a * CAP + k * CAP, CAP)])\
                        .then_inc(S["yst"][k], 1)

            rounds(pool, body)

        @block.vector
        def _(dve):
            def lists(a, k):
                for c in range(NCH):
                    one_hot(dve, hot[:, k, c], m.places, iota, c, a * 2 * E0 + k * E0).then_inc(S["hot"][k], 1)
                for c in range(NCH):
                    dve.wait_ge(S["hot"][k], 2 * a + c + 1)
                    dve.tensor_tensor(pick[:, k, c], hot[:, k, c],
                                      m.probs[:, c, bass.ds(a * 2 * E0 + k * E0, E0)].unsqueeze(2).broadcast_to(
                                          [P, E0, CAP]), ALU.mult).then_inc(S["pick"][k], 1)

            def body(a, b):
                if b is not None:
                    for s in range(2):
                        dve.tensor_scalar(gsel[:, s, :], m.gates[:, 0, D:2 * D],
                                          m.const[0:B, bass.ds(C_ID + 2 * b + s, 1)], None,
                                          ALU.mult).then_inc(s_gsel, 1)
                if a is not None:
                    for k in range(2):
                        if b is not None:
                            dve.wait_ge(S["pickT_ps"][k], a)
                        lists(a, k)
                if b is not None:
                    dve.wait_ge(s_gate, b + 1)
                    dve.wait_ge(s_out, b + 1)
                    for k in range(2):
                        dve.tensor_tensor(out[:, k], ps[6][:, k * L:(k + 1) * L].rearrange("p (c d) -> p c d", c=NCH),
                                          gate[:, k, :].unsqueeze(1).broadcast_to([P, NCH, D]),
                                          ALU.mult).then_inc(S["prod"][k], 1)
                    for k in range(2):
                        dve.wait_ge(S["prod"][k], b + 2)
                        xs = m.x_res[:, bass.ds(b * 2 * NCH + k * NCH, NCH), :]
                        dve.tensor_tensor(xs, out[:, k], xs, ALU.add).then_inc(s_sum, 1)

            rounds(dve, body)

        @block.tensor
        def _(pe):
            def body(a, b):
                if b is not None:
                    pe.wait_ge(s_gsel, 2 * b + 2)
                    pe.matmul(ps[7][:, 0:2 * D], m.ones16[:], gsel[:].rearrange("p s d -> p (s d)"), start=True,
                              stop=True).then_inc(s_gate_ps, 1)
                for k in range(2):
                    if b is not None:
                        pe.wait_ge(S["ysl"][k], b + 1)
                        pe.wait_ge(S["pickT"][k], 2 * b + 2)
                        pe.wait_ge(S["prod"][k], b + 1)
                        for c in range(NCH):
                            for pair in range(E0 // 2):
                                mm = pe.matmul(ps[6][:, (k * NCH + c) * D:(k * NCH + c + 1) * D],
                                               pickT[:, k, pair, c * P:(c + 1) * P], ysl[:, k, pair, :],
                                               start=(pair == 0), stop=(pair == E0 // 2 - 1))
                        if k == 1:
                            mm.then_inc(s_out, 1)
                    if a is not None:
                        for c in range(NCH):
                            pe.wait_ge(S["pick"][k], 2 * a + c + 1)
                            for q in range(E0 // 2):
                                mm = pe.transpose(ps[2 * k + q // 2][:, (q % 2) * L + c * P:(q % 2) * L + (c + 1) * P],
                                                  pick[:, k, c, 2 * q:2 * q + 2, :].rearrange("p e s -> p (e s)"),
                                                  ident)
                        mm.then_inc(S["pickT_ps"][k], 1)
                if a is not None:
                    for k in range(2):
                        pe.wait_ge(S["yst"][k], a + 1)
                        for q in range(E0 // 2):
                            mm = pe.transpose(ps[4 + k][:, q * P:(q + 1) * P],
                                              yst[:, k, 2 * q:2 * q + 2, :].rearrange("p e s -> p (e s)"), ident)
                        mm.then_inc(S["y_ps"][k], 1)

            rounds(pe, body)

        @block.scalar
        def _(act):
            def body(a, b):
                if b is not None:
                    act.wait_ge(s_gate_ps, b + 1)
                    act.activation(gate[:], ps[7][:, 0:2 * D].rearrange("p (s d) -> p s d", s=2),
                                   ACT.Copy).then_inc(s_gate, 1)
                if a is not None:
                    for k in range(2):
                        act.wait_ge(S["pickT_ps"][k], a + 1)
                        for q in range(2):
                            act.activation(pickT[:, k, 2 * q:2 * q + 2, :],
                                           ps[2 * k + q][:, :].rearrange("p (a t) -> p a t", a=2),
                                           ACT.Copy).then_inc(S["pickT"][k], 1)
                    for k in range(2):
                        act.wait_ge(S["y_ps"][k], a + 1)
                        act.activation(ysl[:, k], ps[4 + k][:, :].rearrange("p (a d) -> p a d", d=D), ACT.Copy)\
                           .then_inc(S["ysl"][k], 1)

            rounds(act, body)


SCAN_J = NST // 2
BACK = KCONV - 1
RING = 4


def scan_phase(nc, d, m, ps):
    with ExitStack() as ctx:
        sem = semaphores(nc, ctx, "s_")

        def sb(n, s, dt=F32):
            return ctx.enter_context(nc.sbuf_tensor("s_" + n, s, dt))

        stats, mv = sb("stats", [P, NCH, 6]), sb("mv", [P, NCH, 2])
        lnv, rstd = sb("lnv", [P, NCH]), sb("rstd", [P, NCH])
        ostats, omv = sb("ostats", [P, NCH, 6]), sb("omv", [P, NCH, 2])
        olnv, orstd = sb("olnv", [P, NCH]), sb("orstd", [P, NCH])
        xn = sb("xn", [P, NCH, D])
        hT = sb("hT", [P, 2, BACK + L])
        wc = sb("wc", [P, KCONV, DI])
        acc = sb("acc", [P, NH, L])
        u = sb("u", [P, 2, NH, L])
        z = sb("z", [P, 2, NH, L])
        dlow = sb("dlow", [P, L])
        pos = sb("pos", [P, NH, L])
        soft, e, over, cub = (sb(n, [P, NH, L]) for n in ("soft", "e", "over", "cub"))
        esq, sum1, sum2 = (sb(n, [P, NH, L]) for n in ("esq", "sum1", "sum2"))
        dt = sb("dt", [P, 2, NH, L])
        dtu = sb("dtu", [P, 2, NH, L])
        bc = sb("bc", [3 * 32, 2, L], BF16)
        bcr = sb("bcr", [3 * 32, L])
        r1 = sb("r1", [3 * 32, L])
        mid = sb("mid", [3 * 32, L], BF16)
        spread = sb("spread", [3 * 32, 32, P], BF16)
        aneg = sb("aneg", [P, NH, NST])
        dA = sb("dA", [P, RING, NH, 2, L])
        dbu = sb("dbu", [P, 2, NH, 2, L])
        hs = sb("hs", [P, 2, NH, 2, L])
        hc = sb("hc", [P, 2, NH, 2, L])
        dskip = sb("dskip", [P, NH, P])
        yz = sb("yz", [P, NH, L])
        gsel, gate = sb("gsel", [B, 2, D]), sb("gate", [P, 2, D])
        oh, og = sb("oh", [P, NCH, D]), sb("og", [P, NCH, D])
        names = ("v_passed p_passed p_own v_pre v_prep init a_exp "
                 "B_ps C_ps dA_ready dbu_done scanned hc_ready y_part "
                 "w_turned w_scaled w_back sums e_ready e_parts over st rs xn xT h xs_ps bc_ps z_ps conv dlow "
                 "u_ready z_ready dt_ps pos abs "
                 "ln soft dt_ready dtu_ready bcr bc_parts oln gsel gate_ps gate "
                 "weights yz out_ps ostats ost ors o_read og done").split()
        S = {n: sem(n) for n in names}
        ident = m.const[:, C_ID:C_ID + P]
        bB, bC, bY, bX, bZ, bT = ps[0:2], ps[2:4], ps[4], ps[5], ps[6], ps[7]
        col = lambda h, i: m.bcol[:, h, i:i + 1]
        CONV_B, DT_B, DSKIP, ALOG = 4, 5, 6, 7
        block = ctx.enter_context(nc.Block())

        def sequences(eng, body, last):
            body(0, 0, True, True)
            with eng.Fori(0, PAIRS - 1, 1) as r:
                body(2 * r + 1, 1, False, True)
                body(2 * r + 2, 0, False, True)
            body(B - 1, 1, False, False)
            last(B - 1, 1)

        @block.vector
        def _(dve):
            tick0, settle0, _ = ticker(dve, S["v_pre"])
            tick0(dve.tensor_copy(spread[:], m.const[0:96, C_REP:C_REP + 32].unsqueeze(2).broadcast_to([96, 32, P])))
            tick0(dve.memset(dA[:, :, :, :, 0:1], 0.0))
            for h in range(NH):
                tick0(dve.tensor_scalar(dskip[:, h, :], ident, col(h, DSKIP), None, ALU.mult))
            tick0(dve.memset(hT[:, :, 0:BACK], 0.0))
            dve.wait_ge(S["w_turned"], 1)
            for h in range(NH):
                for tap in range(KCONV):
                    dve.tensor_scalar(hc[:, 0, h, tap // 2, (tap % 2) * P:(tap % 2 + 1) * P],
                                      bX[:, h * P:(h + 1) * P], col(h, tap), None, ALU.mult)\
                        .then_inc(S["w_scaled"], 1)
            dve.wait_ge(S["w_back"], 1)
            for h in range(NH):
                tick0(dve.tensor_copy(wc[:, :, h * P:(h + 1) * P],
                                      bC[h][:, :].rearrange("p (s c) -> p s c", s=KCONV)))
            dve.wait_ge(S["a_exp"], 1)
            tick0(dve.tensor_scalar(aneg[:], aneg[:], -1.0, None, ALU.mult))
            settle0()
            dve.sem_inc(S["init"], 1)

            def prepare(step, b, k, T):
                tick, settle = T
                if step == -1:
                    for c in range(NCH):
                        tick(dve.bn_stats(stats[:, c, :], m.x_res[:, b * NCH + c, :]))
                    settle(b)
                    pause(dve, S["v_passed"])
                    for c in range(NCH):
                        dve.bn_aggr(mv[:, c, :], stats[:, c, :]).then_inc(S["st"], 1)
                if step == 0:
                    dve.wait_ge(S["rs"], b + 1)
                    dve.wait_ge(S["st"], 2 * b + 2)
                    for c in range(NCH):
                        dve.tensor_scalar(xn[:, c, :], m.x_res[:, b * NCH + c, :], mv[:, c, 0:1], rstd[:, c:c + 1],
                                          ALU.subtract, ALU.mult).then_inc(S["xn"], 1)
                if step == 6:
                    dve.wait_ge(S["sums"], 2 * b + 2)
                    dve.tensor_tensor(dt[:, k], sum1[:], sum2[:], ALU.min).then_inc(S["dt_ready"], 1)
                    dve.wait_ge(S["dt_ready"], b + 1)
                    dve.wait_ge(S["u_ready"], b + 1)
                    dve.tensor_tensor(dtu[:, k], dt[:, k], u[:, k], ALU.mult).then_inc(S["dtu_ready"], 1)

            def finish(step, b, k):
                if step == 0:
                    dve.wait_ge(S["y_part"], 8 * b + 8)
                    dve.wait_ge(S["z_ready"], b + 1)
                    dve.tensor_tensor(yz[:], bY[:, :].rearrange("p (h t) -> p h t", h=NH), z[:, k], ALU.mult)\
                        .then_inc(S["yz"], 1)
                if step == 2:
                    dve.wait_ge(S["out_ps"], b + 1)
                    pause(dve, S["v_passed"])
                    for c in range(NCH):
                        ins = dve.bn_stats(ostats[:, c, :], bZ[:, c * D:(c + 1) * D])
                        ins.then_inc(S["ostats"], 1)
                    dve.wait_ge(S["ostats"], 2 * b + 2)
                    pause(dve, S["v_passed"])
                    for c in range(NCH):
                        dve.bn_aggr(omv[:, c, :], ostats[:, c, :]).then_inc(S["ost"], 1)
                if step == 3:
                    dve.wait_ge(S["ors"], b + 1)
                    dve.wait_ge(S["ost"], 2 * b + 2)
                    for c in range(NCH):
                        dve.tensor_scalar(oh[:, c, :], bZ[:, c * D:(c + 1) * D], omv[:, c, 0:1], orstd[:, c:c + 1],
                                          ALU.subtract, ALU.mult).then_inc(S["o_read"], 1)
                if step == 7:
                    dve.wait_ge(S["done"], b + 1)

            def times_B(b, k, j):
                dve.wait_ge(S["B_ps"], 8 * b + j + 1)
                if j == 0:
                    dve.wait_ge(S["dtu_ready"], b + 1)
                dve.tensor_tensor(dbu[:, j % 2], dtu[:, k].unsqueeze(2).broadcast_to([P, NH, 2, L]),
                                  bB[j % 2][:, :].rearrange("p (n t) -> p n t", n=2).unsqueeze(1).broadcast_to(
                                      [P, NH, 2, L]), ALU.mult).then_inc(S["dbu_done"], 1)

            def recur(b, j):
                flat = lambda a: a.rearrange("p h n t -> p (h n t)")
                dve.wait_ge(S["dbu_done"], 8 * b + j + 1)
                dve.wait_ge(S["dA_ready"], 8 * b + j + 1)
                dve.tensor_tensor_scan(flat(hs[:, j % 2]), flat(dA[:, j % RING]), flat(dbu[:, j % 2]), 0.0,
                                       ALU.mult, ALU.add).then_inc(S["scanned"], 1)

            def times_C(b, j, first):
                dve.wait_ge(S["scanned"], 8 * b + j + 1)
                dve.wait_ge(S["C_ps"], 8 * b + j + 1)
                if not (first and j < 2):
                    dve.wait_ge(S["y_part"], 8 * b + j - 1)
                dve.tensor_tensor(hc[:, j % 2], hs[:, j % 2],
                                  bC[j % 2][:, :].rearrange("p (n t) -> p n t", n=2).unsqueeze(1).broadcast_to(
                                      [P, NH, 2, L]), ALU.mult).then_inc(S["hc_ready"], 1)

            def body(b, k, first, prepares):
                tp, sp_, end_prep = ticker(dve, S["v_prep"], SCAN_PREP)
                if prepares:
                    prepare(-1, b + 1, 1 - k, (tp, sp_))
                for j in range(SCAN_J):
                    recur(b, j)
                    if j + 1 < SCAN_J:
                        times_B(b, k, j + 1)
                    elif prepares:
                        times_B(b + 1, 1 - k, 0)
                    if not first:
                        finish(j, b - 1, 1 - k)
                    if prepares:
                        prepare(j, b + 1, 1 - k, (tp, sp_))
                    times_C(b, j, first)
                    if j == SCAN_J - 1:
                        if not first:
                            dve.wait_ge(S["gate_ps"], b)
                        dve.tensor_scalar(gsel[:], m.gates[:, 1, :].rearrange("p (a d) -> p a d", a=3)[:, 0:3:2, :],
                                          m.const[0:B, bass.ds(C_ID + b, 1)], None, ALU.mult).then_inc(S["gsel"], 1)
                if prepares:
                    end_prep()

            def last(b, k):
                for j in range(SCAN_J):
                    finish(j, b, k)

            tp, sp_, _ = ticker(dve, S["v_prep"], SCAN_PREP)
            for j in range(-1, SCAN_J):
                prepare(j, 0, 0, (tp, sp_))
            times_B(0, 0, 0)
            sequences(dve, body, last)

        @block.scalar
        def _(act):
            act.activation(aneg[:], m.bcol[:, :, ALOG:], ACT.Exp).then_inc(S["a_exp"], 1)
            act.preload_act_table_set(EXPLN)
            act.wait_ge(S["init"], 1)

            def prepare(step, b, k):
                if step == -1:
                    act.wait_ge(S["st"], 2 * b + 2)
                    act.activation(lnv[:], mv[:, :, 1], ACT.Ln, bias=m.eps[:, 0:1]).then_inc(S["ln"], 1)
                    act.wait_ge(S["ln"], b + 1)
                    act.activation(rstd[:], lnv[:], ACT.Exp, scale=-0.5).then_inc(S["rs"], 1)
                if step == 1:
                    act.wait_ge(S["xT"], b + 1)
                    act.activation(hT[:, k, BACK:], bT[:, 0:L], ACT.Identity, bias=m.modT[:, 1, 0, bass.ds(b, 1)],
                                   scale=m.modT[:, 1, 1, bass.ds(b, 1)]).then_inc(S["h"], 1)
                if step == 2:
                    act.wait_ge(S["bc_ps"], b + 1)
                    act.activation(dlow[96:96 + RDT, :], bT[96:96 + RDT, 0:L], ACT.Copy).then_inc(S["dlow"], 1)
                    act.activation(bcr[:], bT[0:96, 0:L], ACT.Copy).then_inc(S["bcr"], 1)
                    act.wait_ge(S["xs_ps"], b + 1)
                    for h in range(NH):
                        act.activation(acc[:, h, :], bX[:, h * L:(h + 1) * L], ACT.Identity, bias=col(h, CONV_B))\
                           .then_inc(S["conv"], 1)
                if step == 3:
                    act.wait_ge(S["dt_ps"], b + 1)
                    for h in range(NH):
                        act.activation(soft[:, h, :], bX[:, h * L:(h + 1) * L], ACT.Abs, bias=col(h, DT_B))\
                           .then_inc(S["abs"], 1)
                        act.activation(pos[:, h, :], bX[:, h * L:(h + 1) * L], ACT.Relu, bias=col(h, DT_B))\
                           .then_inc(S["pos"], 1)
                    act.wait_ge(S["abs"], 2 * b + 2)
                    act.activation(e[:], soft[:], ACT.Exp, scale=-1.0).then_inc(S["e_ready"], 1)
                    act.wait_ge(S["e_ready"], b + 1)
                    act.activation(esq[:], e[:], ACT.Square).then_inc(S["e_parts"], 1)
                    act.activation(cub[:], e[:], ACT.Identity, bias=m.eps[:, 4:5], scale=1.0 / 3)\
                       .then_inc(S["e_parts"], 1)
                    act.activation(over[:], e[:], ACT.Relu, bias=m.eps[:, 3:4]).then_inc(S["over"], 1)
                if step == 4:
                    act.wait_ge(S["over"], b + 1)
                    act.activation(soft[:], over[:], ACT.Ln, bias=m.eps[:, 2:3]).then_inc(S["soft"], 1)
                    act.wait_ge(S["conv"], 2 * b + 2)
                    act.activation(u[:, k], acc[:], ACT.Silu).then_inc(S["u_ready"], 1)
                    act.wait_ge(S["z_ps"], b + 1)
                    act.activation(z[:, k], bZ[:, :].rearrange("p (h t) -> p h t", h=NH), ACT.Silu)\
                       .then_inc(S["z_ready"], 1)
                    act.preload_act_table_set(EXPLN)

            def finish(step, b, k):
                if step == 0:
                    act.wait_ge(S["gate_ps"], b + 1)
                    act.activation(gate[:], bT[:, 0:2 * D].rearrange("p (a d) -> p a d", a=2), ACT.Copy)\
                       .then_inc(S["gate"], 1)
                if step == 2:
                    act.wait_ge(S["ost"], 2 * b + 2)
                    act.activation(olnv[:], omv[:, :, 1], ACT.Ln, bias=m.eps[:, 0:1]).then_inc(S["oln"], 1)
                    act.wait_ge(S["oln"], b + 1)
                    act.activation(orstd[:], olnv[:], ACT.Exp, scale=-0.5).then_inc(S["ors"], 1)

            def decays(b, k, j, free):
                if j == 0:
                    act.wait_ge(S["dt_ready"], b + 1)
                if free:
                    act.wait_ge(S["scanned"], 8 * b + j - RING + 1)
                for h in range(NH):
                    for n in range(2):
                        ins = act.activation(dA[:, j % RING, h, n, 1:], dt[:, k, h, 1:], ACT.Exp,
                                             scale=aneg[:, h, 2 * j + n:2 * j + n + 1])
                ins.then_inc(S["dA_ready"], 1)

            def body(b, k, first, prepares):
                if prepares:
                    prepare(-1, b + 1, 1 - k)
                for j in range(SCAN_J):
                    if j < RING:
                        decays(b, k, j + RING, True)
                    if not first:
                        finish(j, b - 1, 1 - k)
                    if prepares:
                        prepare(j, b + 1, 1 - k)
                        if j == 6:
                            decays(b + 1, 1 - k, 0, True)
                            decays(b + 1, 1 - k, 1, True)
                        if j == 7:
                            decays(b + 1, 1 - k, 2, True)
                            decays(b + 1, 1 - k, 3, True)

            def last(b, k):
                for j in range(SCAN_J):
                    finish(j, b, k)

            for j in range(-1, SCAN_J):
                prepare(j, 0, 0)
            for j in range(RING):
                decays(0, 0, j, False)
            sequences(act, body, last)

        @block.sync
        def _(sp):
            sp.dma_start(m.w13[:], d["w13"]).then_inc(S["weights"], 16)
            sp.dma_start(m.w2d[:], d["w2d"]).then_inc(S["weights"], 16)
            sp.wait_ge(S["weights"], 32)

        @block.gpsimd
        def _(pool):
            tick_of = lambda b: ticker(pool, S["p_own"], SCAN_POOL)

            def split(b, k, T):
                tick, settle, _ = T
                pool.wait_ge(S["bcr"], b + 1)
                pause(pool, S["p_passed"])
                pool.tensor_copy(bc[:, k, :], bcr[:]).then_inc(S["bc_parts"], 1)
                pool.wait_ge(S["bc_parts"], 3 * b + 1)
                tick(pool.tensor_tensor(r1[:], bcr[:], bc[:, k, :], ALU.subtract))
                settle(b)
                pause(pool, S["p_passed"])
                tick(pool.tensor_copy(mid[64:96, :], r1[64:96, :]))
                pool.tensor_copy(bc[32:64, k, :], r1[32:64, :]).then_inc(S["bc_parts"], 1)
                settle(b)
                pool.tensor_tensor(bc[64:96, k, :], r1[64:96, :], mid[64:96, :], ALU.subtract)\
                    .then_inc(S["bc_parts"], 1)

            def softplus(b, k, T):
                tick, settle, end = T
                pool.wait_ge(S["e_ready"], b + 1)
                tick(pool.tensor_tensor(sum1[:], pos[:], e[:], ALU.add))
                pool.wait_ge(S["e_parts"], 2 * b + 2)
                tick(pool.tensor_tensor(cub[:], cub[:], esq[:], ALU.mult))
                settle(b)
                pool.tensor_tensor(sum1[:], sum1[:], cub[:], ALU.add).then_inc(S["sums"], 1)
                pool.wait_ge(S["soft"], b + 1)
                pool.tensor_tensor(sum2[:], pos[:], soft[:], ALU.add).then_inc(S["sums"], 1)
                end()

            def residual(b):
                pool.wait_ge(S["gate"], b + 1)
                pool.wait_ge(S["o_read"], 2 * b + 2)
                pool.tensor_tensor(og[:], oh[:], gate[:, 0:1, :].broadcast_to([P, NCH, D]), ALU.mult)\
                    .then_inc(S["og"], 1)
                pool.wait_ge(S["og"], 2 * b + 1)
                pool.tensor_tensor(og[:], og[:], gate[:, 1:2, :].broadcast_to([P, NCH, D]), ALU.add)\
                    .then_inc(S["og"], 1)
                pool.wait_ge(S["og"], 2 * b + 2)
                pause(pool, S["p_passed"])
                xs = m.x_res[:, bass.ds(b * NCH, NCH), :]
                pool.tensor_tensor(xs, xs, og[:], ALU.add).then_inc(S["done"], 1)

            def body(b, k, first, prepares):
                if prepares:
                    T = tick_of(b + 1)
                    split(b + 1, 1 - k, T)
                    pool.wait_ge(S["bc_parts"], 3 * b + 6)
                    softplus(b + 1, 1 - k, T)
                    pool.wait_ge(S["sums"], 2 * b + 4)
                if not first:
                    residual(b - 1)
                    pool.wait_ge(S["done"], b)

            T = tick_of(0)
            split(0, 0, T)
            pool.wait_ge(S["bc_parts"], 3)
            softplus(0, 0, T)
            pool.wait_ge(S["sums"], 2)
            sequences(pool, body, lambda b, k: residual(b))

        @block.tensor
        def _(pe):
            for h in range(NH):
                mm = pe.transpose(bX[:, h * P:(h + 1) * P], m.w_in[:, h * P:(h + 1) * P], ident)
            mm.then_inc(S["w_turned"], 1)
            pe.wait_ge(S["w_scaled"], NH * KCONV)
            for h in range(NH):
                for tap in range(KCONV):
                    mm = pe.transpose(bC[h][:, tap * P:(tap + 1) * P],
                                      hc[:, 0, h, tap // 2, (tap % 2) * P:(tap % 2 + 1) * P], ident)
            mm.then_inc(S["w_back"], 1)
            pe.wait_ge(S["init"], 1)

            def prepare(step, b, k):
                if step == 1:
                    pe.wait_ge(S["xn"], 2 * b + 2)
                    if not (isinstance(b, int) and b <= 1):
                        pe.wait_ge(S["gate"], b - 1)
                    for c in range(NCH):
                        mm = pe.transpose(bT[:, c * P:(c + 1) * P], xn[:, c, :], ident)
                    mm.then_inc(S["xT"], 1)
                if step == 2:
                    pe.wait_ge(S["h"], b + 1)
                    pe.matmul(bT[0:104, 0:L], m.w_in[:, 2 * DI:2 * DI + 104], hT[:, k, BACK:], start=True,
                              stop=True).then_inc(S["bc_ps"], 1)
                    for h in range(NH):
                        for tap in range(KCONV):
                            mm = pe.matmul(bX[:, h * L:(h + 1) * L], wc[:, tap, h * P:(h + 1) * P],
                                           hT[:, k, tap:tap + L], start=(tap == 0), stop=(tap == KCONV - 1))
                    mm.then_inc(S["xs_ps"], 1)
                if step == 3:
                    pe.wait_ge(S["dlow"], b + 1)
                    pe.wait_ge(S["conv"], 2 * b + 2)
                    for h in range(NH):
                        mm = pe.matmul(bX[:, h * L:(h + 1) * L], m.wdt[96:96 + RDT, h * P:(h + 1) * P],
                                       dlow[96:96 + RDT, :], start=True, stop=True)
                    mm.then_inc(S["dt_ps"], 1)
                if step == 4:
                    if not (isinstance(b, int) and b <= 1):
                        pe.wait_ge(S["o_read"], 2 * b - 2)
                    for h in range(NH):
                        mm = pe.matmul(bZ[:, h * L:(h + 1) * L], m.w_in[:, DI + h * P:DI + (h + 1) * P], hT[:, k, BACK:],
                                       start=True, stop=True)
                    mm.then_inc(S["z_ps"], 1)

            def finish(step, b, k):
                if step == 0:
                    pe.wait_ge(S["gsel"], b + 1)
                    pe.matmul(bT[:, 0:2 * D], m.ones16[:], gsel[:].rearrange("p a d -> p (a d)"), start=True,
                              stop=True).then_inc(S["gate_ps"], 1)
                if step == 1:
                    pe.wait_ge(S["yz"], b + 1)
                    for c in range(NCH):
                        o = bZ[:, c * D:(c + 1) * D]
                        for h in range(NH):
                            pe.matmul(o, yz[:, h, c * P:(c + 1) * P], m.w_outT[:, h, :], start=(h == 0), stop=False)
                        mm = pe.matmul(o, hT[:, k, BACK + c * P:BACK + (c + 1) * P], ident, start=False, stop=True)
                    mm.then_inc(S["out_ps"], 1)

            def rows(bank, b, k, j, first_row, ready):
                for n in range(2):
                    mm = pe.matmul(bank[:, n * L:(n + 1) * L], spread[:, first_row + 2 * j + n, :], bc[:, k, :],
                                   start=True, stop=True)
                mm.then_inc(ready, 1)

            def B_rows(b, k, j, first):
                if j == 0:
                    pe.wait_ge(S["bc_parts"], 3 * b + 3)
                if not (first and j < 2):
                    pe.wait_ge(S["dbu_done"], 8 * b + j - 1)
                rows(bB[j % 2], b, k, j, 0, S["B_ps"])

            def C_rows(b, k, j, first):
                if not (first and j < 2):
                    pe.wait_ge(S["hc_ready"], 8 * b + j - 1)
                rows(bC[j % 2], b, k, j, NST, S["C_ps"])

            def sum_states(b, k, j, first):
                halves = bY[:, :].rearrange("p (h t) -> p h t", h=NH)
                if j == 0:
                    pe.wait_ge(S["u_ready"], b + 1)
                    if not first:
                        pe.wait_ge(S["yz"], b)
                    for h in range(NH):
                        pe.matmul(halves[:, h, :], dskip[:, h, :], u[:, k, h, :], start=(h == 0), stop=False,
                                  skip_group_check=True)
                pe.wait_ge(S["hc_ready"], 8 * b + j + 1)
                for n in range(2):
                    mm = pe.matmul(halves, ident, hc[:, j % 2, :, n, :], start=False,
                                   stop=(j == SCAN_J - 1 and n == 1), skip_group_check=True)
                mm.then_inc(S["y_part"], 1)

            def body(b, k, first, prepares):
                for j in range(SCAN_J):
                    if j + 1 < SCAN_J:
                        B_rows(b, k, j + 1, first)
                    elif prepares:
                        B_rows(b + 1, 1 - k, 0, False)
                    C_rows(b, k, j, first)
                    if j > 0:
                        sum_states(b, k, j - 1, first)
                    elif not first:
                        sum_states(b - 1, 1 - k, SCAN_J - 1, False)
                    if not first:
                        finish(j, b - 1, 1 - k)
                    if prepares:
                        prepare(j, b + 1, 1 - k)

            def last(b, k):
                sum_states(b, k, SCAN_J - 1, False)
                for j in range(SCAN_J):
                    finish(j, b, k)

            for j in range(SCAN_J):
                prepare(j, 0, 0)
            B_rows(0, 0, 0, True)
            sequences(pe, body, last)


SCAN_PREP, SCAN_POOL = 2, 4


MAX_TILES = (B * L * TOPK + E1 * (P - 1)) // P
MOE_TILES = MAX_TILES + MAX_TILES % 2
ASSIGN = TILES * TOPK


def router_phase(nc, d, m, ps):
    with ExitStack() as ctx:
        sem = semaphores(nc, ctx, "r_")

        def sb(n, s, dt=F32):
            return ctx.enter_context(nc.sbuf_tensor("r_" + n, s, dt))

        Q = 2 * NCH
        stats, mv = sb("stats", [P, Q, 6]), sb("mv", [P, Q, 2])
        lnv, rstd = sb("lnv", [P, Q]), sb("rstd", [P, Q])
        xn = sb("xn", [P, Q, D])
        hT = sb("hT", [P, 2, 2, L])
        sq = sb("sq", [P, 2 * L])
        lrms, rrms = sb("lrms", [P, 2 * L]), sb("rrms", [P, 2 * L])
        hf = sb("hf", [P, 2 * L])
        rows = sb("rows", [P, Q, D])
        gsel, gate = sb("gsel", [B, 2, D]), sb("gate", [P, 2, D])
        gh = sb("gh", [P, Q, D])
        mx, sh, ex = sb("mx", [P, Q]), sb("sh", [P, Q, E1]), sb("ex", [P, Q, E1])
        top = sb("top", [P, Q, 8])
        idx = sb("idx", [P, Q, 8], U32)
        den, rden = sb("den", [P, Q]), sb("rden", [P, Q])
        names = ("v_head v_tail v_passed a_head a_tail st rs xn xT h sq ms_ps rms hf lg_ps sh ex gsel gate_ps gate "
                 "back_ps rows_ps rows stored rows_free").split()
        S = {n: sem(n) for n in names}
        ident = m.const[:, C_ID:C_ID + P]
        block = ctx.enter_context(nc.Block())
        bT, bM, bH, bG, bL, bR = ps[0:6]
        flat = lambda t: t.rearrange("p s t -> p (s t)")

        def rounds(eng, body):
            body(0, 0, None, None)
            with eng.Fori(0, PAIRS // 2 - 1, 1) as r:
                body(2 * r + 1, 1, 2 * r, 0)
                body(2 * r + 2, 0, 2 * r + 1, 1)
            body(PAIRS - 1, 1, PAIRS - 2, 0)
            body(None, None, PAIRS - 1, 1)

        @block.vector
        def _(dve):
            def body(a, ka, b, kb):
                head, settle_head, end_head = ticker(dve, S["v_head"], Q)
                tail, settle_tail, end_tail = ticker(dve, S["v_tail"], ROUTER_TAIL)
                if a is not None:
                    pause(dve, S["v_passed"])
                    for q in range(Q):
                        head(dve.bn_stats(stats[:, q, :], m.x_res[:, a * Q + q, :]))
                    settle_head(a)
                    pause(dve, S["v_passed"])
                    for q in range(Q):
                        dve.bn_aggr(mv[:, q, :], stats[:, q, :]).then_inc(S["st"], 1)
                    end_head()
                if b is not None:
                    for k in range(2):
                        dve.tensor_scalar(gsel[:, k, :], m.gates[:, 1, D:2 * D],
                                          m.const[0:B, bass.ds(C_ID + 2 * b + k, 1)], None,
                                          ALU.mult).then_inc(S["gsel"], 1)
                if a is not None:
                    dve.wait_ge(S["rs"], a + 1)
                    dve.wait_ge(S["st"], Q * a + Q)
                    for q in range(Q):
                        dve.tensor_scalar(xn[:, q, :], m.x_res[:, a * Q + q, :], mv[:, q, 0:1], rstd[:, q:q + 1],
                                          ALU.subtract, ALU.mult).then_inc(S["xn"], 1)
                if b is not None:
                    dve.wait_ge(S["rms"], b + 1)
                    dve.scalar_tensor_tensor(hf[:], flat(hT[:, kb]), m.gate1[:, E1:E1 + 1], rrms[:],
                                             ALU.mult, ALU.mult).then_inc(S["hf"], 1)
                    dve.wait_ge(S["back_ps"], b + 1)
                    dve.wait_ge(S["gate"], b + 1)
                    for k in range(2):
                        tail(dve.tensor_tensor(gh[:, 2 * k:2 * k + 2, :],
                                               bH[:, k * L:(k + 1) * L].rearrange("p (c d) -> p c d", c=NCH),
                                               gate[:, k:k + 1, :].broadcast_to([P, NCH, D]), ALU.mult))
                    settle_tail(b)
                    xs = m.x_res[:, bass.ds(b * Q, Q), :]
                    tail(dve.tensor_tensor(xs, xs, gh[:], ALU.add))
                    dve.wait_ge(S["lg_ps"], b + 1)
                    lg = bL[:, 0:Q * E1].rearrange("p (q e) -> p q e", q=Q)
                    tail(dve.tensor_reduce(mx[:], lg, AX, ALU.max))
                    settle_tail(b)
                    dve.tensor_tensor(sh[:], lg, mx[:].unsqueeze(2).broadcast_to([P, Q, E1]),
                                      ALU.subtract).then_inc(S["sh"], 1)
                    dve.wait_ge(S["ex"], b + 1)
                    pause(dve, S["v_passed"])
                    for q in range(Q):
                        tail(dve.max(top[:, q, :], ex[:, q, :]))
                    settle_tail(b)
                    pause(dve, S["v_passed"])
                    for q in range(Q):
                        tail(dve.max_index(idx[:, q, :], top[:, q, :], ex[:, q, :]))
                    tail(dve.tensor_tensor(den[:], top[:, :, 0], top[:, :, 1], ALU.add))
                    settle_tail(b)
                    tail(dve.tensor_copy(m.expert[:, bass.ds(b * Q, Q), :], idx[:, :, 0:TOPK]))
                    tail(dve.reciprocal(rden[:], den[:]))
                    settle_tail(b)
                    tail(dve.tensor_tensor(m.weight[:, bass.ds(b * Q, Q), :], top[:, :, 0:TOPK],
                                           rden[:].unsqueeze(2).broadcast_to([P, Q, TOPK]), ALU.mult))
                    settle_tail(b)
                    end_tail()

            rounds(dve, body)

        @block.scalar
        def _(act):
            act.preload_act_table_set(EXPLN)

            def body(a, ka, b, kb):
                head, settle_head, _ = ticker(act, S["a_head"], 1)
                tail, settle_tail, _ = ticker(act, S["a_tail"], 1)
                if b is not None:
                    act.wait_ge(S["ms_ps"], b + 1)
                    tail(act.activation(lrms[:], bM[:, :], ACT.Ln, bias=m.eps[:, 1:2]))
                    settle_tail(b)
                    act.activation(rrms[:], lrms[:], ACT.Exp, scale=-0.5).then_inc(S["rms"], 1)
                if a is not None:
                    act.wait_ge(S["st"], Q * a + Q)
                    head(act.activation(lnv[:], mv[:, :, 1], ACT.Ln, bias=m.eps[:, 0:1]))
                    settle_head(a)
                    act.activation(rstd[:], lnv[:], ACT.Exp, scale=-0.5).then_inc(S["rs"], 1)
                if b is not None:
                    act.wait_ge(S["gate_ps"], b + 1)
                    act.activation(gate[:], bG[:, 0:2 * D].rearrange("p (s d) -> p s d", s=2),
                                   ACT.Copy).then_inc(S["gate"], 1)
                if a is not None:
                    act.wait_ge(S["xT"], a + 1)
                    for k in range(2):
                        act.activation(hT[:, ka, k, :], bT[:, k * L:(k + 1) * L], ACT.Identity,
                                       bias=m.modT[:, 1, 2, bass.ds(2 * a + k, 1)],
                                       scale=m.modT[:, 1, 3, bass.ds(2 * a + k, 1)]).then_inc(S["h"], 1)
                if b is not None:
                    act.wait_ge(S["sh"], b + 1)
                    act.activation(ex[:], sh[:], ACT.Exp).then_inc(S["ex"], 1)
                if a is not None:
                    act.wait_ge(S["h"], 2 * a + 2)
                    act.activation(sq[:], flat(hT[:, ka]), ACT.Square).then_inc(S["sq"], 1)
                if b is not None:
                    act.wait_ge(S["rows_ps"], b + 1)
                    act.wait_ge(S["rows_free"], b + 1)
                    act.activation(rows[:], bR[:, :].rearrange("p (q d) -> p q d", q=Q), ACT.Copy)\
                       .then_inc(S["rows"], 1)

            rounds(act, body)

        @block.sync
        def _(sp):
            sp.sem_inc(S["rows_free"], 1)
            with sp.Fori(0, PAIRS, 1) as r:
                sp.wait_ge(S["rows"], r + 1)
                sp.dma_start(m.hf_rows[bass.ds(r * Q * P, Q * P), :].rearrange("(q p) d -> p q d", p=P),
                             rows[:]).then_inc(S["stored"], 16)
                sp.wait_ge(S["stored"], 16 * (r + 1))
                sp.sem_inc(S["rows_free"], 1)

        @block.tensor
        def _(pe):
            def body(a, ka, b, kb):
                if b is not None:
                    pe.wait_ge(S["sq"], b + 1)
                    pe.matmul(bM[:, :], m.ones128[:], sq[:], start=True, stop=True).then_inc(S["ms_ps"], 1)
                    pe.wait_ge(S["gsel"], 2 * b + 2)
                    pe.matmul(bG[:, 0:2 * D], m.ones16[:], flat(gsel[:]), start=True, stop=True)\
                        .then_inc(S["gate_ps"], 1)
                    for k in range(2):
                        for c in range(NCH):
                            q = k * NCH + c
                            mm = pe.transpose(bH[:, q * D:(q + 1) * D], hT[:, kb, k, c * P:(c + 1) * P], ident)
                    mm.then_inc(S["back_ps"], 1)
                if a is not None:
                    pe.wait_ge(S["xn"], Q * a + Q)
                    for q in range(Q):
                        mm = pe.transpose(bT[:, q * P:(q + 1) * P], xn[:, q, :], ident)
                    mm.then_inc(S["xT"], 1)
                if b is not None:
                    pe.wait_ge(S["hf"], b + 1)
                    for q in range(Q):
                        mm = pe.matmul(bL[:, q * E1:(q + 1) * E1], hf[:, q * P:(q + 1) * P], m.gate1[:, 0:E1],
                                       start=True, stop=True)
                    mm.then_inc(S["lg_ps"], 1)
                    for q in range(Q):
                        mm = pe.transpose(bR[:, q * P:(q + 1) * P], hf[:, q * P:(q + 1) * P], ident)
                    mm.then_inc(S["rows_ps"], 1)

            rounds(pe, body)


ROUTER_TAIL = 16


def slots_phase(nc, d, m, ps):
    with ExitStack() as ctx:
        sem = semaphores(nc, ctx, "m_")

        def sb(n, s, dt=F32):
            return ctx.enter_context(nc.sbuf_tensor("m_" + n, s, dt))

        NT = TILES * E1
        hot = sb("hot", [P, TOPK, TILES, E1])
        cnt = sb("cnt", [P, TILES, E1])
        before = sb("before", [P, P])
        incl = sb("incl", [P, E1, TILES])
        tot = sb("tot", [P, E1, TILES])
        run = sb("run", [P, E1, TILES])
        more = sb("more", [P, E1, TILES])
        full = sb("full", [P, E1])
        ntile, ctile, base, zeros = (sb(n, [P, E1]) for n in ("ntile", "ctile", "base", "zeros"))
        addr = sb("addr", [P, TILES, E1])
        pick = sb("pick", [P, TOPK, TILES, E1])
        slot = sb("slot", [P, TOPK, TILES])
        slot_i, lo_i, hi_i = (sb(n, [P, TOPK, TILES], U32) for n in ("slot_i", "lo_i", "hi_i"))
        lo, hi = sb("lo", [P, TOPK, TILES]), sb("hi", [P, TOPK, TILES])
        cmp = sb("cmp", [P, MOE_TILES, E1])
        etile = sb("etile", [P, MOE_TILES])
        hot_lo = sb("hot_lo", [P, 4, P])
        hot_hi = sb("hot_hi", [P, 4, MOE_TILES])
        idm, off, fil = (sb(n, [P, MOE_TILES]) for n in ("idm", "off", "fil"))
        tok_i = sb("tok_i", [P, MOE_TILES], U32)
        own, s_cnt, s_ps, s_map = sem("own"), sem("cnt"), sem("ps"), sem("map")
        s_hot = [sem(f"hot{i}") for i in range(4)]
        s_used = [sem(f"used{i}") for i in range(4)]
        block = ctx.enter_context(nc.Block())

        @block.tensor
        def _(pe):
            pe.wait_ge(s_cnt, 1)
            flat = cnt[:].rearrange("p t e -> p (t e)")
            pe.matmul(ps[0][:, 0:NT], before[:], flat, start=True, stop=True)
            pe.matmul(ps[1][:, 0:NT], m.ones128[:], flat, start=True, stop=True).then_inc(s_ps, 1)
            for i in range(4):
                pe.wait_ge(s_hot[i], 1)
                pe.matmul(ps[2][:, 0:MOE_TILES], hot_lo[:, i, :], hot_hi[:, i, :], start=(i == 0),
                          stop=False).then_inc(s_used[i], 1)
            with pe.Fori(1, ASSIGN // 4 - 1, 1) as r:
                for i in range(4):
                    pe.wait_ge(s_hot[i], r + 1)
                    pe.matmul(ps[2][:, 0:MOE_TILES], hot_lo[:, i, :], hot_hi[:, i, :], start=False,
                              stop=False).then_inc(s_used[i], 1)
            for i in range(4):
                pe.wait_ge(s_hot[i], ASSIGN // 4)
                mm = pe.matmul(ps[2][:, 0:MOE_TILES], hot_lo[:, i, :], hot_hi[:, i, :], start=False, stop=(i == 3))
            mm.then_inc(s_map, 1)

        @block.vector
        def _(dve):
            tick, settle, _ = ticker(dve, own)
            iota8 = m.const[:, C_IOTA8:C_IOTA8 + E1]
            for k in range(TOPK):
                tick(dve.tensor_tensor(hot[:, k], m.expert[:, :, k:k + 1].broadcast_to([P, TILES, E1]),
                                       iota8.unsqueeze(1).broadcast_to([P, TILES, E1]), ALU.is_equal))
            tick(dve.tensor_tensor(before[:], m.const[:, C_TRI:C_TRI + P], m.const[:, C_ID:C_ID + P], ALU.subtract))
            tick(dve.memset(zeros[:], 0.0))
            tick(dve.memset(run[:], 1.0))
            settle()
            tick(dve.memset(run[:, :, 0:1], 0.0))
            dve.tensor_tensor(cnt[:], hot[:, 0], hot[:, 1], ALU.add).then_inc(s_cnt, 1)
            dve.wait_ge(s_ps, 1)
            tick(dve.tensor_copy(tot[:], ps[1][:, 0:NT].rearrange("p (t e) -> p e t", e=E1)))
            settle()
            flat = lambda a: a[:].rearrange("p e t -> p (e t)")
            tick(dve.tensor_tensor_scan(flat(incl), flat(run), flat(tot), 0.0, ALU.mult, ALU.add))
            settle()
            tick(dve.tensor_scalar(full[:], incl[:, :, TILES - 1], 1.0, None, ALU.add))
            tick(dve.tensor_tensor(tot[:], incl[:], tot[:], ALU.subtract))
            settle()
            tick(dve.tensor_tensor(more[:], full[:].unsqueeze(2).broadcast_to([P, E1, TILES]),
                                   m.const[:, C_IOTA:C_IOTA + TILES].unsqueeze(1).broadcast_to([P, E1, TILES]),
                                   ALU.is_gt))
            settle()
            tick(dve.tensor_reduce(ntile[:], more[:], AX, ALU.add))
            settle()
            tick(dve.tensor_tensor_scan(ctile[:], ntile[:], zeros[:], 0.0, ALU.add, ALU.add))
            settle()
            tick(dve.tensor_tensor(base[:], ctile[:], ntile[:], ALU.subtract))
            settle()
            tick(dve.tensor_tensor(tot[:], tot[:], base[:].unsqueeze(2).broadcast_to([P, E1, TILES]), ALU.add))
            settle()
            tick(dve.scalar_tensor_tensor(addr[:].rearrange("p t e -> p e t"), tot[:], float(P),
                                          ps[0][:, 0:NT].rearrange("p (t e) -> p e t", e=E1), ALU.mult, ALU.add))
            settle()
            for k in range(TOPK):
                tick(dve.tensor_tensor(pick[:, k], hot[:, k], addr[:], ALU.mult))
            settle()
            tick(dve.tensor_reduce(slot[:], pick[:], AX, ALU.add))
            tick(dve.tensor_tensor(cmp[:], ctile[:].unsqueeze(1).broadcast_to([P, MOE_TILES, E1]),
                                   m.const[:, C_T72:C_T72 + MOE_TILES].unsqueeze(2).broadcast_to([P, MOE_TILES, E1]),
                                   ALU.is_le))
            settle()
            tick(dve.tensor_reduce(etile[:], cmp[:], AX, ALU.add))
            tick(dve.tensor_copy(slot_i[:], slot[:]))
            settle()
            tick(dve.tensor_scalar(m.etile[:], etile[:], float(E1 - 1), None, ALU.min))
            tick(dve.tensor_scalar(lo_i[:], slot_i[:], P - 1, None, ALU.bitwise_and))
            tick(dve.tensor_scalar(hi_i[:], slot_i[:], 7, None, ALU.logical_shift_right))
            settle()
            tick(dve.tensor_copy(lo[:], lo_i[:]))
            tick(dve.tensor_copy(hi[:], hi_i[:]))
            settle()
            for i in range(4):
                dve.sem_inc(s_used[i], 1)
            lo_f, hi_f = (a[:].rearrange("p k t -> p (k t)") for a in (lo, hi))
            with dve.Fori(0, ASSIGN // 4, 1) as r:
                for i in range(4):
                    a = bass.ds(4 * r + i, 1)
                    dve.wait_ge(s_used[i], r + 1)
                    dve.tensor_scalar(hot_lo[:, i, :], m.const[:, C_I128:C_I128 + P], lo_f[:, a], None,
                                      ALU.is_equal)
                    dve.tensor_scalar(hot_hi[:, i, :], m.const[:, C_T72:C_T72 + MOE_TILES], hi_f[:, a],
                                      m.const[:, bass.ds(C_VAL + 4 * r + i, 1)], ALU.is_equal,
                                      ALU.mult).then_inc(s_hot[i], 1)
            dve.wait_ge(s_map, 1)
            pad = m.const[:, C_PAD:C_PAD + MOE_TILES]
            tick(dve.tensor_scalar(idm[:], ps[2][:, 0:MOE_TILES], -1.0, None, ALU.add))
            settle()
            tick(dve.tensor_scalar(fil[:], idm[:], 0.0, None, ALU.is_ge))
            tick(dve.tensor_tensor(off[:], idm[:], pad, ALU.subtract))
            settle()
            tick(dve.tensor_tensor(off[:], off[:], fil[:], ALU.mult))
            tick(dve.tensor_scalar(idm[:], idm[:], 0.0, None, ALU.max))
            settle()
            tick(dve.tensor_tensor(m.to_row[:], off[:], pad, ALU.add))
            tick(dve.tensor_copy(tok_i[:], idm[:]))
            settle()
            tick(dve.tensor_scalar(m.from_row[:, 0:MOE_TILES], tok_i[:], 1, None, ALU.logical_shift_right))
            tick(dve.memset(m.from_row[:, MOE_TILES:], 0))
            settle()


def moe_phase(nc, d, m, ps):
    with ExitStack() as ctx:
        new = semaphores(nc, ctx, "x_")
        passed = new("passed")

        def sem(n):
            return [new(f"{n}{k}") for k in range(2)]

        def sb(n, s, dt=F32):
            return ctx.enter_context(nc.sbuf_tensor("x_" + n, s, dt))

        xT = sb("xT", [P, 2, P])
        a = sb("a", [P, 2, I1])
        h = sb("h", [P, 2, I1])
        hT = sb("hT", [IC, 2, NIC, P])
        y = (sb("y0", [P, D]), sb("y1", [P, D]))
        src = (sb("src0", [P, 1], U32), sb("src1", [P, 1], U32))
        dst = (sb("dst0", [P, 1], U32), sb("dst1", [P, 1], U32))
        xg = (sb("xg0", [P, D]), sb("xg1", [P, D]))
        names = "src rows xT_ps xT ag_ps a h hT_ps hT y_ps y y_free dst sent".split()
        S = {n: sem(n) for n in names}
        FREE = "h hT y_ps hT_ps y y_free".split()
        ident = m.const[:, C_ID:C_ID + P]
        block = ctx.enter_context(nc.Block())
        R = MOE_TILES // 2
        assert R % 2 == 0

        def steps(eng, step):
            step(None, (0, 0), None, None)
            step((0, 0), (0, 1), None, None)
            step((0, 1), (1, 0), (0, 0), None)
            with eng.Fori(0, (R - 2) // 2, 1) as four:
                for r in (2 * four, 2 * four + 1):
                    step((r + 1, 0), (r + 1, 1), (r, 1), (r, 0))
                    step((r + 1, 1), (r + 2, 0), (r + 1, 0), (r, 1))
            step((R - 1, 0), (R - 1, 1), (R - 2, 1), (R - 2, 0))
            step((R - 1, 1), None, (R - 1, 0), (R - 2, 1))
            step(None, None, (R - 1, 1), (R - 1, 0))
            step(None, None, None, (R - 1, 1))

        @block.gpsimd
        def _(pool):
            for n in FREE:
                for k in range(2):
                    pool.sem_inc(S[n][k], 1)

            def fetch(r, k):
                pool.wait_ge(S["src"][k], r + 1)
                pause(pool, passed)
                pool.indirect_dma_start(xg[k][:], None, m.hf_rows[:, :],
                                        bass.IndirectOffsetOnAxis(ap=src[k][:, 0:1], axis=0)).then_inc(S["rows"][k], 16)

            def send(r, k):
                pool.wait_ge(S["y"][k], r + 2)
                pause(pool, passed)
                pool.indirect_dma_start(m.y_rows[:, :], bass.IndirectOffsetOnAxis(ap=dst[k][:, 0:1], axis=0),
                                        y[k][:], None).then_inc(S["sent"][k], 16)

            for r in range(3):
                for k in range(2):
                    fetch(r, k)
            with pool.Fori(0, R - 3, 1) as r:
                for k in range(2):
                    fetch(r + 3, k)
                    send(r, k)
            for r in range(R - 3, R):
                for k in range(2):
                    send(r, k)

        @block.sync
        def _(sp):
            with sp.Fori(0, R, 1) as r:
                for k in range(2):
                    sp.wait_ge(S["sent"][k], 16 * (r + 1))
                    sp.sem_inc(S["y_free"][k], 1)

        @block.tensor
        def _(pe):
            def expert(r, k):
                return pe.value_load(m.etile[0:1, bass.ds(2 * r + k, 1)], min_val=0, max_val=E1 - 1)

            def step(now, after, before, last):
                if now is not None:
                    r, k = now
                    e = expert(r, k)
                    pe.wait_ge(S["xT"][k], r + 1)
                    pe.wait_ge(S["h"][k], r + 1)
                    for i in range(2):
                        mm = pe.matmul(ps[2 * k + i][:, 0:I1], xT[:, k, :],
                                       m.w13[:, bass.ds(e * 2 + i, 1), :].rearrange("p e i -> p (e i)"),
                                       start=True, stop=True)
                    mm.then_inc(S["ag_ps"][k], 1)
                if last is not None:
                    e = expert(*last)
                if after is not None:
                    r, k = after
                    pe.wait_ge(S["rows"][k], 16 * (r + 1))
                    pe.transpose(ps[4][:, 0:P], xg[k][:], ident).then_inc(S["xT_ps"][k], 1)
                if before is not None:
                    r, k = before
                    pe.wait_ge(S["h"][k], r + 2)
                    pe.wait_ge(S["hT"][k], r + 1)
                    for i in range(NIC):
                        mm = pe.transpose(ps[6 + k][0:IC, i * P:(i + 1) * P], h[:, k, i * IC:(i + 1) * IC], ident)
                    mm.then_inc(S["hT_ps"][k], 1)
                if last is not None:
                    r, k = last
                    pe.wait_ge(S["hT"][k], r + 2)
                    pe.wait_ge(S["y"][1 - k], r + k + 1)
                    for i in range(NIC):
                        mm = pe.matmul(ps[5][:, 0:D], hT[:, k, i, :],
                                       m.w2d[:, bass.ds(e * NIC + i, 1), :].rearrange("p e d -> p (e d)"),
                                       start=(i == 0), stop=(i == NIC - 1))
                    mm.then_inc(S["y_ps"][k], 1)

            steps(pe, step)

        @block.scalar
        def _(act):
            act.preload_act_table_set("silu_and_others")

            def step(now, after, before, last):
                if now is not None:
                    r, k = now
                    act.wait_ge(S["ag_ps"][k], r + 1)
                    act.wait_ge(S["h"][k], r + 1)
                    act.activation(a[:, k, :], ps[2 * k][:, 0:I1], ACT.Silu).then_inc(S["a"][k], 1)
                if after is not None:
                    r, k = after
                    act.wait_ge(S["xT_ps"][k], r + 1)
                    act.activation(xT[:, k, :], ps[4][:, 0:P], ACT.Copy).then_inc(S["xT"][k], 1)
                if before is not None:
                    r, k = before
                    act.wait_ge(S["hT_ps"][k], r + 2)
                    act.wait_ge(S["y_ps"][k], r + 1)
                    act.activation(hT[:, k], ps[6 + k][0:IC, :].rearrange("p (i t) -> p i t", i=NIC),
                                   ACT.Copy).then_inc(S["hT"][k], 1)

            steps(act, step)

        @block.vector
        def _(dve):
            def step(now, after, before, last):
                if after is not None:
                    r, k = after
                    dve.wait_ge(S["xT_ps"][k], r + 1)
                    dve.tensor_copy(src[k][:], m.from_row[:, bass.ds(2 * r + 2 + k, 1)]).then_inc(S["src"][k], 1)
                if now is not None:
                    r, k = now
                    dve.wait_ge(S["a"][k], r + 1)
                    dve.wait_ge(S["hT_ps"][k], r + 1)
                    dve.tensor_tensor(h[:, k, :], a[:, k, :], ps[2 * k + 1][:, 0:I1], ALU.mult).then_inc(S["h"][k], 1)
                if last is not None:
                    r, k = last
                    dve.wait_ge(S["y_ps"][k], r + 2)
                    dve.wait_ge(S["y_free"][k], r + 1)
                    dve.tensor_copy(dst[k][:], m.to_row[:, bass.ds(2 * r + k, 1)]).then_inc(S["dst"][k], 1)
                    dve.wait_ge(S["dst"][k], r + 1)
                    dve.tensor_copy(y[k][:], ps[5][:, 0:D]).then_inc(S["y"][k], 1)

            for k in range(2):
                dve.tensor_copy(src[k][:], m.from_row[:, k:k + 1]).then_inc(S["src"][k], 1)
            steps(dve, step)


def output_phase(nc, d, m, ps):
    with ExitStack() as ctx:
        new = semaphores(nc, ctx, "o_")

        def sem(n):
            return [new(f"{n}{k}") for k in range(2)]

        def sb(n, s, dt=F32):
            return ctx.enter_context(nc.sbuf_tensor("o_" + n, s, dt))

        Q = 2 * NCH
        yr = sb("yr", [P, 2, Q, TOPK, D])
        wy = sb("wy", [P, 2, Q, TOPK, D])
        sm = sb("sm", [P, 2, Q, D])
        o = sb("o", [P, 2, Q, D])
        gsel, gate = sb("gsel", [B, 2, 2, D]), sb("gate", [P, 2, 2, D])
        names = "loaded wy sum gsel gate_ps gate gated o stored o_free".split()
        S = {n: sem(n) for n in names}
        block = ctx.enter_context(nc.Block())

        @block.gpsimd
        def _(pool):
            for n in ("wy", "gate_ps", "gate", "gated", "o_free"):
                for k in range(2):
                    pool.sem_inc(S[n][k], 1)
            with pool.Fori(0, PAIRS // 2, 1) as r:
                for k in range(2):
                    pool.wait_ge(S["stored"][k], 16 * (r + 1))
                    pool.sem_inc(S["o_free"][k], 1)

        @block.sync
        def _(sp):
            with sp.Fori(0, PAIRS // 2, 1) as r:
                for k in range(2):
                    sp.wait_ge(S["wy"][k], r + 1)
                    sp.dma_start(yr[:, k].rearrange("p q k d -> p q (k d)"),
                                 m.y_rows[bass.ds((2 * r + k) * Q * P * TOPK, Q * P * TOPK), :].rearrange(
                                     "(q p k) d -> p q (k d)", p=P, k=TOPK)).then_inc(S["loaded"][k], 16)

        @block.scalar
        def _(act):
            with act.Fori(0, PAIRS // 2, 1) as r:
                for k in range(2):
                    act.wait_ge(S["gate_ps"][k], r + 2)
                    act.wait_ge(S["gated"][k], r + 1)
                    act.activation(gate[:, k], ps[k][:, 0:2 * D].rearrange("p (s d) -> p s d", s=2),
                                   ACT.Copy).then_inc(S["gate"][k], 1)
                    act.wait_ge(S["o"][k], r + 1)
                    act.dma_start(m.out[bass.ds((2 * r + k) * 2, 2)].rearrange("b (c t) d -> t (b c) d", t=P),
                                  o[:, k]).then_inc(S["stored"][k], 16)
            for k in range(2):
                act.wait_ge(S["stored"][k], 16 * PAIRS // 2)

        @block.tensor
        def _(pe):
            with pe.Fori(0, PAIRS // 2, 1) as r:
                for k in range(2):
                    pe.wait_ge(S["gsel"][k], 2 * r + 2)
                    pe.wait_ge(S["gate"][k], r + 1)
                    pe.matmul(ps[k][:, 0:2 * D], m.ones16[:], gsel[:, k].rearrange("p s d -> p (s d)"), start=True,
                              stop=True).then_inc(S["gate_ps"][k], 1)

        @block.vector
        def _(dve):
            with dve.Fori(0, PAIRS // 2, 1) as r:
                for k in range(2):
                    dve.wait_ge(S["gate_ps"][k], r + 1)
                    for s in range(2):
                        dve.tensor_scalar(gsel[:, k, s, :], m.gates[:, 1, D:2 * D],
                                          m.const[0:B, bass.ds(C_ID + 4 * r + 2 * k + s, 1)], None,
                                          ALU.mult).then_inc(S["gsel"][k], 1)
                for k in range(2):
                    tiles = bass.ds((2 * r + k) * Q, Q)
                    dve.wait_ge(S["loaded"][k], 16 * (r + 1))
                    dve.tensor_tensor(wy[:, k], yr[:, k],
                                      m.weight[:, tiles, :].unsqueeze(3).broadcast_to([P, Q, TOPK, D]),
                                      ALU.mult).then_inc(S["wy"][k], 1)
                    dve.wait_ge(S["wy"][k], r + 2)
                    dve.tensor_tensor(sm[:, k], wy[:, k, :, 0, :], wy[:, k, :, 1, :], ALU.add)\
                       .then_inc(S["sum"][k], 1)
                    dve.wait_ge(S["sum"][k], r + 1)
                    dve.wait_ge(S["gate"][k], r + 2)
                    dve.tensor_tensor(wy[:, k, :, 0, :].rearrange("p (s c) d -> p s c d", s=2),
                                      sm[:, k].rearrange("p (s c) d -> p s c d", s=2),
                                      gate[:, k].unsqueeze(2).broadcast_to([P, 2, NCH, D]), ALU.mult)\
                       .then_inc(S["gated"][k], 1)
                    dve.wait_ge(S["gated"][k], r + 2)
                    dve.wait_ge(S["o_free"][k], r + 1)
                    dve.tensor_tensor(o[:, k], wy[:, k, :, 0, :], m.x_res[:, tiles, :], ALU.add)\
                       .then_inc(S["o"][k], 1)


LAYER0 = [attention_phase, route_phase, gather_phase, expert_phase, combine_phase]
LAYER1 = [scan_phase, router_phase, slots_phase, moe_phase, output_phase]


def build(nc, d, out, phases=99):
    with ExitStack() as ctx:
        def sb(n, s, dt=F32):
            return ctx.enter_context(nc.sbuf_tensor(n, s, dt))

        m = Mem()
        m.out = out
        m.const = sb("const", [P, C_END])
        m.x_res = sb("x_res", [P, TILES, D])
        m.silu_c = sb("silu_c", [P, 2, B])
        m.modT = sb("modT", [P, 2, 4, B])
        m.gates = sb("gates", [B, 2, 3 * D])
        m.eps = sb("eps", [P, 5])
        m.ones16 = sb("ones16", [B, P])
        m.ones128 = sb("ones128", [P, P])
        m.wq, m.wk, m.wv, m.wo = (sb(n, [P, D])[:] for n in ("wq", "wk", "wv", "wo"))
        m.gate0 = sb("gate0", [P, E0])[:]
        m.gn = sb("gn", [P, 2])[:]
        m.w_in = sb("w_in", [P, 2 * DI + 104])[:]
        m.bcol = sb("bcol", [P, NH, 7 + NST])[:]
        m.gate1 = sb("gate1", [P, E1 + 1])[:]
        m.w_outT = sb("w_outT", [P, NH, D])[:]
        m.wdt = sb("wdt", [P, DI])
        ps = [ctx.enter_context(nc.psum_tensor(f"bank{i}", [P, 512], F32)) for i in range(8)]
        setup_phase(nc, d, m, ps)
        with ExitStack() as layer:
            def sb(n, s, dt=F32):
                return layer.enter_context(nc.sbuf_tensor(n, s, dt))

            m.probs = sb("probs", [P, NCH, B * E0])
            m.places = sb("places", [P, NCH, B * E0])
            m.xn2 = sb("xn2", [P, TILES, D])
            m.xin = sb("xin", [P, E0, B * CAP])
            m.yT = sb("yT", [P, E0, B * CAP])
            for ph in LAYER0[:max(phases - 1, 0)]:
                ph(nc, d, m, ps)
        with ExitStack() as layer:
            def sb(n, s, dt=F32):
                return layer.enter_context(nc.sbuf_tensor(n, s, dt))

            m.w13 = sb("w13", [P, E1 * 2, I1])
            m.w2d = sb("w2d", [IC, E1 * NIC, D])
            m.expert, m.weight = sb("expert", [P, TILES, TOPK]), sb("weight", [P, TILES, TOPK])
            m.etile = sb("etile", [P, MOE_TILES], U32)
            m.from_row, m.to_row = sb("from_row", [P, MOE_TILES + 2], U32), sb("to_row", [P, MOE_TILES], U32)
            m.hf_rows = nc.dram_tensor("hf_rows", (B * L, D), F32).ap()
            m.y_rows = nc.dram_tensor("y_rows", (B * L * TOPK + MOE_TILES * P, D), F32).ap()
            for ph in LAYER1[:max(phases - 6, 0)]:
                ph(nc, d, m, ps)
        if phases < 11:
            s_out = ctx.enter_context(nc.semaphore("stored"))
            with nc.Block() as block:
                @block.sync
                def _(sp):
                    for i in range(4):
                        sp.dma_start(out[4 * i:4 * i + 4].rearrange("b (c t) d -> t (b c) d", t=P),
                                     m.x_res[:, 8 * i:8 * i + 8, :]).then_inc(s_out, 16)
                    sp.wait_ge(s_out, 64)


def lay_out(i):
    f = lambda a: np.ascontiguousarray(np.asarray(a))
    win = f(i["L1_attn_W_in"])
    bc, dt = win[2 * DI:2 * DI + 2 * NST], win[2 * DI + 2 * NST:]
    half = lambda a: f(a).reshape(NH, P, -1).transpose(1, 0, 2)
    return {
        "x": f(i["L0_attn_x"]),
        "const": constants(),
        "cT": f(np.stack([f(i["L0_c"]).T, f(i["L1_c"]).T], 1)),
        "wmod": f(np.stack([f(i["L0_wmod"]), f(i["L1_wmod"])], 1)),
        "lnrow": f(np.broadcast_to(np.stack([f(i["L1_attn_ln_g"]), f(i["L1_attn_ln_b"])])[None], (B, 2, D))),
        "wqT": f(f(i["L0_attn_Wq"]).T), "wkT": f(f(i["L0_attn_Wk"]).T),
        "wvT": f(f(i["L0_attn_Wv"]).T), "woT": f(f(i["L0_attn_Wo"]).T),
        "gate0": f(i["L0_ffn_gate_w"]),
        "gn": f(np.stack([f(i["L0_attn_gn_weight"]), f(i["L0_attn_gn_bias"])], 1)),
        "w1": f(i["L0_ffn_w1"]), "w2": f(i["L0_ffn_w2"]),
        "winT": f(np.concatenate([win[:2 * DI], bc, bc, bc, dt]).T),
        "cols": f(np.concatenate([half(i["L1_attn_conv_w"]), half(i["L1_attn_conv_b"]), half(i["L1_attn_b_dt"]),
                                  half(i["L1_attn_D"]), half(i["L1_attn_A_log"])], 2)),
        "gate1T": f(np.concatenate([f(i["L1_ffn_gate_w"]).T, f(i["L1_ffn_rms_weight"])[:, None]], 1)),
        "woutT": f(f(i["L1_attn_W_out"]).T.reshape(NH, P, D).transpose(1, 0, 2)),
        "wdtT": f(f(i["L1_attn_W_dt"]).T),
        "w13": f(np.stack([f(i["L1_ffn_w1"]).transpose(2, 0, 1), f(i["L1_ffn_w3"]).transpose(2, 0, 1)], 2).reshape(P, E1 * 2, I1)),
        "w2d": f(f(i["L1_ffn_w2"]).transpose(2, 0, 1).reshape(NIC, IC, E1, D).transpose(1, 2, 0, 3).reshape(IC, E1 * NIC, D)),
    }


def kernel(**inputs):
    import concourse.bacc as bacc
    from concourse.bass_utils import run_bass_kernel_spmd

    nc = bacc.Bacc("TRN2", target_bir_lowering=False, num_devices=1)
    arrays = lay_out(inputs)
    d = {n: nc.dram_tensor("in_" + n, a.shape, mybir.dt.from_np(a.dtype), kind="ExternalInput").ap() for n, a in arrays.items()}
    out = nc.dram_tensor("out", (B, L, D), F32, kind="ExternalOutput").ap()
    build(nc, d, out)
    return run_bass_kernel_spmd(nc, [{"in_" + n: a for n, a in arrays.items()}], core_ids=[0]).results[0]["out"]
```
